# Optimizing a Trainium2 kernel written in Bass

```python
import numpy as np
import jax
import jax.numpy as jnp

def _softmax(x, axis=-1):
    return jax.nn.softmax(x, axis=axis)

def _gelu(x):
    return jax.nn.gelu(x, approximate=True)

def _silu(x):
    return jax.nn.silu(x)

def _sigmoid(x):
    return jax.nn.sigmoid(x)

def _layernorm(x, axis=-1, eps=1e-05):
    m = jnp.mean(x, axis=axis, keepdims=True)
    v = jnp.var(x, axis=axis, keepdims=True)
    return (x - m) / jnp.sqrt(v + eps)

def _scatter_add(tgt, idx, src, axis=0):
    return tgt.at[idx].add(src)

def _segment_sum(src, seg, n):
    return jax.ops.segment_sum(src, seg, n)
kernel_name = 'mk_xattn_seq_d2_seqx_r4_a5117e'

def setup_inputs(seed: int=0):
    np.random.seed(seed)
    _w = jnp.asarray

    def _rec_inputs():
        import jax
        import jax.numpy as jnp
        _rk = jax.random.key(seed)
        x = -0.000125 + 0.9999 * jax.random.normal(jax.random.fold_in(_rk, 1), (4, 512, 512), jnp.float32)
        _lenS = 512 - jax.random.randint(jax.random.fold_in(_rk, 7), (4,), 0, max(1, 512 // 4) + 1, jnp.int32)
        _lenS2 = 1601 - jax.random.randint(jax.random.fold_in(_rk, 8), (4,), 0, max(1, 1601 // 4) + 1, jnp.int32)
        _ctx_1024P = jax.random.normal(jax.random.fold_in(_rk, 11), (4, 16, 256), jnp.float32)
        _ctx_1024c = jax.random.dirichlet(jax.random.fold_in(_rk, 511), 0.3 * jnp.ones((16,), jnp.float32), (4, 1601))
        _ctx_1024t = jnp.einsum('bsk,bkd->bsd', _ctx_1024c, _ctx_1024P)
        _ctx_1024t = _ctx_1024t * jax.lax.rsqrt(jnp.mean(jnp.square(_ctx_1024t)) + 1e-12) * 0.953939
        ctx_1024 = 4.13588e-05 + 0.999923 * (_ctx_1024t + 0.3 * jax.random.normal(jax.random.fold_in(_rk, 611), (4, 1601, 256), jnp.float32))
        pos_1xS = jnp.broadcast_to(jnp.arange(512, dtype=jnp.int32), (1, 512))
        _validS = jnp.arange(512)[None, :] < _lenS[:, None]
        _validS2 = jnp.arange(1601)[None, :] < _lenS2[:, None]
        _causal = jnp.tril(jnp.ones((512, 512), dtype=bool))
        mask_BxS_ik0 = jnp.where(jnp.broadcast_to(_validS[:, :], (4, 512)), 0, 1).astype(jnp.int32)
        return (x, ctx_1024, pos_1xS, mask_BxS_ik0)
    x, ctx_1024, pos_1xS, mask_BxS_ik0 = _rec_inputs()

    def _L0_xattn_setup():
        import jax, jax.numpy as jnp
        import numpy as np
        EPS = 1e-06

        def _rmsnorm(x, w):
            var = jnp.mean(jnp.square(x), axis=-1, keepdims=True)
            return x * jax.lax.rsqrt(var + EPS) * w
        key = jax.random.key(seed)
        ks = jax.random.split(key, 6)
        B, N, M = (4, 1024, 512)
        d_model, memory_dim = (512, 256)
        hidden_states = jax.random.normal(ks[0], (B, N, d_model), dtype=jnp.float32)
        memory = jax.random.normal(ks[1], (B, M, memory_dim), dtype=jnp.float32)
        W_mem = jax.random.normal(ks[2], (d_model, memory_dim), dtype=jnp.float32) / np.sqrt(memory_dim)
        W_gate = jax.random.normal(ks[3], (d_model, 2 * d_model), dtype=jnp.float32) / np.sqrt(2 * d_model)
        b_gate = jax.random.normal(ks[4], (d_model,), dtype=jnp.float32) * 0.01
        norm_w = jnp.ones((d_model,), dtype=jnp.float32)
        return {'hidden_states': hidden_states, 'memory': memory, 'W_mem': W_mem, 'W_gate': W_gate, 'b_gate': b_gate, 'norm_w': norm_w}
    _L0_xattn_all = _L0_xattn_setup()
    _L0_xattn_in = {k: v for k, v in _L0_xattn_all.items() if k in ('W_mem', 'W_gate', 'b_gate', 'norm_w')}
    del _L0_xattn_all

    def _L1_xattn_setup():
        import jax, jax.numpy as jnp
        import numpy as np
        H = 512
        NH = 16
        HD = H // NH
        CH = 256
        CC = 256
        CHD = CC // NH
        I = 1376
        B = 2
        L = 512
        LE = 256
        EPS = 1e-06

        def rms_norm(x, w):
            xf = x.astype(jnp.float32)
            var = jnp.mean(xf * xf, axis=-1, keepdims=True)
            return (w * (xf * jax.lax.rsqrt(var + EPS))).astype(x.dtype)

        def expert_mask(tt):
            vm = jnp.zeros(tt.shape, dtype=bool)
            vm = vm.at[:, :-1].set((tt[:, :-1] == 1) & (tt[:, 1:] == 1))
            return vm

        def rotate_half(x):
            d = x.shape[-1] // 2
            return jnp.concatenate([-x[..., d:], x[..., :d]], axis=-1)

        def apply_rotary(q, k, position_ids, seq_len):
            inv = 1.0 / 10000.0 ** (jnp.arange(0, HD, 2, dtype=jnp.float32) / HD)
            t = jnp.arange(seq_len, dtype=jnp.float32)
            freqs = jnp.outer(t, inv)
            emb = jnp.concatenate([freqs, freqs], axis=-1)
            cos = jnp.cos(emb)[position_ids][:, None].astype(q.dtype)
            sin = jnp.sin(emb)[position_ids][:, None].astype(q.dtype)
            return (q * cos + rotate_half(q) * sin, k * cos + rotate_half(k) * sin)

        def sdpa(q, k, v, causal):
            scale = 1.0 / np.sqrt(q.shape[-1])
            scores = jnp.einsum('bhqd,bhkd->bhqk', q * scale, k)
            if causal:
                mask = jnp.tril(jnp.ones((q.shape[-2], k.shape[-2]), dtype=bool))
                scores = jnp.where(mask, scores, jnp.finfo(jnp.float32).min)
            p = jax.nn.softmax(scores.astype(jnp.float32), axis=-1).astype(q.dtype)
            return jnp.einsum('bhqk,bhkd->bhqd', p, v)

        def heads(x, nh, hd):
            b, l, _ = x.shape
            return x.reshape(b, l, nh, hd).transpose(0, 2, 1, 3)
        key = jax.random.key(seed)
        ks = jax.random.split(key, 20)
        s = 0.02
        f32 = jnp.float32
        return {'hidden_states': jax.random.normal(ks[0], (B, L, H), f32), 'encoder_outputs': jax.random.normal(ks[1], (B, LE, CH), f32), 'token_type_ids': jax.random.randint(ks[2], (B, L), 0, 2, jnp.int32), 'position_ids': jnp.arange(L, dtype=jnp.int32)[None, :], 'ln_in_w': jnp.ones((H,), f32), 'ln_post_attn_w': jnp.ones((H,), f32), 'ln_post_cross_w': jnp.ones((H,), f32), 'v_qkv': jax.random.normal(ks[3], (H, 3 * H), f32) * s, 'l_qkv': jax.random.normal(ks[4], (H, 3 * H), f32) * s, 'v_dense': jax.random.normal(ks[5], (H, H), f32) * s, 'l_dense': jax.random.normal(ks[6], (H, H), f32) * s, 'cq_w': jax.random.normal(ks[7], (H, CC), f32) * s, 'ckv_w': jax.random.normal(ks[8], (CH, 2 * CC), f32) * s, 'cdense_w': jax.random.normal(ks[9], (CC, H), f32) * s, 'v_gate': jax.random.normal(ks[10], (H, I), f32) * s, 'v_up': jax.random.normal(ks[11], (H, I), f32) * s, 'v_down': jax.random.normal(ks[12], (I, H), f32) * s, 'l_gate': jax.random.normal(ks[13], (H, I), f32) * s, 'l_up': jax.random.normal(ks[14], (H, I), f32) * s, 'l_down': jax.random.normal(ks[15], (I, H), f32) * s}
    _L1_xattn_all = _L1_xattn_setup()
    _L1_xattn_in = {k: v for k, v in _L1_xattn_all.items() if k in ('ln_in_w', 'ln_post_attn_w', 'ln_post_cross_w', 'v_qkv', 'l_qkv', 'v_dense', 'l_dense', 'cq_w', 'ckv_w', 'cdense_w', 'v_gate', 'v_up', 'v_down', 'l_gate', 'l_up', 'l_down')}
    del _L1_xattn_all
    return {'x': x, 'ctx_1024': ctx_1024, 'pos_1xS': pos_1xS, 'mask_BxS_ik0': mask_BxS_ik0, 'L0_xattn_W_mem': _L0_xattn_in['W_mem'], 'L0_xattn_W_gate': _L0_xattn_in['W_gate'], 'L0_xattn_b_gate': _L0_xattn_in['b_gate'], 'L0_xattn_norm_w': _L0_xattn_in['norm_w'], 'L1_xattn_ln_in_w': _L1_xattn_in['ln_in_w'], 'L1_xattn_ln_post_attn_w': _L1_xattn_in['ln_post_attn_w'], 'L1_xattn_ln_post_cross_w': _L1_xattn_in['ln_post_cross_w'], 'L1_xattn_v_qkv': _L1_xattn_in['v_qkv'], 'L1_xattn_l_qkv': _L1_xattn_in['l_qkv'], 'L1_xattn_v_dense': _L1_xattn_in['v_dense'], 'L1_xattn_l_dense': _L1_xattn_in['l_dense'], 'L1_xattn_cq_w': _L1_xattn_in['cq_w'], 'L1_xattn_ckv_w': _L1_xattn_in['ckv_w'], 'L1_xattn_cdense_w': _L1_xattn_in['cdense_w'], 'L1_xattn_v_gate': _L1_xattn_in['v_gate'], 'L1_xattn_v_up': _L1_xattn_in['v_up'], 'L1_xattn_v_down': _L1_xattn_in['v_down'], 'L1_xattn_l_gate': _L1_xattn_in['l_gate'], 'L1_xattn_l_up': _L1_xattn_in['l_up'], 'L1_xattn_l_down': _L1_xattn_in['l_down']}

def reference(x, ctx_1024, pos_1xS, mask_BxS_ik0, L0_xattn_W_mem, L0_xattn_W_gate, L0_xattn_b_gate, L0_xattn_norm_w, L1_xattn_ln_in_w, L1_xattn_ln_post_attn_w, L1_xattn_ln_post_cross_w, L1_xattn_v_qkv, L1_xattn_l_qkv, L1_xattn_v_dense, L1_xattn_l_dense, L1_xattn_cq_w, L1_xattn_ckv_w, L1_xattn_cdense_w, L1_xattn_v_gate, L1_xattn_v_up, L1_xattn_v_down, L1_xattn_l_gate, L1_xattn_l_up, L1_xattn_l_down):
    import jax
    import jax.numpy as jnp

    def _L0_xattn_ref(hidden_states, memory, W_mem, W_gate, b_gate, norm_w):
        import jax, jax.numpy as jnp
        import numpy as np
        EPS = 1e-06

        def _rmsnorm(x, w):
            var = jnp.mean(jnp.square(x), axis=-1, keepdims=True)
            return x * jax.lax.rsqrt(var + EPS) * w
        D = hidden_states.shape[-1]
        memory_proj = jnp.einsum('bme,de->bmd', memory, W_mem)
        scores = jnp.einsum('bnd,bmd->bnm', hidden_states, memory_proj) / jnp.sqrt(jnp.float32(D))
        attn = jax.nn.softmax(scores, axis=-1)
        memory_context = jnp.einsum('bnm,bmd->bnd', attn, memory_proj)
        gate_input = jnp.concatenate([hidden_states, memory_context], axis=-1)
        gate = jax.nn.sigmoid(jnp.einsum('bnf,df->bnd', gate_input, W_gate) + b_gate)
        fused = hidden_states + gate * memory_context
        return _rmsnorm(fused, norm_w)

    def _L1_xattn_ref(hidden_states, encoder_outputs, token_type_ids, position_ids, ln_in_w, ln_post_attn_w, ln_post_cross_w, v_qkv, l_qkv, v_dense, l_dense, cq_w, ckv_w, cdense_w, v_gate, v_up, v_down, l_gate, l_up, l_down):
        import jax, jax.numpy as jnp
        import numpy as np
        H = 512
        NH = 16
        HD = H // NH
        CH = 256
        CC = 256
        CHD = CC // NH
        I = 1376
        B = 2
        L = 512
        LE = 256
        EPS = 1e-06

        def rms_norm(x, w):
            xf = x.astype(jnp.float32)
            var = jnp.mean(xf * xf, axis=-1, keepdims=True)
            return (w * (xf * jax.lax.rsqrt(var + EPS))).astype(x.dtype)

        def expert_mask(tt):
            vm = jnp.zeros(tt.shape, dtype=bool)
            vm = vm.at[:, :-1].set((tt[:, :-1] == 1) & (tt[:, 1:] == 1))
            return vm

        def rotate_half(x):
            d = x.shape[-1] // 2
            return jnp.concatenate([-x[..., d:], x[..., :d]], axis=-1)

        def apply_rotary(q, k, position_ids, seq_len):
            inv = 1.0 / 10000.0 ** (jnp.arange(0, HD, 2, dtype=jnp.float32) / HD)
            t = jnp.arange(seq_len, dtype=jnp.float32)
            freqs = jnp.outer(t, inv)
            emb = jnp.concatenate([freqs, freqs], axis=-1)
            cos = jnp.cos(emb)[position_ids][:, None].astype(q.dtype)
            sin = jnp.sin(emb)[position_ids][:, None].astype(q.dtype)
            return (q * cos + rotate_half(q) * sin, k * cos + rotate_half(k) * sin)

        def sdpa(q, k, v, causal):
            scale = 1.0 / np.sqrt(q.shape[-1])
            scores = jnp.einsum('bhqd,bhkd->bhqk', q * scale, k)
            if causal:
                mask = jnp.tril(jnp.ones((q.shape[-2], k.shape[-2]), dtype=bool))
                scores = jnp.where(mask, scores, jnp.finfo(jnp.float32).min)
            p = jax.nn.softmax(scores.astype(jnp.float32), axis=-1).astype(q.dtype)
            return jnp.einsum('bhqk,bhkd->bhqd', p, v)

        def heads(x, nh, hd):
            b, l, _ = x.shape
            return x.reshape(b, l, nh, hd).transpose(0, 2, 1, 3)
        b, l, _ = hidden_states.shape
        vm = expert_mask(token_type_ids)[..., None]
        residual = hidden_states
        x = rms_norm(hidden_states, ln_in_w)
        mixed = jnp.where(vm, x @ v_qkv, x @ l_qkv)
        q, k, v = jnp.split(mixed, 3, axis=-1)
        q, k, v = (heads(q, NH, HD), heads(k, NH, HD), heads(v, NH, HD))
        q, k = apply_rotary(q, k, position_ids, l)
        ctx = sdpa(q, k, v, causal=True)
        ctx = ctx.transpose(0, 2, 1, 3).reshape(b, l, H)
        attn_out = jnp.where(vm, ctx @ v_dense, ctx @ l_dense)
        hidden_states = residual + attn_out
        ci = rms_norm(hidden_states, ln_post_cross_w)
        cq = heads(ci @ cq_w, NH, CHD)
        ckv = encoder_outputs @ ckv_w
        ck, cv = jnp.split(ckv, 2, axis=-1)
        ck, cv = (heads(ck, NH, CHD), heads(cv, NH, CHD))
        cctx = sdpa(cq, ck, cv, causal=False)
        cctx = cctx.transpose(0, 2, 1, 3).reshape(b, l, CC)
        hidden_states = hidden_states + cctx @ cdense_w
        mi = rms_norm(hidden_states, ln_post_attn_w)
        v_out = jax.nn.silu(mi @ v_gate) * (mi @ v_up) @ v_down
        l_out = jax.nn.silu(mi @ l_gate) * (mi @ l_up) @ l_down
        hidden_states = hidden_states + jnp.where(vm, v_out, l_out)
        return hidden_states
    x = _L0_xattn_ref(x, ctx_1024, L0_xattn_W_mem, L0_xattn_W_gate, L0_xattn_b_gate, L0_xattn_norm_w)
    x = _L1_xattn_ref(x, ctx_1024, mask_BxS_ik0, pos_1xS, L1_xattn_ln_in_w, L1_xattn_ln_post_attn_w, L1_xattn_ln_post_cross_w, L1_xattn_v_qkv, L1_xattn_l_qkv, L1_xattn_v_dense, L1_xattn_l_dense, L1_xattn_cq_w, L1_xattn_ckv_w, L1_xattn_cdense_w, L1_xattn_v_gate, L1_xattn_v_up, L1_xattn_v_down, L1_xattn_l_gate, L1_xattn_l_up, L1_xattn_l_down)
    return x

_drawn_inputs = setup_inputs


def setup_inputs(seed=0):
    import zlib

    import numpy as np

    out = dict(_drawn_inputs(seed))
    spreads = {'L0_xattn_norm_w': (1.0, 0.2),
     'L1_xattn_ln_in_w': (1.0, 0.6),
     'L1_xattn_ln_post_attn_w': (1.0, 0.6),
     'L1_xattn_ln_post_cross_w': (1.0, 0.6)}
    factors = {'L0_xattn_b_gate': 8.0,
     'L1_xattn_v_qkv': 8.0,
     'L1_xattn_v_dense': 3.31,
     'L1_xattn_cq_w': 37.968,
     'L1_xattn_ckv_w': 2.769,
     'L1_xattn_cdense_w': 2.856,
     'L1_xattn_v_gate': 2.947,
     'L1_xattn_v_up': 2.845,
     'L1_xattn_v_down': 2.852}
    for name, (base, spread) in spreads.items():
        noise = np.random.default_rng([zlib.crc32(name.encode()), seed]).standard_normal(out[name].shape)
        drawn = base * np.exp(spread * noise) if base else spread * noise
        out[name] = jnp.asarray(drawn.astype(out[name].dtype))
    for name, factor in factors.items():
        out[name] = (out[name] * factor).astype(out[name].dtype)
    return out
```

```python
import concourse.bass as bass
from concourse import mybir
from contextlib import ExitStack

B, S, D = 4, 512, 512
KEYS, E = 1601, 256
P = 128
DT, ET, ST = D // P, E // P, S // P
KT = -(-KEYS // P)
KEY_TILES = [(i * P, min(P, KEYS - i * P)) for i in range(KT)]
KEY_BANKS = [(i * S, min(S, KEYS - i * S)) for i in range(-(-KEYS // S))]
KPAD = KEYS + KEYS % 2
NH, HD, CHD = 16, 32, 16
HIDDEN = 1376
HID_TILES = [(i * P, min(P, HIDDEN - i * P)) for i in range(-(-HIDDEN // P))]
EPS = 1e-6
MAXW = 402
MAX_STARTS = [0, 400, 800, KEYS - MAXW]
BIG = -1e30


def program(nc, t, out):
    f32, f32r, bf16, i32 = mybir.dt.float32, mybir.dt.float32r, mybir.dt.bfloat16, mybir.dt.int32
    ALU, ACT, AX = mybir.AluOpType, mybir.ActivationFunctionType, mybir.AxisListType

    def scratch(name, shape, dt=f32):
        return nc.dram_tensor(name, shape, dt, kind="Internal").ap()

    wmT_d = scratch("w_mem_transposed", [E, D])
    wgT_d = scratch("w_gate_transposed", [2 * D, D])
    cd_d = scratch("w_cross_dense_padded", [D, D])
    ones_d = scratch("ones_rows", [NH // 2, KPAD])
    h_d = scratch("stream_after_attention", [B, P, DT, S])
    keep_d = scratch("keep_expert_by_token", [2, B, S])

    with ExitStack() as keep:
        made = {}

        def sb(name, shape, dt=f32, ctx=keep):
            made[name] = made.get(name, 0) + 1
            return ctx.enter_context(nc.sbuf_tensor(f"{name}_{made[name]}" if made[name] > 1 else name, shape, dt))

        ps = keep.enter_context(nc.psum_tensor("ps", [P, 8, 512], f32))
        ident, neg_ident, ones = sb("ident", [P, P]), sb("neg_ident", [P, P]), sb("ones", [P, P])
        ones_r = sb("ones_r", [P, P], f32r)
        ident_b = sb("ident_b", [P, P], bf16)
        mask_qk, mask_kq = sb("mask_qk", [P, P], bf16), sb("mask_kq", [P, P], bf16)
        rot = sb("rot", [P, P])
        cos_t, sin_t = sb("cos_t", [P, S]), sb("sin_t", [P, S])
        cols = sb("cols", [P, 5, DT])
        eps_col = sb("eps_col", [P, 1])
        h = sb("h", [P, DT, S])
        sel = sb("sel", [P, P])
        RAW, SPLIT = 4, 4
        w_raw = sb("w_raw", [P, RAW, 512])
        w_hi, w_lo = sb("w_hi", [P, SPLIT, 512], f32r), sb("w_lo", [P, SPLIT, 512], f32r)
        rstd = sb("rstd", [P, S])
        keep_expert = sb("keep_expert", [P, 2, S])

        def clear(sems):
            nc.all_engine_barrier()
            lo, hi = min(s.num for s in sems), max(s.num for s in sems)
            nc.gpsimd.sem_clear(range(lo, hi + 1))
            nc.all_engine_barrier()

        def stage(names):
            ctx = ExitStack()
            sems = [ctx.enter_context(nc.semaphore(n)) for n in names.split()]
            return ctx, sems

        ctx, sems = stage("s_z s_zd s_one s_const s_raw s_tr s_ev s_st s_pos s_hot s_tab s_cast s_w s_ms")
        s_z, s_zd, s_one, s_const, s_raw, s_tr, s_ev, s_st, s_pos, s_hot, s_tab, s_cast, s_w, s_ms = sems
        with ctx:
            tab = sb("tab", [P, ST, 2, P], ctx=ctx)
            masks = sb("masks", [P, 2, P], ctx=ctx)
            posi = sb("posi", [P, S], i32, ctx=ctx)
            posf, wrap = sb("posf", [P, S], ctx=ctx), sb("wrap", [P, S], ctx=ctx)
            tpos = sb("tpos", [P, ST], ctx=ctx)
            hot = sb("hot", [P, ST, S], ctx=ctx)
            wm = sb("wm", [P, DT, E], ctx=ctx)
            wg = sb("wg", [P, DT, 2 * D], ctx=ctx)
            ones_big = sb("ones_big", [NH // 2, KPAD], ctx=ctx)
            zeros = sb("zeros", [P, DT, D], ctx=ctx)
            wmT, wgT = sb("wmT", [P, ET, D], ctx=ctx), sb("wgT", [P, 2 * DT, D], ctx=ctx)
            with nc.Block() as block:
                @block.sync
                def _(sp):
                    for dst, src in ((ident[:, :], t["c_ident"]), (rot[:, :], t["c_rot"]), (sel[:, :], t["c_sel"]),
                                     (masks[:, :, :], t["c_masks"]),
                                     (tab[:, :, :, :], t["c_tab"].rearrange("(a p) c n -> p a c n", p=P)),
                                     (tpos[:, :], t["c_tpos"])):
                        sp.dma_start(dst, src).then_inc(s_const, 16)
                    sp.dma_start(wm[:, :, :], t["L0_xattn_W_mem"].rearrange("(a p) n -> p a n", p=P)).then_inc(s_raw, 16)
                    sp.dma_start(wg[:, :, :], t["L0_xattn_W_gate"].rearrange("(a p) n -> p a n", p=P)).then_inc(s_raw, 16)
                    sp.wait_ge(s_ev, 10)
                    sp.dma_start(wmT_d.rearrange("(a p) n -> p a n", p=P), wmT[:, :, :]).then_inc(s_st, 16)
                    sp.dma_start(wgT_d.rearrange("(a p) n -> p a n", p=P), wgT[:, :, :]).then_inc(s_st, 16)
                    sp.wait_ge(s_z, 1)
                    sp.dma_start(cd_d.rearrange("(a p) n -> p a n", p=P), zeros[:, :, :]).then_inc(s_zd, 16)
                    sp.wait_ge(s_zd, 16)
                    sp.dma_start(cd_d.rearrange("(h r) n -> h r n", r=HD)[:, 0:CHD, :],
                                 t["L1_xattn_cdense_w"].rearrange("(h r) n -> h r n", r=CHD)).then_inc(s_st, 16)
                    sp.wait_ge(s_one, 1)
                    sp.dma_start(ones_d, ones_big[:, :]).then_inc(s_st, 16)
                    sp.wait_ge(s_st, 64)

                @block.scalar
                def _(act):
                    act.dma_start(posi[:, :], t["pos_1xS"].broadcast_to((P, S))).then_inc(s_pos, 16)
                    act.dma_start(cols[:, :, :], t["columns"]).then_inc(s_w, 16)
                    act.wait_ge(s_w, 16)

                @block.vector
                def _(dve):
                    nc.vector.memset(ones[:, :], 1.0).then_inc(s_ms, 1)
                    nc.vector.memset(eps_col[:, :], EPS).then_inc(s_ms, 1)
                    nc.vector.memset(zeros[:, :, :], 0.0).then_inc(s_z, 1)
                    dve.wait_ge(s_ms, 2)
                    nc.vector.tensor_copy(ones_r[:, :], ones[:, :])
                    nc.vector.memset(ones_big[:, :], 1.0).then_inc(s_one, 1)
                    dve.wait_ge(s_pos, 16)
                    nc.vector.tensor_copy(posf[:, :], posi[:, :]).then_inc(s_hot, 1)
                    dve.wait_ge(s_hot, 1)
                    nc.vector.tensor_scalar(wrap[:, :], posf[:, :], 0.0, float(S), ALU.is_lt, ALU.mult).then_inc(s_hot, 1)
                    dve.wait_ge(s_hot, 2)
                    nc.vector.tensor_tensor(out=posf[:, :], in0=posf[:, :], in1=wrap[:, :], op=ALU.add).then_inc(s_hot, 1)
                    dve.wait_ge(s_hot, 3)
                    nc.vector.tensor_scalar(posf[:, :], posf[:, :], 0.0, float(S - 1), ALU.max, ALU.min).then_inc(s_hot, 1)
                    dve.wait_ge(s_hot, 4)
                    dve.wait_ge(s_const, 96)
                    nc.vector.tensor_copy(ident_b[:, :], ident[:, :])
                    nc.vector.tensor_scalar(neg_ident[:, :], ident[:, :], -1.0, None, ALU.mult)
                    nc.vector.tensor_copy(mask_qk[:, :], masks[:, 0, :])
                    nc.vector.tensor_copy(mask_kq[:, :], masks[:, 1, :])
                    for a in range(ST):
                        nc.vector.tensor_scalar(hot[:, a, :], posf[:, :], tpos[:, a:a + 1], None,
                                                ALU.is_equal).then_inc(s_hot, 1)
                    dve.wait_ge(s_tab, 2)
                    nc.vector.tensor_copy(cos_t[:, :], ps[:, 0, :]).then_inc(s_cast, 1)
                    nc.vector.tensor_copy(sin_t[:, :], ps[:, 1, :]).then_inc(s_cast, 1)
                    for i in range(10):
                        dve.wait_ge(s_tr, i + 1)
                        dst = wmT[:, i, :] if i < ET else wgT[:, i - ET, :]
                        nc.vector.tensor_copy(dst, ps[:, 2 + i % 6, :]).then_inc(s_ev, 1)

                @block.tensor
                def _(pe):
                    pe.wait_ge(s_hot, 4 + ST)
                    for c in range(2):
                        for a in range(ST):
                            last = nc.tensor.matmul(ps[:, c, :], tab[:, a, c, :], hot[:, a, :],
                                                    start=a == 0, stop=a == ST - 1)
                        last.then_inc(s_tab, 1)
                    pe.wait_ge(s_raw, 32)
                    for i in range(10):
                        if i >= 6:
                            pe.wait_ge(s_ev, i - 5)
                        src, e = (wm, i) if i < ET else (wg, i - ET)
                        for a in range(DT):
                            last = nc.tensor.transpose(ps[:, 2 + i % 6, a * P:(a + 1) * P],
                                                       src[:, a, e * P:(e + 1) * P], ident[:, :])
                        last.then_inc(s_tr, 1)
            clear(sems)


        def load_w(sp, n, src, s_loaded, s_split):
            rows, width = src.shape[0], src.shape[-1] * (src.shape[1] if len(src.shape) == 3 else 1)
            if n >= RAW:
                sp.wait_ge(s_split, n - RAW + 1)
            dst = w_raw[0:rows, n % RAW, 0:width]
            if len(src.shape) == 3:
                dst = dst.rearrange("p (a n) -> p a n", n=src.shape[-1])
            sp.dma_start(dst, src).then_inc(s_loaded[n % RAW], 16)

        def split_w(dve, n, s_loaded, s_high, s_split, s_used, rows=P, width=512):
            raw, hi, lo = (x[0:rows, n % k, 0:width] for x, k in ((w_raw, RAW), (w_hi, SPLIT), (w_lo, SPLIT)))
            dve.wait_ge(s_loaded[n % RAW], 16 * (n // RAW + 1))
            if n >= SPLIT:
                dve.wait_ge(s_used, n - SPLIT + 1)
            nc.vector.tensor_copy(hi, raw).then_inc(s_high, 1)
            dve.wait_ge(s_high, n + 1)
            nc.vector.tensor_tensor(out=lo, in0=raw, in1=hi.bitcast(f32), op=ALU.subtract).then_inc(s_split, 1)

        def three(dst, ah, al, bh, bl, start, stop):
            nc.tensor.matmul(dst, ah, bh, start=start, stop=False)
            nc.tensor.matmul(dst, al, bh, start=False, stop=False)
            return nc.tensor.matmul(dst, ah, bl, start=False, stop=stop)

        WSEMS = " ".join(f"s_wl{i}" for i in range(RAW)) + " s_wh s_ws s_wu "

        def memory_attention(b, xT, xh, xl, cn_h, cn_l):
            NU = DT + ET * len(KEY_BANKS)
            names = ("s_x s_c s_tr s_th s_tl s_uh s_ul s_max s_mx s_dg s_sc s_exp s_acc s_pv s_pad "
                     "s_sum s_cn " + WSEMS)
            ctx, sems = stage(names)
            s = dict(zip(names.split(), sems))
            wl = [s[f"s_wl{i}"] for i in range(RAW)]
            with ctx:
                xs = sb("xs", [P, ST, D], ctx=ctx)
                cs = sb("cs", [P, KT, E], ctx=ctx)
                ch, cl = sb("ch", [P, ET, KPAD], f32r, ctx=ctx), sb("cl", [P, ET, KPAD], f32r, ctx=ctx)
                uh, ul = sb("uh", [P, ET, S], f32r, ctx=ctx), sb("ul", [P, ET, S], f32r, ctx=ctx)
                row_max = sb("row_max", [P, ST], ctx=ctx)
                shift = sb("shift", [P, ST, P], f32r, ctx=ctx)
                pT = sb("pT", [P, 3, S], ctx=ctx)
                acc = sb("acc", [P, S], ctx=ctx)
                rin, tmp = sb("rin", [P, S], ctx=ctx), sb("tmp", [P, ET, S], ctx=ctx)
                units = [("x", k, 0) for k in range(DT)] + [("c", e, kb) for e in range(ET)
                                                            for kb in range(len(KEY_BANKS))]
                with nc.Block() as block:
                    @block.sync
                    def _(sp):
                        sp.dma_start(xs[:, :, :], t["x"][b].rearrange("(a p) n -> p a n", p=P)).then_inc(s["s_x"], 16)
                        full = KEYS // P
                        sp.dma_start(cs[:, 0:full, :], t["ctx_1024"][b, 0:full * P].rearrange("(a p) n -> p a n", p=P))\
                            .then_inc(s["s_c"], 16)
                        sp.dma_start(cs[0:KEYS - full * P, full, :], t["ctx_1024"][b, full * P:KEYS]).then_inc(s["s_c"], 16)
                        for k in range(DT):
                            load_w(sp, k, t["L0_xattn_W_mem"][k * P:(k + 1) * P, :], wl, s["s_ws"])

                    @block.scalar
                    def _(act):
                        for i, (what, k, kb) in enumerate(units):
                            act.wait_ge(s["s_tr"], i + 1)
                            k0, kn = (0, S) if what == "x" else KEY_BANKS[kb]
                            dst = xh[:, k, :] if what == "x" else ch[:, k, k0:k0 + kn]
                            nc.scalar.activation(dst, ps[:, i % 8, 0:kn], ACT.Copy).then_inc(s["s_th"], 1)
                        act.wait_ge(s["s_wu"], DT)
                        for e in range(ET):
                            nc.scalar.activation(uh[:, e, :], ps[:, e, :], ACT.Copy).then_inc(s["s_uh"], 1)
                        for kt, (k0, kn) in enumerate(KEY_TILES):
                            act.wait_ge(s["s_sc"], kt + 1)
                            if kt >= 3:
                                act.wait_ge(s["s_pv"], kt - 2)
                                act.wait_ge(s["s_acc"], kt - 2)
                            nc.scalar.activation(pT[0:kn, kt % 3, :], ps[0:kn, 4 + kt % 3, :], ACT.Exp,
                                                 scale=float(D) ** -0.5).then_inc(s["s_exp"], 1)

                    @block.gpsimd
                    def _(pool):
                        for kt, (k0, kn) in enumerate(KEY_TILES):
                            pool.wait_ge(s["s_exp"], kt + 1)
                            if kt == 0:
                                nc.gpsimd.tensor_copy(acc[:, :], pT[:, 0, :]).then_inc(s["s_acc"], 1)
                            else:
                                pool.wait_ge(s["s_acc"], kt)
                                nc.gpsimd.tensor_tensor(out=acc[0:kn, :], in0=acc[0:kn, :], in1=pT[0:kn, kt % 3, :],
                                                        op=ALU.add).then_inc(s["s_acc"], 1)

                    @block.vector
                    def _(dve):
                        nc.vector.memset(ch[:, :, KEYS:KPAD].bitcast(f32), 0.0)
                        nc.vector.memset(cl[:, :, KEYS:KPAD].bitcast(f32), 0.0)
                        for k in range(SPLIT):
                            split_w(dve, k, wl, s["s_wh"], s["s_ws"], s["s_wu"], width=E)
                        for i, (what, k, kb) in enumerate(units):
                            dve.wait_ge(s["s_th"], i + 1)
                            if what == "x":
                                nc.vector.tensor_copy(xT[:, k, :], ps[:, i % 8, :])
                            k0, kn = (0, S) if what == "x" else KEY_BANKS[kb]
                            hi, lo = (xh[:, k, :], xl[:, k, :]) if what == "x" else (ch[:, k, k0:k0 + kn], cl[:, k, k0:k0 + kn])
                            nc.vector.tensor_tensor(out=lo, in0=ps[:, i % 8, 0:kn], in1=hi.bitcast(f32),
                                                    op=ALU.subtract).then_inc(s["s_tl"], 1)
                        for k in range(SPLIT, DT):
                            split_w(dve, k, wl, s["s_wh"], s["s_ws"], s["s_wu"], width=E)
                        for e in range(ET):
                            dve.wait_ge(s["s_uh"], e + 1)
                            nc.vector.tensor_tensor(out=ul[:, e, :], in0=ps[:, e, :], in1=uh[:, e, :].bitcast(f32),
                                                    op=ALU.subtract).then_inc(s["s_ul"], 1)
                        for q in range(ST):
                            dve.wait_ge(s["s_max"], q + 1)
                            at = 4 - 4 * (q % 2)
                            nc.vector.tensor_reduce(out=row_max[:, q:q + 1], in_=ps[:, at:at + 4, 0:MAXW],
                                                    axis=AX.XY, op=ALU.max).then_inc(s["s_mx"], 1)
                            dve.wait_ge(s["s_mx"], q + 1)
                            nc.vector.tensor_scalar(shift[:, q, :], neg_ident[:, :], row_max[:, q:q + 1], None,
                                                    ALU.mult).then_inc(s["s_dg"], 1)
                        dve.wait_ge(s["s_sum"], 1)
                        nc.vector.reciprocal(rin[:, :], ps[:, 7, :]).then_inc(s["s_cn"], 1)
                        dve.wait_ge(s["s_cn"], 1)
                        for e in range(ET):
                            nc.vector.tensor_tensor(out=tmp[:, e, :], in0=ps[:, e, :], in1=rin[:, :], op=ALU.mult)\
                                .then_inc(s["s_cn"], 1)
                            dve.wait_ge(s["s_cn"], 2 + 3 * e)
                            nc.vector.tensor_copy(cn_h[:, e, :], tmp[:, e, :]).then_inc(s["s_cn"], 1)
                            dve.wait_ge(s["s_cn"], 3 + 3 * e)
                            nc.vector.tensor_tensor(out=cn_l[:, e, :], in0=tmp[:, e, :], in1=cn_h[:, e, :].bitcast(f32),
                                                    op=ALU.subtract).then_inc(s["s_cn"], 1)

                    @block.tensor
                    def _(pe):
                        pe.wait_ge(s["s_x"], 16)
                        for i, (what, k, kb) in enumerate(units):
                            if i == DT:
                                pe.wait_ge(s["s_c"], 32)
                            if i >= 8:
                                pe.wait_ge(s["s_tl"], i - 7)
                            if what == "x":
                                for a in range(ST):
                                    last = nc.tensor.transpose(ps[:, i % 8, a * P:(a + 1) * P],
                                                               xs[:, a, k * P:(k + 1) * P], ident[:, :])
                            else:
                                k0, kn = KEY_BANKS[kb]
                                for a in range(-(-kn // P)):
                                    n = min(P, kn - a * P)
                                    last = nc.tensor.transpose(ps[:, i % 8, a * P:a * P + n],
                                                               cs[0:n, k0 // P + a, k * P:(k + 1) * P],
                                                               ident[0:n, 0:n])
                            last.then_inc(s["s_tr"], 1)
                        pe.wait_ge(s["s_tl"], NU)
                        for k in range(DT):
                            pe.wait_ge(s["s_ws"], k + 1)
                            for e in range(ET):
                                cut = slice(e * P, (e + 1) * P)
                                last = three(ps[:, e, :], w_hi[:, k % SPLIT, cut], w_lo[:, k % SPLIT, cut],
                                             xh[:, k, :], xl[:, k, :], k == 0, k == DT - 1)
                            last.then_inc(s["s_wu"], 1)
                        pe.wait_ge(s["s_uh"], ET)
                        for q in range(ST):
                            at = 4 - 4 * (q % 2)
                            if q == 1:
                                pe.wait_ge(s["s_ul"], ET)
                            if q >= 2:
                                pe.wait_ge(s["s_mx"], q - 1)
                            for e in range(ET):
                                for n, k0 in enumerate(MAX_STARTS):
                                    last = nc.tensor.matmul(ps[:, at + n, 0:MAXW], uh[:, e, q * P:(q + 1) * P],
                                                            ch[:, e, k0:k0 + MAXW], start=e == 0, stop=e == ET - 1)
                            last.then_inc(s["s_max"], 1)
                        pe.wait_ge(s["s_mx"], ST)
                        pe.wait_ge(s["s_dg"], ST)

                        def scores(kt):
                            k0, kn = KEY_TILES[kt]
                            if kt >= 3:
                                pe.wait_ge(s["s_exp"], kt - 2)
                            bank = ps[0:kn, 4 + kt % 3, :]
                            nc.tensor.matmul(bank, ones_r[:, 0:kn], shift[:, :, :].rearrange("p a n -> p (a n)"),
                                             start=True, stop=False)
                            for e in range(ET):
                                last = three(bank, ch[:, e, k0:k0 + kn], cl[:, e, k0:k0 + kn], uh[:, e, :], ul[:, e, :],
                                             False, e == ET - 1)
                            last.then_inc(s["s_sc"], 1)

                        scores(0)
                        scores(1)
                        for kt, (k0, kn) in enumerate(KEY_TILES):
                            if kt + 2 < KT:
                                scores(kt + 2)
                            pe.wait_ge(s["s_exp"], kt + 1)
                            for e in range(ET):
                                last = nc.tensor.matmul(ps[:, e, :], cs[0:kn, kt, e * P:(e + 1) * P],
                                                        pT[0:kn, kt % 3, :], start=kt == 0, stop=kt == KT - 1)
                            last.then_inc(s["s_pv"], 1)
                        pe.wait_ge(s["s_acc"], KT)
                        nc.tensor.matmul(ps[:, 7, :], ones[:, :], acc[:, :], start=True, stop=True).then_inc(s["s_sum"], 1)
                clear(sems)

        def gate(xT, xh, xl, cn_h, cn_l):
            names = "s_mch s_mcc s_mcl s_eg s_g " + WSEMS
            ctx, sems = stage(names)
            s = dict(zip(names.split(), sems))
            wl = [s[f"s_wl{i}"] for i in range(RAW)]
            NW = ET + 2 * DT
            with ctx:
                mc, eg = sb("mc", [P, DT, S], ctx=ctx), sb("eg", [P, DT, S], ctx=ctx)
                mch, mcl = sb("mch", [P, DT, S], f32r, ctx=ctx), sb("mcl", [P, DT, S], f32r, ctx=ctx)
                with nc.Block() as block:
                    @block.sync
                    def _(sp):
                        for n in range(NW):
                            src = wmT_d[n * P:(n + 1) * P, :] if n < ET else wgT_d[(n - ET) * P:(n - ET + 1) * P, :]
                            load_w(sp, n, src, wl, s["s_ws"])

                    @block.scalar
                    def _(act):
                        act.wait_ge(s["s_wu"], ET)
                        for j in range(DT):
                            nc.scalar.activation(mch[:, j, :], ps[:, j, :], ACT.Copy).then_inc(s["s_mch"], 1)
                        act.wait_ge(s["s_wu"], NW)
                        for j in range(DT):
                            nc.scalar.activation(eg[:, j, :], ps[:, 4 + j, :], ACT.Sigmoid, bias=cols[:, 4, j:j + 1])\
                                .then_inc(s["s_eg"], 1)

                    @block.vector
                    def _(dve):
                        for n in range(NW):
                            if n == ET + SPLIT:
                                for j in range(DT):
                                    dve.wait_ge(s["s_mch"], j + 1)
                                    nc.vector.tensor_copy(mc[:, j, :], ps[:, j, :]).then_inc(s["s_mcc"], 1)
                                    nc.vector.tensor_tensor(out=mcl[:, j, :], in0=ps[:, j, :],
                                                            in1=mch[:, j, :].bitcast(f32), op=ALU.subtract)\
                                        .then_inc(s["s_mcl"], 1)
                            split_w(dve, n, wl, s["s_wh"], s["s_ws"], s["s_wu"])
                        for j in range(DT):
                            dve.wait_ge(s["s_eg"], j + 1)
                            nc.vector.tensor_tensor(out=eg[:, j, :], in0=eg[:, j, :], in1=mc[:, j, :], op=ALU.mult)\
                                .then_inc(s["s_g"], 1)
                            dve.wait_ge(s["s_g"], 2 * j + 1)
                            nc.vector.tensor_tensor(out=h[:, j, :], in0=eg[:, j, :], in1=xT[:, j, :], op=ALU.add)\
                                .then_inc(s["s_g"], 1)

                    @block.tensor
                    def _(pe):
                        for n in range(NW):
                            pe.wait_ge(s["s_ws"], n + 1)
                            if n < ET:
                                rh, rl, at = cn_h[:, n, :], cn_l[:, n, :], 0
                                first, end = n == 0, n == ET - 1
                            else:
                                k = n - ET
                                if k == DT:
                                    pe.wait_ge(s["s_mcl"], DT)
                                rh, rl = (xh[:, k, :], xl[:, k, :]) if k < DT else (mch[:, k - DT, :], mcl[:, k - DT, :])
                                at, first, end = 4, k == 0, k == 2 * DT - 1
                            for j in range(DT):
                                cut = slice(j * P, (j + 1) * P)
                                last = three(ps[:, at + j, :], w_hi[:, n % SPLIT, cut], w_lo[:, n % SPLIT, cut], rh, rl,
                                             first, end)
                            last.then_inc(s["s_wu"], 1)
                clear(sems)

        def norm(w, outs):
            names = "s_sq s_ss s_ln s_rs s_n s_hi"
            ctx, sems = stage(names)
            s = dict(zip(names.split(), sems))
            with ctx:
                sq = sb("sq", [P, DT, S], ctx=ctx)
                lnv = sb("lnv", [P, S], ctx=ctx)
                kept = sb("kept", [P, 2, S], ctx=ctx)
                full = sb("full", [P, 2, S], ctx=ctx)
                with nc.Block() as block:
                    @block.scalar
                    def _(act):
                        for k in range(DT):
                            nc.scalar.activation(sq[:, k, :], h[:, k, :], ACT.Square).then_inc(s["s_sq"], 1)
                        act.wait_ge(s["s_ss"], 1)
                        nc.scalar.activation(lnv[:, :], ps[:, 0, :], ACT.Ln, bias=eps_col[:, 0:1], scale=1.0 / D)\
                            .then_inc(s["s_ln"], 1)
                        act.wait_ge(s["s_ln"], 1)
                        nc.scalar.activation(rstd[:, :], lnv[:, :], ACT.Exp, scale=-0.5).then_inc(s["s_rs"], 1)
                        if outs is not h:
                            for n, (e, k) in enumerate((e, k) for e in range(len(outs)) for k in range(DT)):
                                act.wait_ge(s["s_n"], 2 * n + 1)
                                nc.scalar.activation(outs[e][0][:, k, :], full[:, n % 2, :], ACT.Copy).then_inc(s["s_hi"], 1)

                    @block.tensor
                    def _(pe):
                        for k in range(DT):
                            pe.wait_ge(s["s_sq"], k + 1)
                            last = nc.tensor.matmul(ps[:, 0, :], ones[:, :], sq[:, k, :], start=k == 0, stop=k == DT - 1)
                        last.then_inc(s["s_ss"], 1)

                    @block.vector
                    def _(dve):
                        dve.wait_ge(s["s_rs"], 1)
                        if outs is h:
                            for k in range(DT):
                                nc.vector.scalar_tensor_tensor(out=h[:, k, :], in0=h[:, k, :], scalar=cols[:, w, k:k + 1],
                                                               in1=rstd[:, :], op0=ALU.mult, op1=ALU.mult)
                        else:
                            for e in range(len(outs)):
                                scale = rstd
                                if len(outs) == 2:
                                    nc.vector.tensor_tensor(out=kept[:, e, :], in0=rstd[:, :], in1=keep_expert[:, e, :],
                                                            op=ALU.mult).then_inc(s["s_rs"], 1)
                                    dve.wait_ge(s["s_rs"], 2 + e)
                                for k in range(DT):
                                    n = e * DT + k
                                    by = kept[:, e, :] if len(outs) == 2 else rstd[:, :]
                                    nc.vector.scalar_tensor_tensor(out=full[:, n % 2, :], in0=h[:, k, :],
                                                                   scalar=cols[:, w, k:k + 1], in1=by,
                                                                   op0=ALU.mult, op1=ALU.mult).then_inc(s["s_n"], 1)
                                    dve.wait_ge(s["s_hi"], n + 1)
                                    nc.vector.tensor_tensor(out=outs[e][1][:, k, :], in0=full[:, n % 2, :],
                                                            in1=outs[e][0][:, k, :].bitcast(f32), op=ALU.subtract)\
                                        .then_inc(s["s_n"], 1)
                clear(sems)

        def experts(b):
            names = "s_tt s_k"
            ctx, (s_tt, s_k) = stage(names)
            with ctx:
                tti = sb("tti", [P, S], i32, ctx=ctx)
                one = sb("one", [P, S], ctx=ctx)
                with nc.Block() as block:
                    @block.sync
                    def _(sp):
                        sp.dma_start(tti[:, :], t["mask_BxS_ik0"][b].rearrange("(a n) -> a n", a=1).broadcast_to((P, S)))\
                            .then_inc(s_tt, 16)

                    @block.vector
                    def _(dve):
                        dve.wait_ge(s_tt, 16)
                        nc.vector.tensor_scalar(one[:, :], tti[:, :], 1.0, None, ALU.is_equal).then_inc(s_k, 1)
                        nc.vector.memset(keep_expert[:, 1, S - 1:S], 0.0).then_inc(s_k, 1)
                        dve.wait_ge(s_k, 2)
                        nc.vector.tensor_tensor(out=keep_expert[:, 1, 0:S - 1], in0=one[:, 0:S - 1], in1=one[:, 1:S],
                                                op=ALU.mult).then_inc(s_k, 1)
                        dve.wait_ge(s_k, 3)
                        nc.vector.tensor_scalar(keep_expert[:, 0, :], keep_expert[:, 1, :], -1.0, 1.0, ALU.mult, ALU.add)
                clear([s_tt, s_k])

        def qkv(xe, v_nat, q_st, k_st):
            names = "s_qf s_rot s_t1 s_rp s_rh s_rl s_stk s_v " + WSEMS
            ctx, sems = stage(names)
            s = dict(zip(names.split(), sems))
            wl = [s[f"s_wl{i}"] for i in range(RAW)]
            weights = [t["L1_xattn_l_qkv"], t["L1_xattn_v_qkv"]]
            G = 2 * DT
            with ctx:
                plain = sb("plain", [P, 2 * DT, S], ctx=ctx)
                hi, lo = sb("rhi", [P, 2 * DT, S], f32r, ctx=ctx), sb("rlo", [P, 2 * DT, S], f32r, ctx=ctx)
                t1, t2 = sb("t1", [P, 2, S], ctx=ctx), sb("t2", [P, 2, S], ctx=ctx)
                with nc.Block() as block:
                    @block.sync
                    def _(sp):
                        for n in range(3 * G):
                            g, e, k = n // G, n // DT % 2, n % DT
                            load_w(sp, n, weights[e][k * P:(k + 1) * P, g * D:(g + 1) * D], wl, s["s_ws"])
                        sp.dma_start(k_st[3 * HD:3 * HD + 1, :, :].bitcast(f32).rearrange("a (r h) n -> a r (h n)", r=8),
                                     ones_d[:, 0:NH // 8 * S].rearrange("(a r) n -> a r n", a=1)).then_inc(s["s_stk"], 16)
                        for qk, (st, parts) in enumerate(((q_st, (hi, hi, lo)), (k_st, (hi, lo, hi)))):
                            sp.wait_ge(s["s_rl"], (qk + 1) * DT)
                            for j in range(P // HD):
                                for r, part in enumerate(parts):
                                    sp.dma_start(st[r * HD:(r + 1) * HD, j:NH:P // HD, :].bitcast(f32),
                                                 part[j * HD:(j + 1) * HD, qk * DT:(qk + 1) * DT, :].bitcast(f32))\
                                        .then_inc(s["s_stk"], 16)
                        sp.wait_ge(s["s_stk"], 16 * (1 + 2 * 3 * P // HD))

                    @block.scalar
                    def _(act):
                        for c in range(2 * DT):
                            if c % DT == 0:
                                act.wait_ge(s["s_wu"], G * (c // DT + 1))
                            nc.scalar.activation(plain[:, c, :], ps[:, c, :], ACT.Copy).then_inc(s["s_qf"], 1)
                        for c in range(2 * DT):
                            act.wait_ge(s["s_rp"], 3 * c + 3)
                            nc.scalar.activation(hi[:, c, :], t1[:, c % 2, :], ACT.Copy).then_inc(s["s_rh"], 1)
                        act.wait_ge(s["s_wu"], 3 * G)
                        for a in range(ST):
                            nc.scalar.activation(v_nat[:, a, :], ps[:, a, :], ACT.Copy)

                    @block.vector
                    def _(dve):
                        for n in range(2 * G + SPLIT):
                            split_w(dve, n, wl, s["s_wh"], s["s_ws"], s["s_wu"])
                        for c in range(2 * DT):
                            dve.wait_ge(s["s_rot"], c + 1)
                            nc.vector.tensor_tensor(out=t2[:, c % 2, :], in0=ps[:, c, :], in1=sin_t[:, :], op=ALU.mult)\
                                .then_inc(s["s_rp"], 1)
                            nc.vector.tensor_tensor(out=t1[:, c % 2, :], in0=plain[:, c, :], in1=cos_t[:, :], op=ALU.mult)\
                                .then_inc(s["s_rp"], 1)
                            dve.wait_ge(s["s_rp"], 3 * c + 2)
                            nc.vector.tensor_tensor(out=t1[:, c % 2, :], in0=t1[:, c % 2, :], in1=t2[:, c % 2, :],
                                                    op=ALU.add).then_inc(s["s_rp"], 1)
                            dve.wait_ge(s["s_rh"], c + 1)
                            nc.vector.tensor_tensor(out=lo[:, c, :], in0=t1[:, c % 2, :], in1=hi[:, c, :].bitcast(f32),
                                                    op=ALU.subtract).then_inc(s["s_rl"], 1)
                            if c >= DT - 1 and 2 * G + SPLIT + c - DT + 1 < 3 * G:
                                split_w(dve, 2 * G + SPLIT + c - DT + 1, wl, s["s_wh"], s["s_ws"], s["s_wu"])

                    @block.tensor
                    def _(pe):
                        def project(n):
                            g, e, k = n // G, n // DT % 2, n % DT
                            xh_, xl_ = xe[e]
                            pe.wait_ge(s["s_ws"], n + 1)
                            first, end = n % G == 0, n % G == G - 1
                            for j in range(DT):
                                cut = slice(j * P, (j + 1) * P)
                                if g < 2:
                                    last = three(ps[:, g * 4 + j, :], w_hi[:, n % SPLIT, cut], w_lo[:, n % SPLIT, cut],
                                                 xh_[:, k, :], xl_[:, k, :], first, end)
                                else:
                                    last = three(ps[:, j, :], xh_[:, k, cut], xl_[:, k, cut],
                                                 w_hi[:, n % SPLIT, :], w_lo[:, n % SPLIT, :], first, end)
                            last.then_inc(s["s_wu"], 1)

                        for n in range(2 * G):
                            project(n)
                        for c in range(2 * DT):
                            pe.wait_ge(s["s_qf"], c + 1)
                            nc.tensor.matmul(ps[:, c, :], rot[:, :], plain[:, c, :], start=True, stop=True)\
                                .then_inc(s["s_rot"], 1)
                        pe.wait_ge(s["s_rp"], 3 * DT)
                        for n in range(2 * G, 3 * G):
                            project(n)
                clear(sems)

        def self_attention(v_nat, q_st, k_st, att):
            names = "s_max s_mx s_mt s_mc s_sh s_sc s_exp s_pv s_o s_n"
            ctx, sems = stage(names)
            s = dict(zip(names.split(), sems))
            NG, SCALE = NH // 4, float(HD) ** -0.5
            with ctx:
                row_max = sb("row_max_s", [P, NG, ST, 4], ctx=ctx)
                shift = sb("shift_s", [4, NG, S], ctx=ctx, dt=f32r)
                pT = sb("pT_s", [P, 2, 4, S], ctx=ctx)
                rin = sb("rin_s", [P, S], ctx=ctx)
                with nc.Block() as block:
                    @block.sync
                    def _(sp):
                        for g in range(NG):
                            sp.wait_ge(s["s_mc"], g + 1)
                            for j in range(4):
                                sp.dma_start(q_st[3 * HD:3 * HD + 1, 4 * g + j, :].bitcast(f32),
                                             shift[j:j + 1, g, :].bitcast(f32)).then_inc(s["s_sh"], 16)

                    @block.scalar
                    def _(act):
                        for g in range(NG):
                            for kt in range(ST):
                                u, n = g * ST + kt, S - kt * P
                                for half in range(2):
                                    act.wait_ge(s["s_sc"], 2 * u + half + 1)
                                    if u >= 2:
                                        act.wait_ge(s["s_pv"], u - 1)
                                    nc.scalar.activation(pT[:, u % 2, 2 * half:2 * half + 2, 0:n],
                                                         ps[:, 2 + 2 * half:4 + 2 * half, 0:n], ACT.Exp, scale=SCALE)\
                                        .then_inc(s["s_exp"], 1)

                    @block.vector
                    def _(dve):
                        def maxima(g):
                            for q in range(ST):
                                for half in range(2):
                                    n = (g * ST + q) * 2 + half
                                    dve.wait_ge(s["s_max"], n + 1)
                                    nc.vector.tensor_reduce(out=row_max[:, g, q, 2 * half:2 * half + 2],
                                                            in_=ps[:, 0:2, 0:(q + 1) * P], axis=AX.X, op=ALU.max)\
                                        .then_inc(s["s_mx"], 1)
                            dve.wait_ge(s["s_mt"], g + 1)
                            nc.vector.tensor_copy(shift[:, g, :], ps[0:4, 0, :]).then_inc(s["s_mc"], 1)

                        maxima(0)
                        for g in range(NG):
                            if g + 1 < NG:
                                maxima(g + 1)
                            dve.wait_ge(s["s_o"], g + 1)
                            nc.vector.reciprocal(rin[:, :], ps[:, 7, :]).then_inc(s["s_n"], 1)
                            dve.wait_ge(s["s_n"], 2 * g + 1)
                            nc.vector.tensor_tensor(out=att[:, g, :], in0=ps[:, 6, :], in1=rin[:, :], op=ALU.mult)\
                                .then_inc(s["s_n"], 1)

                    @block.tensor
                    def _(pe):
                        def maxima(g, q):
                            for half in range(2):
                                n = (g * ST + q) * 2 + half
                                if n >= 1:
                                    pe.wait_ge(s["s_mx"], n)
                                if n and n % (2 * ST) == 0:
                                    pe.wait_ge(s["s_mc"], g)
                                for j in range(2):
                                    hd = 4 * g + 2 * half + j
                                    nc.tensor.matmul(ps[:, j, q * P:(q + 1) * P], ident_b[:, :], mask_qk[:, :],
                                                     start=True, stop=False, skip_group_check=True)
                                    last = nc.tensor.matmul(ps[:, j, 0:(q + 1) * P], q_st[0:3 * HD, hd, q * P:(q + 1) * P],
                                                            k_st[0:3 * HD, hd, 0:(q + 1) * P], start=False, stop=True,
                                                            skip_group_check=True)
                                last.then_inc(s["s_max"], 1)

                        def turn_maxima(g):
                            pe.wait_ge(s["s_mx"], (g + 1) * ST * 2)
                            for q in range(ST):
                                last = nc.tensor.matmul(ps[0:4, 0, q * P:(q + 1) * P], row_max[:, g, q, :], neg_ident[:, :],
                                                        start=True, stop=True)
                            last.then_inc(s["s_mt"], 1)

                        def scores(u):
                            g, kt = divmod(u, ST)
                            n = S - kt * P
                            if kt == 0:
                                pe.wait_ge(s["s_sh"], 64 * (g + 1))
                            for half in range(2):
                                if u >= 1:
                                    pe.wait_ge(s["s_exp"], 2 * (u - 1) + half + 1)
                                for j in range(2):
                                    hd, bank = 4 * g + 2 * half + j, 2 + 2 * half + j
                                    nc.tensor.matmul(ps[:, bank, 0:P], ident_b[:, :], mask_kq[:, :],
                                                     start=True, stop=False, skip_group_check=True)
                                    last = nc.tensor.matmul(ps[:, bank, 0:n], k_st[0:3 * HD + 1, hd, kt * P:(kt + 1) * P],
                                                            q_st[0:3 * HD + 1, hd, kt * P:S], start=False, stop=True,
                                                            skip_group_check=True)
                                last.then_inc(s["s_sc"], 1)

                        for q in range(ST):
                            maxima(0, q)
                        turn_maxima(0)
                        scores(0)
                        for u in range(NG * ST):
                            g, kt = divmod(u, ST)
                            if g + 1 < NG:
                                maxima(g + 1, kt)
                                if kt == ST - 1:
                                    turn_maxima(g + 1)
                            if u + 1 < NG * ST:
                                scores(u + 1)
                            pe.wait_ge(s["s_exp"], 2 * u + 2)
                            if kt == 0 and g:
                                pe.wait_ge(s["s_n"], 2 * g)
                            n = S - kt * P
                            for j in range(4):
                                nc.tensor.matmul(ps[j * HD:(j + 1) * HD, 6, kt * P:S],
                                                 v_nat[:, kt, (4 * g + j) * HD:(4 * g + j + 1) * HD],
                                                 pT[:, u % 2, j, 0:n], start=kt == 0, stop=kt == ST - 1)
                            for j in range(4):
                                last = nc.tensor.matmul(ps[j * HD:(j + 1) * HD, 7, kt * P:S], ones[:, 0:HD],
                                                        pT[:, u % 2, j, 0:n], start=kt == 0, stop=kt == ST - 1)
                            last.then_inc(s["s_pv"], 1)
                            if kt == ST - 1:
                                pe.wait_ge(s["s_pv"], u + 1)
                                nc.tensor.sem_inc(s["s_o"], 1)
                clear(sems)

        def add_projection(tiles, parts):
            names = "s_add " + WSEMS
            ctx, sems = stage(names)
            s = dict(zip(names.split(), sems))
            wl = [s[f"s_wl{i}"] for i in range(RAW)]
            NW = len(tiles)
            with ctx:
                with nc.Block() as block:
                    @block.sync
                    def _(sp):
                        for n in range(NW):
                            load_w(sp, n, tiles[n], wl, s["s_ws"])

                    @block.vector
                    def _(dve):
                        for n in range(NW):
                            split_w(dve, n, wl, s["s_wh"], s["s_ws"], s["s_wu"])
                        dve.wait_ge(s["s_wu"], NW)
                        for j in range(DT):
                            nc.vector.tensor_tensor(out=h[:, j, :], in0=h[:, j, :], in1=ps[:, j, :], op=ALU.add)

                    @block.tensor
                    def _(pe):
                        for n in range(NW):
                            pe.wait_ge(s["s_ws"], n + 1)
                            for j in range(DT):
                                cut = slice(j * P, (j + 1) * P)
                                last = three(ps[:, j, :], w_hi[:, n % SPLIT, cut], w_lo[:, n % SPLIT, cut],
                                             parts[n][0], parts[n][1], n == 0, n == NW - 1)
                            last.then_inc(s["s_wu"], 1)
                clear(sems)

        def split(src, hi, lo, by=None):
            names = "s_m s_h s_l"
            ctx, (s_m, s_h, s_l) = stage(names)
            n = src.shape[1]
            with ctx:
                tmp = sb("split_tmp", [P, n, S], ctx=ctx) if by is not None else src
                with nc.Block() as block:
                    @block.scalar
                    def _(act):
                        for k in range(n):
                            if by is not None:
                                act.wait_ge(s_m, k + 1)
                            nc.scalar.activation(hi[:, k, :], tmp[:, k, :], ACT.Copy).then_inc(s_h, 1)

                    @block.vector
                    def _(dve):
                        if by is not None:
                            for k in range(n):
                                nc.vector.tensor_tensor(out=tmp[:, k, :], in0=src[:, k, :], in1=by, op=ALU.mult)\
                                    .then_inc(s_m, 1)
                        for k in range(n):
                            dve.wait_ge(s_h, k + 1)
                            nc.vector.tensor_tensor(out=lo[:, k, :], in0=tmp[:, k, :], in1=hi[:, k, :].bitcast(f32),
                                                    op=ALU.subtract)
                clear([s_m, s_h, s_l])

        def context_parts(b, ch, cl):
            names = "s_c s_tr s_th s_tl"
            ctx, sems = stage(names)
            s_c, s_tr, s_th, s_tl = sems
            units = [(e, kb) for e in range(ET) for kb in range(len(KEY_BANKS))]
            with ctx:
                cs = sb("cs_x", [P, KT, E], ctx=ctx)
                with nc.Block() as block:
                    @block.sync
                    def _(sp):
                        full = KEYS // P
                        sp.dma_start(cs[:, 0:full, :], t["ctx_1024"][b, 0:full * P].rearrange("(a p) n -> p a n", p=P))\
                            .then_inc(s_c, 16)
                        sp.dma_start(cs[0:KEYS - full * P, full, :], t["ctx_1024"][b, full * P:KEYS]).then_inc(s_c, 16)

                    @block.scalar
                    def _(act):
                        for i, (k, kb) in enumerate(units):
                            act.wait_ge(s_tr, i + 1)
                            k0, kn = KEY_BANKS[kb]
                            nc.scalar.activation(ch[:, k, k0:k0 + kn], ps[:, i, 0:kn], ACT.Copy).then_inc(s_th, 1)

                    @block.vector
                    def _(dve):
                        nc.vector.memset(ch[:, :, KEYS:KPAD].bitcast(f32), 0.0)
                        nc.vector.memset(cl[:, :, KEYS:KPAD].bitcast(f32), 0.0)
                        for i, (k, kb) in enumerate(units):
                            dve.wait_ge(s_th, i + 1)
                            k0, kn = KEY_BANKS[kb]
                            nc.vector.tensor_tensor(out=cl[:, k, k0:k0 + kn], in0=ps[:, i, 0:kn],
                                                    in1=ch[:, k, k0:k0 + kn].bitcast(f32), op=ALU.subtract)

                    @block.tensor
                    def _(pe):
                        pe.wait_ge(s_c, 32)
                        for i, (k, kb) in enumerate(units):
                            k0, kn = KEY_BANKS[kb]
                            for a in range(-(-kn // P)):
                                n = min(P, kn - a * P)
                                last = nc.tensor.transpose(ps[:, i, a * P:a * P + n], cs[0:n, k0 // P + a, k * P:(k + 1) * P],
                                                           ident[0:n, 0:n])
                            last.then_inc(s_tr, 1)
                clear(sems)

        STEP, SHIFT = P // 2, 3 * CHD

        def to_stack(sp, st, c, parts, sem):
            for par in range(2):
                for r, part in enumerate(parts):
                    for m in range(4):
                        i = 2 * m + par
                        sp.dma_start(st[par * STEP + r * CHD:par * STEP + (r + 1) * CHD, 4 * c + m, :].bitcast(f32),
                                     part[i * CHD:(i + 1) * CHD, c, :].bitcast(f32)).then_inc(sem, 16)
            return 2 * 3 * 4 * 16

        def cross_queries(ci, q_st):
            names = "s_h s_l s_st " + WSEMS
            ctx, sems = stage(names)
            s = dict(zip(names.split(), sems))
            wl = [s[f"s_wl{i}"] for i in range(RAW)]
            with ctx:
                hi, lo = sb("qc_h", [P, ET, S], f32r, ctx=ctx), sb("qc_l", [P, ET, S], f32r, ctx=ctx)
                with nc.Block() as block:
                    @block.sync
                    def _(sp):
                        for k in range(DT):
                            load_w(sp, k, t["L1_xattn_cq_w"][k * P:(k + 1) * P, :], wl, s["s_ws"])
                        total = 0
                        for c in range(ET):
                            sp.wait_ge(s["s_l"], c + 1)
                            total += to_stack(sp, q_st, c, (hi, hi, lo), s["s_st"])
                        sp.wait_ge(s["s_st"], total)

                    @block.scalar
                    def _(act):
                        act.wait_ge(s["s_wu"], DT)
                        for c in range(ET):
                            nc.scalar.activation(hi[:, c, :], ps[:, c, :], ACT.Copy).then_inc(s["s_h"], 1)

                    @block.vector
                    def _(dve):
                        for k in range(DT):
                            split_w(dve, k, wl, s["s_wh"], s["s_ws"], s["s_wu"], width=E)
                        for c in range(ET):
                            dve.wait_ge(s["s_h"], c + 1)
                            nc.vector.tensor_tensor(out=lo[:, c, :], in0=ps[:, c, :], in1=hi[:, c, :].bitcast(f32),
                                                    op=ALU.subtract).then_inc(s["s_l"], 1)

                    @block.tensor
                    def _(pe):
                        for k in range(DT):
                            pe.wait_ge(s["s_ws"], k + 1)
                            for c in range(ET):
                                cut = slice(c * P, (c + 1) * P)
                                last = three(ps[:, c, :], w_hi[:, k % SPLIT, cut], w_lo[:, k % SPLIT, cut],
                                             ci[0][:, k, :], ci[1][:, k, :], k == 0, k == DT - 1)
                            last.then_inc(s["s_wu"], 1)
                clear(sems)

        def cross_keys(ch, cl, k_st, v_aug):
            names = "s_k s_h s_l s_v s_vc s_st s_ms " + WSEMS
            ctx, sems = stage(names)
            s = dict(zip(names.split(), sems))
            wl = [s[f"s_wl{i}"] for i in range(RAW)]
            NB = len(KEY_BANKS)
            with ctx:
                hi, lo = sb("kc_h", [P, ET, KPAD], f32r, ctx=ctx), sb("kc_l", [P, ET, KPAD], f32r, ctx=ctx)
                with nc.Block() as block:
                    @block.sync
                    def _(sp):
                        for k in range(ET):
                            load_w(sp, k, t["L1_xattn_ckv_w"][k * P:(k + 1) * P, :], wl, s["s_ws"])
                        for par in range(2):
                            row = par * STEP + SHIFT
                            sp.dma_start(k_st[row:row + 1, :, :].bitcast(f32), ones_d.rearrange("(a h) n -> a h n", a=1))\
                                .then_inc(s["s_st"], 16)
                        total = 32
                        for c in range(ET):
                            sp.wait_ge(s["s_l"], (c + 1) * NB)
                            total += to_stack(sp, k_st, c, (hi, lo, hi), s["s_st"])
                        sp.wait_ge(s["s_st"], total)

                    @block.gpsimd
                    def _(pool):
                        nc.gpsimd.memset(v_aug[:, :, :, CHD:2 * CHD], 0.0).then_inc(s["s_ms"], 1)
                        pool.wait_ge(s["s_ms"], 1)
                        nc.gpsimd.memset(v_aug[:, :, :, CHD:CHD + 1], 1.0)

                    @block.scalar
                    def _(act):
                        for i in range(ET * NB):
                            c, (k0, kn) = i // NB, KEY_BANKS[i % NB]
                            kn += kn % 2
                            act.wait_ge(s["s_k"], i + 1)
                            nc.scalar.activation(hi[:, c, k0:k0 + kn], ps[:, i, 0:kn], ACT.Copy).then_inc(s["s_h"], 1)
                        for kt, (k0, kn) in enumerate(KEY_TILES):
                            act.wait_ge(s["s_v"], kt + 1)
                            nc.scalar.activation(v_aug[0:kn, kt, :, 0:CHD],
                                                 ps[0:kn, kt % 8, 0:E].rearrange("p (h d) -> p h d", d=CHD), ACT.Copy)\
                                .then_inc(s["s_vc"], 1)

                    @block.vector
                    def _(dve):
                        for k in range(ET):
                            split_w(dve, k, wl, s["s_wh"], s["s_ws"], s["s_wu"])
                        for i in range(ET * NB):
                            c, (k0, kn) = i // NB, KEY_BANKS[i % NB]
                            kn += kn % 2
                            dve.wait_ge(s["s_h"], i + 1)
                            nc.vector.tensor_tensor(out=lo[:, c, k0:k0 + kn], in0=ps[:, i, 0:kn],
                                                    in1=hi[:, c, k0:k0 + kn].bitcast(f32), op=ALU.subtract)\
                                .then_inc(s["s_l"], 1)

                    @block.tensor
                    def _(pe):
                        pe.wait_ge(s["s_ws"], ET)
                        for i in range(ET * NB):
                            c, (k0, kn) = i // NB, KEY_BANKS[i % NB]
                            kn += kn % 2
                            cut = slice(c * P, (c + 1) * P)
                            for e in range(ET):
                                last = three(ps[:, i, 0:kn], w_hi[:, e, cut], w_lo[:, e, cut],
                                             ch[:, e, k0:k0 + kn], cl[:, e, k0:k0 + kn], e == 0, e == ET - 1)
                            last.then_inc(s["s_k"], 1)
                        for kt, (k0, kn) in enumerate(KEY_TILES):
                            if kt < 8:
                                pe.wait_ge(s["s_l"], kt + 1)
                            else:
                                pe.wait_ge(s["s_vc"], kt - 7)
                            for e in range(ET):
                                last = three(ps[0:kn, kt % 8, 0:E], ch[:, e, k0:k0 + kn], cl[:, e, k0:k0 + kn],
                                             w_hi[:, e, E:2 * E], w_lo[:, e, E:2 * E], e == 0, e == ET - 1)
                            last.then_inc(s["s_v"], 1)
                clear(sems)

        def cross_attention(q_st, k_st, v_aug, att):
            names = "s_fill s_used s_rm s_sh s_sc s_exp s_pv s_ob s_n"
            ctx, sems = stage(names)
            s = dict(zip(names.split(), sems))
            NG, SCALE = NH // 4, float(CHD) ** -0.5
            UNITS = 4 * ST * 2
            PER = 3
            with ctx:
                halves = sb("halves", [P, ST, 4, 2], ctx=ctx)
                row_max = sb("row_max_x", [P, NG, ST, 4], ctx=ctx)
                shift = sb("shift_x", [4, NG, S], ctx=ctx, dt=f32r)
                pT = sb("pT_x", [P, 2, 4, S], ctx=ctx)
                rin, osb = sb("rin_x", [P, S], ctx=ctx), sb("osb", [P, S], ctx=ctx)

                order = []
                for g in range(NG + 1):
                    if g:
                        if g >= 2:
                            order.append(("sums", g - 2))
                    if g < NG:
                        order += [("max", g, i) for i in range(UNITS)] + [("turn", g)]
                order.append(("sums", NG - 1))
                place = {o: n for n, o in enumerate(order)}

                with nc.Block() as block:
                    @block.sync
                    def _(sp):
                        for g in range(NG):
                            sp.wait_ge(s["s_used"], place["turn", g] + 1)
                            for j in range(4):
                                hd = 4 * g + j
                                row = hd % 2 * STEP + SHIFT
                                sp.dma_start(q_st[row:row + 1, hd // 2, :].bitcast(f32),
                                             shift[j:j + 1, g, :].bitcast(f32)).then_inc(s["s_sh"], 16)

                    @block.scalar
                    def _(act):
                        for u in range(NG * KT):
                            kn = KEY_TILES[u % KT][1]
                            for j in range(4):
                                v = 4 * u + j
                                act.wait_ge(s["s_sc"], v + 1)
                                if u >= 2 and j == 0:
                                    act.wait_ge(s["s_pv"], u - 1)
                                nc.scalar.activation(pT[0:kn, u % 2, j, :], ps[0:kn, 5 + v % 3, :], ACT.Exp, scale=SCALE)\
                                    .then_inc(s["s_exp"], 1)

                    @block.vector
                    def _(dve):
                        for n, o in enumerate(order):
                            g = o[1]
                            at = 2 * (n % 2)
                            if o[0] == "max":
                                j, q, half = o[2] // (2 * ST), o[2] // 2 % ST, o[2] % 2
                                dve.wait_ge(s["s_fill"], n + 1)
                                nc.vector.tensor_reduce(out=halves[:, q, j, half:half + 1], in_=ps[:, at:at + 2, 0:MAXW],
                                                        axis=AX.XY, op=ALU.max).then_inc(s["s_used"], 1)
                                if o[2] == UNITS - 1:
                                    dve.wait_ge(s["s_used"], n + 1)
                                    nc.vector.tensor_reduce(out=row_max[:, g, :, :], in_=halves[:, :, :, :], axis=AX.X,
                                                            op=ALU.max).then_inc(s["s_rm"], 1)
                            elif o[0] == "turn":
                                dve.wait_ge(s["s_fill"], n + 1)
                                nc.vector.tensor_copy(shift[:, g, :], ps[0:4, at, :]).then_inc(s["s_used"], 1)
                            if o[0] == "turn" and g >= 1 or n == len(order) - 1:
                                out_g = g - 1 if o[0] == "turn" else g
                                dve.wait_ge(s["s_pv"], (out_g + 1) * KT)
                                if out_g:
                                    dve.wait_ge(s["s_n"], out_g)
                                nc.vector.tensor_copy(osb[:, :], ps[:, 4, :]).then_inc(s["s_ob"], 1)
                            if o[0] == "sums":
                                dve.wait_ge(s["s_fill"], n + 1)
                                nc.vector.reciprocal(rin[:, :], ps[:, at, :]).then_inc(s["s_used"], 1)
                                dve.wait_ge(s["s_used"], n + 1)
                                dve.wait_ge(s["s_ob"], g + 1)
                                nc.vector.tensor_tensor(out=att[:, g, :], in0=osb[:, :], in1=rin[:, :], op=ALU.mult)\
                                    .then_inc(s["s_n"], 1)

                    @block.tensor
                    def _(pe):
                        def fill(o):
                            n = place[o]
                            g, at = o[1], 2 * (n % 2)
                            if n >= 2:
                                pe.wait_ge(s["s_used"], n - 1)
                            if o[0] == "max":
                                j, q, half = o[2] // (2 * ST), o[2] // 2 % ST, o[2] % 2
                                hd = 4 * g + j
                                rows = slice(hd % 2 * STEP, hd % 2 * STEP + SHIFT)
                                for i in range(2):
                                    k0 = MAX_STARTS[2 * half + i]
                                    last = nc.tensor.matmul(ps[:, at + i, 0:MAXW], q_st[rows, hd // 2, q * P:(q + 1) * P],
                                                            k_st[rows, hd // 2, k0:k0 + MAXW], start=True, stop=True)
                            elif o[0] == "turn":
                                pe.wait_ge(s["s_rm"], g + 1)
                                for q in range(ST):
                                    last = nc.tensor.matmul(ps[0:4, at, q * P:(q + 1) * P], row_max[:, g, q, :],
                                                            neg_ident[:, :], start=True, stop=True)
                            else:
                                pe.wait_ge(s["s_ob"], g + 1)
                                last = nc.tensor.matmul(ps[:, at, :], sel[:, :], osb[:, :], start=True, stop=True)
                            last.then_inc(s["s_fill"], 1)

                        def score(u, j):
                            g, kt = divmod(u, KT)
                            k0, kn = KEY_TILES[kt]
                            v, hd = 4 * u + j, 4 * g + j
                            if kt == 0 and j == 0:
                                pe.wait_ge(s["s_sh"], 64 * (g + 1))
                            if v >= 3:
                                pe.wait_ge(s["s_exp"], v - 2)
                            rows = slice(hd % 2 * STEP, hd % 2 * STEP + SHIFT + 1)
                            nc.tensor.matmul(ps[0:kn, 5 + v % 3, :], k_st[rows, hd // 2, k0:k0 + kn], q_st[rows, hd // 2, :],
                                             start=True, stop=True).then_inc(s["s_sc"], 1)

                        for i in range(UNITS):
                            fill(("max", 0, i))
                        fill(("turn", 0))
                        for j in range(4):
                            score(0, j)
                        for u in range(NG * KT):
                            g, kt = divmod(u, KT)
                            todo = [("max", g + 1, i) for i in range(kt * PER, min(UNITS, (kt + 1) * PER))] if g + 1 < NG else []
                            if kt == 0 and g:
                                todo.insert(0, ("sums", g - 1))
                            if kt == -(-UNITS // PER) and g + 1 < NG:
                                todo.append(("turn", g + 1))
                            for j in range(4):
                                if u + 1 < NG * KT:
                                    score(u + 1, j)
                                if todo:
                                    fill(todo.pop(0))
                            pe.wait_ge(s["s_exp"], 4 * u + 4)
                            if kt == 0 and g:
                                pe.wait_ge(s["s_ob"], g)
                            kn = KEY_TILES[kt][1]
                            for j in range(4):
                                last = nc.tensor.matmul(ps[j * HD:(j + 1) * HD, 4, :], v_aug[0:kn, kt, 4 * g + j, :],
                                                        pT[0:kn, u % 2, j, :], start=kt == 0, stop=kt == KT - 1)
                            last.then_inc(s["s_pv"], 1)
                        fill(("sums", NG - 1))
                clear(sems)

        def store_stream(b):
            ctx, (s_st,) = stage("s_st")
            with ctx:
                with nc.Block() as block:
                    @block.sync
                    def _(sp):
                        sp.dma_start(h_d[b], h[:, :, :]).then_inc(s_st, 16)
                        sp.dma_start(keep_d[:, b, :].rearrange("e (a n) -> a e n", a=1), keep_expert[0:1, :, :]).then_inc(s_st, 16)
                        sp.wait_ge(s_st, 32)
                clear([s_st])

        def load_stream(g):
            ctx, (s_ld,) = stage("s_ld")
            with ctx:
                with nc.Block() as block:
                    @block.sync
                    def _(sp):
                        for b in range(B):
                            sp.dma_start(h[:, :, b * P:(b + 1) * P], h_d[b, :, :, bass.ts(g, P)]).then_inc(s_ld, 16)
                        for e in range(2):
                            for b in range(B):
                                sp.dma_start(keep_expert[:, e, b * P:(b + 1) * P],
                                             keep_d[e, b:b + 1, bass.ts(g, P)].broadcast_to((P, P))).then_inc(s_ld, 16)
                        sp.wait_ge(s_ld, 16 * 3 * B)
                clear([s_ld])

        def feed_forward(x, gate_w, up_w, down_w):
            names = "s_gu s_si s_mu s_hi s_lo s_dn " + WSEMS
            ctx, sems = stage(names)
            s = dict(zip(names.split(), sems))
            wl = [s[f"s_wl{i}"] for i in range(RAW)]
            NC = len(HID_TILES)
            tiles = [(w, c) for c in range(2) for w in "gu"]
            for c in range(NC):
                tiles.append(("d", c))
                if c + 2 < NC:
                    tiles += [("g", c + 2), ("u", c + 2)]
            place = {o: n for n, o in enumerate(tiles)}
            with ctx:
                sg, prod = sb("sg", [P, 2, S], ctx=ctx), sb("prod", [P, 2, S], ctx=ctx)
                hi, lo = sb("hid_h", [P, 2, S], f32r, ctx=ctx), sb("hid_l", [P, 2, S], f32r, ctx=ctx)
                with nc.Block() as block:
                    @block.sync
                    def _(sp):
                        for n, (w, c) in enumerate(tiles):
                            c0, cn = HID_TILES[c]
                            if w == "d":
                                src = down_w[c0:c0 + cn, :]
                            else:
                                src = (gate_w if w == "g" else up_w)[:, c0:c0 + cn].rearrange("(a p) n -> p a n", p=P)
                            load_w(sp, n, src, wl, s["s_ws"])

                    @block.scalar
                    def _(act):
                        for c, (c0, cn) in enumerate(HID_TILES):
                            act.wait_ge(s["s_wu"], place["g", c] + 1)
                            if c >= 2:
                                act.wait_ge(s["s_mu"], c - 1)
                            nc.scalar.activation(sg[0:cn, c % 2, :], ps[0:cn, 4 + c % 2, :], ACT.Silu).then_inc(s["s_si"], 1)
                            act.wait_ge(s["s_mu"], c + 1)
                            if c >= 2:
                                act.wait_ge(s["s_wu"], place["d", c - 2] + 1)
                            nc.scalar.activation(hi[0:cn, c % 2, :], prod[0:cn, c % 2, :], ACT.Copy).then_inc(s["s_hi"], 1)

                    @block.vector
                    def _(dve):
                        def split_tile(w, c):
                            cn = HID_TILES[c][1]
                            rows, width = (cn, D) if w == "d" else (P, DT * cn)
                            split_w(dve, place[w, c], wl, s["s_wh"], s["s_ws"], s["s_wu"], rows, width)

                        for w, c in tiles[0:4]:
                            split_tile(w, c)
                        for c, (c0, cn) in enumerate(HID_TILES):
                            dve.wait_ge(s["s_si"], c + 1)
                            dve.wait_ge(s["s_wu"], place["u", c] + 1)
                            nc.vector.tensor_tensor(out=prod[0:cn, c % 2, :], in0=ps[0:cn, 6 + c % 2, :], in1=sg[0:cn, c % 2, :],
                                                    op=ALU.mult).then_inc(s["s_mu"], 1)
                            split_tile("d", c)
                            dve.wait_ge(s["s_hi"], c + 1)
                            nc.vector.tensor_tensor(out=lo[0:cn, c % 2, :], in0=prod[0:cn, c % 2, :],
                                                    in1=hi[0:cn, c % 2, :].bitcast(f32), op=ALU.subtract).then_inc(s["s_lo"], 1)
                            if c + 2 < NC:
                                split_tile("g", c + 2)
                                split_tile("u", c + 2)
                        dve.wait_ge(s["s_wu"], len(tiles))
                        for j in range(DT):
                            nc.vector.tensor_tensor(out=h[:, j, :], in0=h[:, j, :], in1=ps[:, j, :], op=ALU.add)

                    @block.tensor
                    def _(pe):
                        for n, (w, c) in enumerate(tiles):
                            cn, slot = HID_TILES[c][1], n % SPLIT
                            pe.wait_ge(s["s_ws"], n + 1)
                            if w == "d":
                                pe.wait_ge(s["s_lo"], c + 1)
                                for j in range(DT):
                                    cut = slice(j * P, (j + 1) * P)
                                    last = three(ps[:, j, :], w_hi[0:cn, slot, cut], w_lo[0:cn, slot, cut],
                                                 hi[0:cn, c % 2, :], lo[0:cn, c % 2, :], c == 0, c == NC - 1)
                            else:
                                if c >= 2:
                                    pe.wait_ge(s["s_mu"], c - 1)
                                bank = ps[0:cn, (4 if w == "g" else 6) + c % 2, :]
                                for k in range(DT):
                                    cut = slice(k * cn, (k + 1) * cn)
                                    last = three(bank, w_hi[:, slot, cut], w_lo[:, slot, cut], x[0][:, k, :], x[1][:, k, :],
                                                 k == 0, k == DT - 1)
                            last.then_inc(s["s_wu"], 1)
                clear(sems)

        def write_out(g):
            names = "s_t s_e s_o"
            ctx, (s_t, s_e, s_o) = stage(names)
            with ctx:
                rows = sb("rows", [P, B, D], ctx=ctx)
                with nc.Block() as block:
                    @block.sync
                    def _(sp):
                        for b in range(B):
                            sp.wait_ge(s_e, b + 1)
                            sp.dma_start(out[b, bass.ts(g, P), :], rows[:, b, :]).then_inc(s_o, 16)
                        sp.wait_ge(s_o, 16 * B)

                    @block.scalar
                    def _(act):
                        for b in range(B):
                            act.wait_ge(s_t, b + 1)
                            nc.scalar.activation(rows[:, b, :], ps[:, b, :], ACT.Copy).then_inc(s_e, 1)

                    @block.tensor
                    def _(pe):
                        for b in range(B):
                            for k in range(DT):
                                last = nc.tensor.transpose(ps[:, b, k * P:(k + 1) * P], h[:, k, b * P:(b + 1) * P], ident[:, :])
                            last.then_inc(s_t, 1)
                clear([s_t, s_e, s_o])

        with nc.Fori(0, B) as b:
            with ExitStack() as mem:
                xT = sb("xT", [P, DT, S], ctx=mem)
                xh, xl = sb("xh", [P, DT, S], f32r, ctx=mem), sb("xl", [P, DT, S], f32r, ctx=mem)
                cn_h, cn_l = sb("cn_h", [P, ET, S], f32r, ctx=mem), sb("cn_l", [P, ET, S], f32r, ctx=mem)
                memory_attention(b, xT, xh, xl, cn_h, cn_l)
                gate(xT, xh, xl, cn_h, cn_l)
            norm(0, h)
            experts(b)
            with ExitStack() as mem:
                v_nat = sb("v_nat", [P, ST, D], ctx=mem)
                q_st, k_st = sb("q_st", [3 * HD + 1, NH, S], f32r, ctx=mem), sb("k_st", [3 * HD + 1, NH, S], f32r, ctx=mem)
                with ExitStack() as inner:
                    xe = [(sb(f"xe{e}h", [P, DT, S], f32r, ctx=inner), sb(f"xe{e}l", [P, DT, S], f32r, ctx=inner))
                          for e in range(2)]
                    norm(1, xe)
                    qkv(xe, v_nat, q_st, k_st)
                att = sb("att", [P, DT, S], ctx=mem)
                self_attention(v_nat, q_st, k_st, att)
                ae = [(sb(f"ae{e}h", [P, DT, S], f32r, ctx=mem), sb(f"ae{e}l", [P, DT, S], f32r, ctx=mem))
                      for e in range(2)]
                for e in range(2):
                    split(att, ae[e][0], ae[e][1], keep_expert[:, e, :])
                add_projection([t[n][k * P:(k + 1) * P, :] for n in ("L1_xattn_l_dense", "L1_xattn_v_dense") for k in range(DT)],
                               [(ae[e][0][:, k, :], ae[e][1][:, k, :]) for e in range(2) for k in range(DT)])
            with ExitStack() as mem:
                q_st, k_st = sb("qx_st", [P, NH // 2, S], f32r, ctx=mem), sb("kx_st", [P, NH // 2, KPAD], f32r, ctx=mem)
                v_aug = sb("v_aug", [P, KT, NH, 2 * CHD], ctx=mem)
                with ExitStack() as inner:
                    ci = (sb("ci_h", [P, DT, S], f32r, ctx=inner), sb("ci_l", [P, DT, S], f32r, ctx=inner))
                    norm(2, [ci])
                    cross_queries(ci, q_st)
                with ExitStack() as inner:
                    ch, cl = sb("chx", [P, ET, KPAD], f32r, ctx=inner), sb("clx", [P, ET, KPAD], f32r, ctx=inner)
                    context_parts(b, ch, cl)
                    cross_keys(ch, cl, k_st, v_aug)
                att = sb("att_x", [P, DT, S], ctx=mem)
                cross_attention(q_st, k_st, v_aug, att)
                ah, al = sb("ax_h", [P, DT, S], f32r, ctx=mem), sb("ax_l", [P, DT, S], f32r, ctx=mem)
                split(att, ah, al)
                add_projection([cd_d[k * P:(k + 1) * P, :] for k in range(DT)], [(ah[:, k, :], al[:, k, :]) for k in range(DT)])
            store_stream(b)

        with nc.Fori(0, ST) as g:
            load_stream(g)
            with ExitStack() as mem:
                xe = [(sb(f"me{e}h", [P, DT, S], f32r, ctx=mem), sb(f"me{e}l", [P, DT, S], f32r, ctx=mem)) for e in range(2)]
                norm(3, xe)
                for e, w in enumerate("lv"):
                    feed_forward(xe[e], *(t[f"L1_xattn_{w}_{n}"] for n in ("gate", "up", "down")))
            write_out(g)


INPUTS = ["x", "ctx_1024", "pos_1xS", "mask_BxS_ik0"] + ["L0_xattn_" + n for n in ("W_mem", "W_gate", "b_gate", "norm_w")] + [
    "L1_xattn_" + n for n in ("ln_in_w", "ln_post_attn_w", "ln_post_cross_w", "v_qkv", "l_qkv", "v_dense", "l_dense",
                              "cq_w", "ckv_w", "cdense_w", "v_gate", "v_up", "v_down", "l_gate", "l_up", "l_down")]


def constants():
    import numpy as np
    p = np.arange(P)
    c = {"c_ident": np.eye(P, dtype=np.float32)}
    rot = np.zeros((P, P), np.float32)
    low = p % HD < HD // 2
    rot[p[low] + HD // 2, p[low]] = -1.0
    rot[p[~low] - HD // 2, p[~low]] = 1.0
    c["c_rot"] = rot
    c["c_sel"] = (p[:, None] == (p[None, :] // HD) * HD + CHD).astype(np.float32)
    later = p[None, :] > p[:, None]
    c["c_masks"] = np.stack([np.where(later, BIG, 0.0), np.where(later.T, BIG, 0.0)], 1).astype(np.float32)
    inv = (np.float32(1.0) / np.power(np.float32(10000.0), np.arange(0, HD, 2, dtype=np.float32) / np.float32(HD)))
    angle = (np.arange(S, dtype=np.float32)[:, None] * inv[None, :].astype(np.float32)).astype(np.float64)
    angle = np.tile(angle, (1, 2 * P // HD))
    c["c_tab"] = np.stack([np.cos(angle), np.sin(angle)], 1).astype(np.float32)
    c["c_tpos"] = (p[:, None] + P * np.arange(ST)[None, :]).astype(np.float32)
    return c


def columns(arrays):
    import numpy as np
    names = ("L0_xattn_norm_w", "L1_xattn_ln_in_w", "L1_xattn_ln_post_cross_w", "L1_xattn_ln_post_attn_w",
             "L0_xattn_b_gate")
    return np.ascontiguousarray(np.stack([arrays[n].reshape(DT, P).T for n in names], 1))


def kernel(**inputs):
    import numpy as np
    import concourse.bacc as bacc
    from concourse.bass_utils import run_bass_kernel_spmd

    nc = bacc.Bacc("TRN2", target_bir_lowering=False, num_devices=1)
    arrays = {n: np.ascontiguousarray(inputs[n]) for n in INPUTS} | constants()
    arrays["columns"] = columns(arrays)
    t = {n: nc.dram_tensor(n, a.shape, mybir.dt.from_np(a.dtype), kind="ExternalInput").ap() for n, a in arrays.items()}
    out = nc.dram_tensor("out", [B, S, D], mybir.dt.float32, kind="ExternalOutput").ap()
    program(nc, t, out)
    r = run_bass_kernel_spmd(nc, [arrays], core_ids=[0])
    return r.results[0]["out"]
```

```python
import concourse.bass as bass
from concourse import mybir
from contextlib import ExitStack

B, S, D = 4, 512, 512
KEYS, E = 1601, 256
P = 128
DT, ET, ST = D // P, E // P, S // P
KT = -(-KEYS // P)
KEY_TILES = [(i * P, min(P, KEYS - i * P)) for i in range(KT)]
KEY_BANKS = [(i * S, min(S, KEYS - i * S)) for i in range(-(-KEYS // S))]
KPAD = KEYS + KEYS % 2
NH, HD, CHD = 16, 32, 16
HIDDEN = 1376
HID_TILES = [(i * P, min(P, HIDDEN - i * P)) for i in range(-(-HIDDEN // P))]
EPS = 1e-6
MAXW = 402
MAX_STARTS = [0, 400, 800, KEYS - MAXW]
BIG = -1e30


def program(nc, t, out):
    f32, f32r, bf16, i32 = mybir.dt.float32, mybir.dt.float32r, mybir.dt.bfloat16, mybir.dt.int32
    ALU, ACT, AX = mybir.AluOpType, mybir.ActivationFunctionType, mybir.AxisListType

    def scratch(name, shape, dt=f32):
        return nc.dram_tensor(name, shape, dt, kind="Internal").ap()

    wmT_d = scratch("w_mem_transposed", [E, D])
    wgT_d = scratch("w_gate_transposed", [2 * D, D])
    cd_d = scratch("w_cross_dense_padded", [D, D])
    ones_d = scratch("ones_rows", [NH // 2, KPAD])
    heads_d = scratch("cross_heads_by_part", [2, ET * P, KPAD])
    h_d = scratch("stream_after_attention", [B, P, DT, S])
    keep_d = scratch("keep_expert_by_token", [2, B, S])

    with ExitStack() as keep:
        made = {}

        def sb(name, shape, dt=f32, ctx=keep):
            made[name] = made.get(name, 0) + 1
            return ctx.enter_context(nc.sbuf_tensor(f"{name}_{made[name]}" if made[name] > 1 else name, shape, dt))

        ps = keep.enter_context(nc.psum_tensor("ps", [P, 8, 512], f32))
        ident, neg_ident, ones = sb("ident", [P, P]), sb("neg_ident", [P, P]), sb("ones", [P, P])
        ones_r = sb("ones_r", [P, P], f32r)
        ident_b = sb("ident_b", [P, P], bf16)
        mask_qk, mask_kq = sb("mask_qk", [P, P], bf16), sb("mask_kq", [P, P], bf16)
        rot = sb("rot", [P, P])
        cos_t, sin_t = sb("cos_t", [P, S]), sb("sin_t", [P, S])
        cols = sb("cols", [P, 5, DT])
        eps_col = sb("eps_col", [P, 1])
        h = sb("h", [P, DT, S])
        sel = sb("sel", [P, 8])
        RAW, SPLIT = 4, 4
        w_raw = sb("w_raw", [P, RAW, 512])
        w_hi, w_lo = sb("w_hi", [P, SPLIT, 512], f32r), sb("w_lo", [P, SPLIT, 512], f32r)
        keep_expert = sb("keep_expert", [P, 2, S])

        def clear(sems):
            nc.all_engine_barrier()
            lo, hi = min(s.num for s in sems), max(s.num for s in sems)
            nc.gpsimd.sem_clear(range(lo, hi + 1))
            nc.all_engine_barrier()

        def stage(names):
            ctx = ExitStack()
            sems = [ctx.enter_context(nc.semaphore(n)) for n in names.split()]
            return ctx, sems

        ctx, sems = stage("s_z s_zd s_one s_const s_raw s_tr s_ev s_st s_pos s_hot s_tab s_cast s_w s_ms")
        s_z, s_zd, s_one, s_const, s_raw, s_tr, s_ev, s_st, s_pos, s_hot, s_tab, s_cast, s_w, s_ms = sems
        with ctx:
            tab = sb("tab", [P, ST, 2, P], ctx=ctx)
            masks = sb("masks", [P, 2, P], ctx=ctx)
            posi = sb("posi", [P, S], i32, ctx=ctx)
            posf, wrap = sb("posf", [P, S], ctx=ctx), sb("wrap", [P, S], ctx=ctx)
            tpos = sb("tpos", [P, ST], ctx=ctx)
            hot = sb("hot", [P, ST, S], ctx=ctx)
            wm = sb("wm", [P, DT, E], ctx=ctx)
            wg = sb("wg", [P, DT, 2 * D], ctx=ctx)
            ones_big = sb("ones_big", [NH // 2, KPAD], ctx=ctx)
            zeros = sb("zeros", [P, DT, D], ctx=ctx)
            wmT, wgT = sb("wmT", [P, ET, D], ctx=ctx), sb("wgT", [P, 2 * DT, D], ctx=ctx)
            with nc.Block() as block:
                @block.sync
                def _(sp):
                    for dst, src in ((ident[:, :], t["c_ident"]), (rot[:, :], t["c_rot"]), (sel[:, :], t["c_sel"]),
                                     (masks[:, :, :], t["c_masks"]),
                                     (tab[:, :, :, :], t["c_tab"].rearrange("(a p) c n -> p a c n", p=P)),
                                     (tpos[:, :], t["c_tpos"])):
                        sp.dma_start(dst, src).then_inc(s_const, 16)
                    sp.dma_start(wm[:, :, :], t["L0_xattn_W_mem"].rearrange("(a p) n -> p a n", p=P)).then_inc(s_raw, 16)
                    sp.dma_start(wg[:, :, :], t["L0_xattn_W_gate"].rearrange("(a p) n -> p a n", p=P)).then_inc(s_raw, 16)
                    sp.wait_ge(s_ev, 10)
                    sp.dma_start(wmT_d.rearrange("(a p) n -> p a n", p=P), wmT[:, :, :]).then_inc(s_st, 16)
                    sp.dma_start(wgT_d.rearrange("(a p) n -> p a n", p=P), wgT[:, :, :]).then_inc(s_st, 16)
                    sp.wait_ge(s_z, 1)
                    sp.dma_start(cd_d.rearrange("(a p) n -> p a n", p=P), zeros[:, :, :]).then_inc(s_zd, 16)
                    sp.wait_ge(s_zd, 16)
                    sp.dma_start(cd_d.rearrange("(h r) n -> h r n", r=HD)[:, 0:CHD, :],
                                 t["L1_xattn_cdense_w"].rearrange("(h r) n -> h r n", r=CHD)).then_inc(s_st, 16)
                    sp.wait_ge(s_one, 1)
                    sp.dma_start(ones_d, ones_big[:, :]).then_inc(s_st, 16)
                    sp.wait_ge(s_st, 64)

                @block.scalar
                def _(act):
                    act.dma_start(posi[:, :], t["pos_1xS"].broadcast_to((P, S))).then_inc(s_pos, 16)
                    act.dma_start(cols[:, :, :], t["columns"]).then_inc(s_w, 16)
                    act.wait_ge(s_w, 16)

                @block.vector
                def _(dve):
                    nc.vector.memset(ones[:, :], 1.0).then_inc(s_ms, 1)
                    nc.vector.memset(eps_col[:, :], EPS).then_inc(s_ms, 1)
                    nc.vector.memset(zeros[:, :, :], 0.0).then_inc(s_z, 1)
                    dve.wait_ge(s_ms, 2)
                    nc.vector.tensor_copy(ones_r[:, :], ones[:, :])
                    nc.vector.memset(ones_big[:, :], 1.0).then_inc(s_one, 1)
                    dve.wait_ge(s_pos, 16)
                    nc.vector.tensor_copy(posf[:, :], posi[:, :]).then_inc(s_hot, 1)
                    dve.wait_ge(s_hot, 1)
                    nc.vector.tensor_scalar(wrap[:, :], posf[:, :], 0.0, float(S), ALU.is_lt, ALU.mult).then_inc(s_hot, 1)
                    dve.wait_ge(s_hot, 2)
                    nc.vector.tensor_tensor(out=posf[:, :], in0=posf[:, :], in1=wrap[:, :], op=ALU.add).then_inc(s_hot, 1)
                    dve.wait_ge(s_hot, 3)
                    nc.vector.tensor_scalar(posf[:, :], posf[:, :], 0.0, float(S - 1), ALU.max, ALU.min).then_inc(s_hot, 1)
                    dve.wait_ge(s_hot, 4)
                    dve.wait_ge(s_const, 96)
                    nc.vector.tensor_copy(ident_b[:, :], ident[:, :])
                    nc.vector.tensor_scalar(neg_ident[:, :], ident[:, :], -1.0, None, ALU.mult)
                    nc.vector.tensor_copy(mask_qk[:, :], masks[:, 0, :])
                    nc.vector.tensor_copy(mask_kq[:, :], masks[:, 1, :])
                    for a in range(ST):
                        nc.vector.tensor_scalar(hot[:, a, :], posf[:, :], tpos[:, a:a + 1], None,
                                                ALU.is_equal).then_inc(s_hot, 1)
                    dve.wait_ge(s_tab, 2)
                    nc.vector.tensor_copy(cos_t[:, :], ps[:, 0, :]).then_inc(s_cast, 1)
                    nc.vector.tensor_copy(sin_t[:, :], ps[:, 1, :]).then_inc(s_cast, 1)
                    for i in range(10):
                        dve.wait_ge(s_tr, i + 1)
                        dst = wmT[:, i, :] if i < ET else wgT[:, i - ET, :]
                        nc.vector.tensor_copy(dst, ps[:, 2 + i % 6, :]).then_inc(s_ev, 1)

                @block.tensor
                def _(pe):
                    pe.wait_ge(s_hot, 4 + ST)
                    for c in range(2):
                        for a in range(ST):
                            last = nc.tensor.matmul(ps[:, c, :], tab[:, a, c, :], hot[:, a, :],
                                                    start=a == 0, stop=a == ST - 1)
                        last.then_inc(s_tab, 1)
                    pe.wait_ge(s_raw, 32)
                    for i in range(10):
                        if i >= 6:
                            pe.wait_ge(s_ev, i - 5)
                        src, e = (wm, i) if i < ET else (wg, i - ET)
                        for a in range(DT):
                            last = nc.tensor.transpose(ps[:, 2 + i % 6, a * P:(a + 1) * P],
                                                       src[:, a, e * P:(e + 1) * P], ident[:, :])
                        last.then_inc(s_tr, 1)
            clear(sems)


        def load_w(sp, n, src, s_loaded, s_split):
            rows, width = src.shape[0], src.shape[-1] * (src.shape[1] if len(src.shape) == 3 else 1)
            if n >= RAW:
                sp.wait_ge(s_split, n - RAW + 1)
            dst = w_raw[0:rows, n % RAW, 0:width]
            if len(src.shape) == 3:
                dst = dst.rearrange("p (a n) -> p a n", n=src.shape[-1])
            sp.dma_start(dst, src).then_inc(s_loaded[n % RAW], 16)

        def split_w(dve, n, s_loaded, s_high, s_split, s_used, rows=P, width=512):
            raw, hi, lo = (x[0:rows, n % k, 0:width] for x, k in ((w_raw, RAW), (w_hi, SPLIT), (w_lo, SPLIT)))
            dve.wait_ge(s_loaded[n % RAW], 16 * (n // RAW + 1))
            if n >= SPLIT:
                dve.wait_ge(s_used, n - SPLIT + 1)
            nc.vector.tensor_copy(hi, raw).then_inc(s_high, 1)
            dve.wait_ge(s_high, n + 1)
            nc.vector.tensor_tensor(out=lo, in0=raw, in1=hi.bitcast(f32), op=ALU.subtract).then_inc(s_split, 1)

        def three(dst, ah, al, bh, bl, start, stop, **how):
            nc.tensor.matmul(dst, ah, bh, start=start, stop=False, **how)
            nc.tensor.matmul(dst, al, bh, start=False, stop=False, **how)
            return nc.tensor.matmul(dst, ah, bl, start=False, stop=stop, **how)

        def for_v_tokens(early_v, run):
            early = nc.tensor.value_load(early_v[0:1, 0:1], min_val=0, max_val=1)
            with nc.tensor.If(early > 0):
                run(0)
            with nc.tensor.If(early < 1):
                run(S - P)

        WSEMS = " ".join(f"s_wl{i}" for i in range(RAW)) + " s_wh s_ws s_wu "

        def memory_attention(b, xT, xh, xl, cn_h, cn_l, early_v):
            NU = DT + ET * len(KEY_BANKS)
            names = ("s_x s_c s_tr s_th s_tl s_uh s_ul s_max s_mx s_dg s_sc s_exp s_acc s_pv s_pad "
                     "s_sum s_cn s_tt s_k " + WSEMS)
            ctx, sems = stage(names)
            s = dict(zip(names.split(), sems))
            wl = [s[f"s_wl{i}"] for i in range(RAW)]
            with ctx:
                xs = sb("xs", [P, ST, D], ctx=ctx)
                cs = sb("cs", [P, KT, E], ctx=ctx)
                ch, cl = sb("ch", [P, ET, KPAD], f32r, ctx=ctx), sb("cl", [P, ET, KPAD], f32r, ctx=ctx)
                uh, ul = sb("uh", [P, ET, S], f32r, ctx=ctx), sb("ul", [P, ET, S], f32r, ctx=ctx)
                row_max = sb("row_max", [P, ST], ctx=ctx)
                tti, one = sb("tti", [P, S], i32, ctx=ctx), sb("one", [P, S], ctx=ctx)
                any_early = sb("any_early", [1, 1], ctx=ctx)
                shift = sb("shift", [P, ST, P], f32r, ctx=ctx)
                pT = sb("pT", [P, 3, S], ctx=ctx)
                acc = sb("acc", [P, S], ctx=ctx)
                rq = sb("rq", [P, ST], ctx=ctx)
                unscaled, tmp = sb("unscaled", [P, ET, S], ctx=ctx), sb("tmp", [P, ET, S], ctx=ctx)
                units = [("x", k, 0) for k in range(DT)] + [("c", e, kb) for e in range(ET)
                                                            for kb in range(len(KEY_BANKS))]
                with nc.Block() as block:
                    @block.sync
                    def _(sp):
                        sp.dma_start(xs[:, :, :], t["x"][b].rearrange("(a p) n -> p a n", p=P)).then_inc(s["s_x"], 16)
                        full = KEYS // P
                        sp.dma_start(cs[:, 0:full, :], t["ctx_1024"][b, 0:full * P].rearrange("(a p) n -> p a n", p=P))\
                            .then_inc(s["s_c"], 16)
                        sp.dma_start(cs[0:KEYS - full * P, full, :], t["ctx_1024"][b, full * P:KEYS]).then_inc(s["s_c"], 16)
                        for k in range(DT):
                            load_w(sp, k, t["L0_xattn_W_mem"][k * P:(k + 1) * P, :], wl, s["s_ws"])
                        sp.dma_start(tti[:, :], t["mask_BxS_ik0"][b].rearrange("(a n) -> a n", a=1).broadcast_to((P, S)))\
                            .then_inc(s["s_tt"], 16)

                    @block.scalar
                    def _(act):
                        for i, (what, k, kb) in enumerate(units):
                            act.wait_ge(s["s_tr"], i + 1)
                            k0, kn = (0, S) if what == "x" else KEY_BANKS[kb]
                            dst = xh[:, k, :] if what == "x" else ch[:, k, k0:k0 + kn]
                            nc.scalar.activation(dst, ps[:, i % 8, 0:kn], ACT.Copy).then_inc(s["s_th"], 1)
                        act.wait_ge(s["s_wu"], DT)
                        for e in range(ET):
                            nc.scalar.activation(uh[:, e, :], ps[:, e, :], ACT.Copy).then_inc(s["s_uh"], 1)
                        for kt, (k0, kn) in enumerate(KEY_TILES):
                            act.wait_ge(s["s_sc"], kt + 1)
                            if kt >= 3:
                                act.wait_ge(s["s_pv"], kt - 2)
                                act.wait_ge(s["s_acc"], kt - 2)
                            nc.scalar.activation(pT[0:kn, kt % 3, :], ps[0:kn, 4 + kt % 3, :], ACT.Exp,
                                                 scale=float(D) ** -0.5).then_inc(s["s_exp"], 1)

                    @block.gpsimd
                    def _(pool):
                        for kt, (k0, kn) in enumerate(KEY_TILES):
                            pool.wait_ge(s["s_exp"], kt + 1)
                            if kt == 0:
                                nc.gpsimd.tensor_copy(acc[:, :], pT[:, 0, :]).then_inc(s["s_acc"], 1)
                            else:
                                pool.wait_ge(s["s_acc"], kt)
                                nc.gpsimd.tensor_tensor(out=acc[0:kn, :], in0=acc[0:kn, :], in1=pT[0:kn, kt % 3, :],
                                                        op=ALU.add).then_inc(s["s_acc"], 1)

                    @block.vector
                    def _(dve):
                        nc.vector.memset(ch[:, :, KEYS:KPAD].bitcast(f32), 0.0)
                        nc.vector.memset(cl[:, :, KEYS:KPAD].bitcast(f32), 0.0)
                        for k in range(SPLIT):
                            split_w(dve, k, wl, s["s_wh"], s["s_ws"], s["s_wu"], width=E)
                        for i, (what, k, kb) in enumerate(units):
                            dve.wait_ge(s["s_th"], i + 1)
                            if what == "x":
                                nc.vector.tensor_copy(xT[:, k, :], ps[:, i % 8, :])
                            k0, kn = (0, S) if what == "x" else KEY_BANKS[kb]
                            hi, lo = (xh[:, k, :], xl[:, k, :]) if what == "x" else (ch[:, k, k0:k0 + kn], cl[:, k, k0:k0 + kn])
                            nc.vector.tensor_tensor(out=lo, in0=ps[:, i % 8, 0:kn], in1=hi.bitcast(f32),
                                                    op=ALU.subtract).then_inc(s["s_tl"], 1)
                        for k in range(SPLIT, DT):
                            split_w(dve, k, wl, s["s_wh"], s["s_ws"], s["s_wu"], width=E)
                        for e in range(ET):
                            dve.wait_ge(s["s_uh"], e + 1)
                            nc.vector.tensor_tensor(out=ul[:, e, :], in0=ps[:, e, :], in1=uh[:, e, :].bitcast(f32),
                                                    op=ALU.subtract).then_inc(s["s_ul"], 1)
                        for q in range(ST):
                            dve.wait_ge(s["s_max"], q + 1)
                            at = 4 - 4 * (q % 2)
                            nc.vector.tensor_reduce(out=row_max[:, q:q + 1], in_=ps[:, at:at + 4, 0:MAXW],
                                                    axis=AX.XY, op=ALU.max).then_inc(s["s_mx"], 1)
                            dve.wait_ge(s["s_mx"], q + 1)
                            nc.vector.tensor_scalar(shift[:, q, :], neg_ident[:, :], row_max[:, q:q + 1], None,
                                                    ALU.mult).then_inc(s["s_dg"], 1)
                        dve.wait_ge(s["s_tt"], 16)
                        nc.vector.tensor_scalar(one[:, :], tti[:, :], 1.0, None, ALU.is_equal).then_inc(s["s_k"], 1)
                        nc.vector.memset(keep_expert[:, 1, S - 1:S], 0.0).then_inc(s["s_k"], 1)
                        dve.wait_ge(s["s_k"], 2)
                        nc.vector.tensor_tensor(out=keep_expert[:, 1, 0:S - 1], in0=one[:, 0:S - 1], in1=one[:, 1:S],
                                                op=ALU.mult).then_inc(s["s_k"], 1)
                        dve.wait_ge(s["s_k"], 3)
                        nc.vector.tensor_scalar(keep_expert[:, 0, :], keep_expert[:, 1, :], -1.0, 1.0, ALU.mult, ALU.add)
                        nc.vector.tensor_reduce(out=any_early[:, :], in_=keep_expert[0:1, 1, 0:S - P], axis=AX.X, op=ALU.max)\
                            .then_inc(s["s_k"], 1)
                        dve.wait_ge(s["s_k"], 4)
                        nc.vector.tensor_copy(early_v[:, :], any_early[:, :])
                        dve.wait_ge(s["s_sum"], 1)
                        nc.vector.reciprocal(rq[:, :], ps[:, 7, 0:ST]).then_inc(s["s_cn"], 1)
                        for e in range(ET):
                            nc.vector.tensor_copy(unscaled[:, e, :], ps[:, e, :]).then_inc(s["s_cn"], 1)
                        dve.wait_ge(s["s_sum"], 2)
                        dve.wait_ge(s["s_cn"], 1 + ET)
                        for e in range(ET):
                            nc.vector.tensor_tensor(out=tmp[:, e, :], in0=unscaled[:, e, :], in1=ps[:, 6, :], op=ALU.mult)\
                                .then_inc(s["s_cn"], 1)
                        for e in range(ET):
                            dve.wait_ge(s["s_cn"], 2 + ET + e)
                            nc.vector.tensor_copy(cn_h[:, e, :], tmp[:, e, :]).then_inc(s["s_cn"], 1)
                        for e in range(ET):
                            dve.wait_ge(s["s_cn"], 2 + 2 * ET + e)
                            nc.vector.tensor_tensor(out=cn_l[:, e, :], in0=tmp[:, e, :], in1=cn_h[:, e, :].bitcast(f32),
                                                    op=ALU.subtract).then_inc(s["s_cn"], 1)

                    @block.tensor
                    def _(pe):
                        pe.wait_ge(s["s_x"], 16)
                        for i, (what, k, kb) in enumerate(units):
                            if i == DT:
                                pe.wait_ge(s["s_c"], 32)
                            if i >= 8:
                                pe.wait_ge(s["s_tl"], i - 7)
                            if what == "x":
                                for a in range(ST):
                                    last = nc.tensor.transpose(ps[:, i % 8, a * P:(a + 1) * P],
                                                               xs[:, a, k * P:(k + 1) * P], ident[:, :])
                            else:
                                k0, kn = KEY_BANKS[kb]
                                for a in range(-(-kn // P)):
                                    n = min(P, kn - a * P)
                                    last = nc.tensor.transpose(ps[:, i % 8, a * P:a * P + n],
                                                               cs[0:n, k0 // P + a, k * P:(k + 1) * P],
                                                               ident[0:n, 0:n])
                            last.then_inc(s["s_tr"], 1)
                        pe.wait_ge(s["s_tl"], NU)
                        for k in range(DT):
                            pe.wait_ge(s["s_ws"], k + 1)
                            for e in range(ET):
                                cut = slice(e * P, (e + 1) * P)
                                last = three(ps[:, e, :], w_hi[:, k % SPLIT, cut], w_lo[:, k % SPLIT, cut],
                                             xh[:, k, :], xl[:, k, :], k == 0, k == DT - 1)
                            last.then_inc(s["s_wu"], 1)
                        pe.wait_ge(s["s_uh"], ET)
                        for q in range(ST):
                            at = 4 - 4 * (q % 2)
                            if q == 1:
                                pe.wait_ge(s["s_ul"], ET)
                            if q >= 2:
                                pe.wait_ge(s["s_mx"], q - 1)
                            for e in range(ET):
                                for n, k0 in enumerate(MAX_STARTS):
                                    last = nc.tensor.matmul(ps[:, at + n, 0:MAXW], uh[:, e, q * P:(q + 1) * P],
                                                            ch[:, e, k0:k0 + MAXW], start=e == 0, stop=e == ET - 1)
                            last.then_inc(s["s_max"], 1)
                        pe.wait_ge(s["s_mx"], ST)
                        pe.wait_ge(s["s_dg"], ST)

                        def scores(kt):
                            k0, kn = KEY_TILES[kt]
                            if kt >= 3:
                                pe.wait_ge(s["s_exp"], kt - 2)
                            bank = ps[0:kn, 4 + kt % 3, :]
                            nc.tensor.matmul(bank, ones_r[:, 0:kn], shift[:, :, :].rearrange("p a n -> p (a n)"),
                                             start=True, stop=False)
                            for e in range(ET):
                                last = three(bank, ch[:, e, k0:k0 + kn], cl[:, e, k0:k0 + kn], uh[:, e, :], ul[:, e, :],
                                             False, e == ET - 1)
                            last.then_inc(s["s_sc"], 1)

                        scores(0)
                        scores(1)
                        for kt, (k0, kn) in enumerate(KEY_TILES):
                            if kt + 2 < KT:
                                scores(kt + 2)
                            pe.wait_ge(s["s_exp"], kt + 1)
                            for e in range(ET):
                                last = nc.tensor.matmul(ps[:, e, :], cs[0:kn, kt, e * P:(e + 1) * P],
                                                        pT[0:kn, kt % 3, :], start=kt == 0, stop=kt == KT - 1)
                            last.then_inc(s["s_pv"], 1)
                        pe.wait_ge(s["s_acc"], KT)
                        for q in range(ST):
                            last = nc.tensor.matmul(ps[:, 7, q:q + 1], acc[:, q * P:(q + 1) * P], ones[:, 0:1],
                                                    start=True, stop=True)
                        last.then_inc(s["s_sum"], 1)
                        pe.wait_ge(s["s_cn"], 1)
                        for q in range(ST):
                            last = nc.tensor.matmul(ps[:, 6, q * P:(q + 1) * P], rq[:, q:q + 1].broadcast_to((P, P)),
                                                    ident[:, :], start=True, stop=True)
                        last.then_inc(s["s_sum"], 1)
                clear(sems)

        def gate(xT, xh, xl, cn_h, cn_l):
            names = "s_mch s_mcc s_mcl s_eg s_g " + WSEMS
            ctx, sems = stage(names)
            s = dict(zip(names.split(), sems))
            wl = [s[f"s_wl{i}"] for i in range(RAW)]
            NW = ET + 2 * DT
            with ctx:
                mc, eg = sb("mc", [P, DT, S], ctx=ctx), sb("eg", [P, DT, S], ctx=ctx)
                mch, mcl = sb("mch", [P, DT, S], f32r, ctx=ctx), sb("mcl", [P, DT, S], f32r, ctx=ctx)
                with nc.Block() as block:
                    @block.sync
                    def _(sp):
                        for n in range(NW):
                            src = wmT_d[n * P:(n + 1) * P, :] if n < ET else wgT_d[(n - ET) * P:(n - ET + 1) * P, :]
                            load_w(sp, n, src, wl, s["s_ws"])

                    @block.scalar
                    def _(act):
                        act.wait_ge(s["s_wu"], ET)
                        for j in range(DT):
                            nc.scalar.activation(mch[:, j, :], ps[:, j, :], ACT.Copy).then_inc(s["s_mch"], 1)
                        act.wait_ge(s["s_wu"], NW)
                        for j in range(DT):
                            nc.scalar.activation(eg[:, j, :], ps[:, 4 + j, :], ACT.Sigmoid, bias=cols[:, 4, j:j + 1])\
                                .then_inc(s["s_eg"], 1)

                    @block.vector
                    def _(dve):
                        for n in range(NW):
                            if n == ET + SPLIT:
                                for j in range(DT):
                                    dve.wait_ge(s["s_mch"], j + 1)
                                    nc.vector.tensor_copy(mc[:, j, :], ps[:, j, :]).then_inc(s["s_mcc"], 1)
                                    nc.vector.tensor_tensor(out=mcl[:, j, :], in0=ps[:, j, :],
                                                            in1=mch[:, j, :].bitcast(f32), op=ALU.subtract)\
                                        .then_inc(s["s_mcl"], 1)
                            split_w(dve, n, wl, s["s_wh"], s["s_ws"], s["s_wu"])
                        for j in range(DT):
                            dve.wait_ge(s["s_eg"], j + 1)
                            nc.vector.tensor_tensor(out=eg[:, j, :], in0=eg[:, j, :], in1=mc[:, j, :], op=ALU.mult)\
                                .then_inc(s["s_g"], 1)
                            dve.wait_ge(s["s_g"], 2 * j + 1)
                            nc.vector.tensor_tensor(out=h[:, j, :], in0=eg[:, j, :], in1=xT[:, j, :], op=ALU.add)\
                                .then_inc(s["s_g"], 1)

                    @block.tensor
                    def _(pe):
                        for n in range(NW):
                            pe.wait_ge(s["s_ws"], n + 1)
                            if n < ET:
                                rh, rl, at = cn_h[:, n, :], cn_l[:, n, :], 0
                                first, end = n == 0, n == ET - 1
                            else:
                                k = n - ET
                                if k == DT:
                                    pe.wait_ge(s["s_mcl"], DT)
                                rh, rl = (xh[:, k, :], xl[:, k, :]) if k < DT else (mch[:, k - DT, :], mcl[:, k - DT, :])
                                at, first, end = 4, k == 0, k == 2 * DT - 1
                            for j in range(DT):
                                cut = slice(j * P, (j + 1) * P)
                                last = three(ps[:, at + j, :], w_hi[:, n % SPLIT, cut], w_lo[:, n % SPLIT, cut], rh, rl,
                                             first, end)
                            last.then_inc(s["s_wu"], 1)
                clear(sems)

        def norm(w, outs, twice=False):
            NS = 2 if twice else 1
            names = "s_sq s_ss s_ln s_ex s_rs s_kp s_h s_n s_hi s_lo"
            ctx, sems = stage(names)
            s = dict(zip(names.split(), sems))
            with ctx:
                sq = sb("sq", [P, NS, DT, S], ctx=ctx)
                lnv, rstd = sb("lnv", [P, NS, S], ctx=ctx), sb("rstd", [P, NS, S], ctx=ctx)
                sums2 = sb("sums2", [P, S], ctx=ctx) if twice else None
                rs = [rstd[:, n, :] for n in range(NS)]
                kept = sb("kept", [P, 2, S], ctx=ctx) if len(outs) == 2 else None
                full = sq[:, 0, 0:2, :]
                with nc.Block() as block:
                    @block.scalar
                    def _(act):
                        for n in range(NS):
                            for k in range(DT):
                                nc.scalar.activation(sq[:, n, k, :], h[:, k, :], ACT.Square,
                                                     scale=cols[:, 0, k:k + 1] if n else 1.0).then_inc(s["s_sq"], 1)
                        for n in range(NS):
                            act.wait_ge(s["s_ss"], n + 1)
                            if n:
                                act.wait_ge(s["s_rs"], 2)
                            nc.scalar.activation(lnv[:, n, :], sums2[:, :] if n else ps[:, 0, :], ACT.Ln, bias=eps_col[:, 0:1],
                                                 scale=1.0 / D).then_inc(s["s_ln"], 1)
                            act.wait_ge(s["s_ln"], n + 1)
                            nc.scalar.activation(rs[n], lnv[:, n, :], ACT.Exp, scale=-0.5).then_inc(s["s_ex"], 1)
                        for n, (e, k) in enumerate((e, k) for e in range(len(outs)) for k in range(DT)):
                            act.wait_ge(s["s_n"], n + 1)
                            nc.scalar.activation(outs[e][0][:, k, :], full[:, n % 2, :], ACT.Copy).then_inc(s["s_hi"], 1)

                    @block.tensor
                    def _(pe):
                        for n in range(NS):
                            for k in range(DT):
                                pe.wait_ge(s["s_sq"], n * DT + k + 1)
                                last = nc.tensor.matmul(ps[:, n, :], ones[:, :], sq[:, n, k, :], start=k == 0, stop=k == DT - 1)
                            last.then_inc(s["s_ss"], 1)

                    @block.vector
                    def _(dve):
                        dve.wait_ge(s["s_ex"], 1)
                        if twice:
                            nc.vector.tensor_tensor(out=sums2[:, :], in0=rs[0], in1=rs[0], op=ALU.mult).then_inc(s["s_rs"], 1)
                            dve.wait_ge(s["s_ss"], 2)
                            dve.wait_ge(s["s_rs"], 1)
                            nc.vector.tensor_tensor(out=sums2[:, :], in0=sums2[:, :], in1=ps[:, 1, :], op=ALU.mult)\
                                .then_inc(s["s_rs"], 1)
                            for k in range(DT):
                                nc.vector.scalar_tensor_tensor(out=h[:, k, :], in0=h[:, k, :], scalar=cols[:, 0, k:k + 1],
                                                               in1=rs[0], op0=ALU.mult, op1=ALU.mult).then_inc(s["s_h"], 1)
                            dve.wait_ge(s["s_h"], DT)
                            dve.wait_ge(s["s_ex"], 2)
                        by = [rs[-1]]
                        if len(outs) == 2:
                            for e in range(2):
                                nc.vector.tensor_tensor(out=kept[:, e, :], in0=rs[-1], in1=keep_expert[:, e, :],
                                                        op=ALU.mult).then_inc(s["s_kp"], 1)
                            dve.wait_ge(s["s_kp"], 2)
                            by = [kept[:, e, :] for e in range(2)]
                        tiles = [(e, k) for e in range(len(outs)) for k in range(DT)]
                        for n in range(len(tiles) + 1):
                            if n < len(tiles):
                                e, k = tiles[n]
                                if n >= 2:
                                    dve.wait_ge(s["s_lo"], n - 1)
                                nc.vector.scalar_tensor_tensor(out=full[:, n % 2, :], in0=h[:, k, :],
                                                               scalar=cols[:, w, k:k + 1], in1=by[e],
                                                               op0=ALU.mult, op1=ALU.mult).then_inc(s["s_n"], 1)
                            if n >= 1:
                                e, k = tiles[n - 1]
                                dve.wait_ge(s["s_hi"], n)
                                nc.vector.tensor_tensor(out=outs[e][1][:, k, :], in0=full[:, (n - 1) % 2, :],
                                                        in1=outs[e][0][:, k, :].bitcast(f32), op=ALU.subtract)\
                                    .then_inc(s["s_lo"], 1)
                clear(sems)

        HALF = DT // 2
        STACKED_HEADS = 16 * 3 * P // HD

        def stack_heads(sp, st, parts, c0, n, at, done):
            for j in range(P // HD):
                for r, part in enumerate(parts):
                    sp.dma_start(st[r * HD:(r + 1) * HD, 4 * c0 + j:4 * (c0 + n):P // HD, :].bitcast(f32),
                                 part[j * HD:(j + 1) * HD, at:at + n, :].bitcast(f32)).then_inc(done, 16)

        def qkv(xe, v_nat, q_st, k_st, early_v, late):
            names = "s_z s_qf s_rot s_t1 s_rp s_rh s_rl s_stk s_v " + WSEMS
            ctx, sems = stage(names)
            s = dict(zip(names.split(), sems))
            wl = [s[f"s_wl{i}"] for i in range(RAW)]
            weights = [t["L1_xattn_l_qkv"], t["L1_xattn_v_qkv"]]
            G = 2 * DT
            with ctx:
                plain = sb("plain", [P, 2 * DT, S], ctx=ctx)
                soon = (sb("rhi", [P, 2 * DT - HALF, S], f32r, ctx=ctx), sb("rlo", [P, 2 * DT - HALF, S], f32r, ctx=ctx))
                hi, lo = ([soon[i][:, c, :] for c in range(2 * DT - HALF)] + [late[i][:, c, :] for c in range(HALF)]
                          for i in range(2))
                t1, t2 = sb("t1", [P, 2, S], ctx=ctx), sb("t2", [P, 2, S], ctx=ctx)
                with nc.Block() as block:
                    @block.sync
                    def _(sp):
                        for n in range(3 * G):
                            g, k, e = n // G, n % G // 2, n % 2
                            load_w(sp, n, weights[e][k * P:(k + 1) * P, g * D:(g + 1) * D], wl, s["s_ws"])
                        sp.wait_ge(s["s_z"], 2)
                        sp.dma_start(k_st[3 * HD:3 * HD + 1, :, :].bitcast(f32).rearrange("a (r h) n -> a r (h n)", r=8),
                                     ones_d[:, 0:NH // 8 * S].rearrange("(a r) n -> a r n", a=1)).then_inc(s["s_stk"], 16)
                        sp.wait_ge(s["s_rl"], DT)
                        stack_heads(sp, q_st, (soon[0], soon[0], soon[1]), 0, DT, 0, s["s_stk"])
                        sp.wait_ge(s["s_rl"], DT + HALF)
                        stack_heads(sp, k_st, (soon[0], soon[1], soon[0]), 0, HALF, DT, s["s_stk"])
                        sp.wait_ge(s["s_stk"], 16 + 2 * STACKED_HEADS)

                    @block.scalar
                    def _(act):
                        for c in range(2 * DT):
                            if c % DT == 0:
                                act.wait_ge(s["s_wu"], G * (c // DT + 1))
                            nc.scalar.activation(plain[:, c, :], ps[:, c, :], ACT.Copy).then_inc(s["s_qf"], 1)
                        for c in range(2 * DT):
                            act.wait_ge(s["s_rp"], 2 * c + 2)
                            nc.scalar.activation(hi[c], t1[:, c % 2, :], ACT.Copy).then_inc(s["s_rh"], 1)
                        act.wait_ge(s["s_wu"], 3 * G)
                        for a in range(ST):
                            nc.scalar.activation(v_nat[:, a, :], ps[:, a, :], ACT.Copy)

                    @block.gpsimd
                    def _(pool):
                        nc.gpsimd.memset(q_st[3 * HD:P, :, :].bitcast(f32), 0.0).then_inc(s["s_z"], 1)
                        pool.wait_ge(s["s_z"], 1)
                        nc.gpsimd.memset(k_st[3 * HD:P, :, :].bitcast(f32), 0.0).then_inc(s["s_z"], 1)
                        pool.wait_ge(s["s_z"], 2)
                        for c in range(2 * DT):
                            pool.wait_ge(s["s_qf"], c + 1)
                            if c >= 2:
                                pool.wait_ge(s["s_rl"], c - 1)
                            nc.gpsimd.tensor_tensor(out=t1[:, c % 2, :], in0=plain[:, c, :], in1=cos_t[:, :], op=ALU.mult)\
                                .then_inc(s["s_t1"], 1)

                    @block.vector
                    def _(dve):
                        for n in range(2 * G + SPLIT):
                            split_w(dve, n, wl, s["s_wh"], s["s_ws"], s["s_wu"])
                        for c in range(2 * DT + 1):
                            if c < 2 * DT:
                                dve.wait_ge(s["s_rot"], c + 1)
                                nc.vector.tensor_tensor(out=t2[:, c % 2, :], in0=ps[:, c, :], in1=sin_t[:, :], op=ALU.mult)\
                                    .then_inc(s["s_rp"], 1)
                                dve.wait_ge(s["s_rp"], 2 * c + 1)
                                dve.wait_ge(s["s_t1"], c + 1)
                                nc.vector.tensor_tensor(out=t1[:, c % 2, :], in0=t1[:, c % 2, :], in1=t2[:, c % 2, :],
                                                        op=ALU.add).then_inc(s["s_rp"], 1)
                            if c >= 1:
                                dve.wait_ge(s["s_rh"], c)
                                nc.vector.tensor_tensor(out=lo[c - 1], in0=t1[:, (c - 1) % 2, :], in1=hi[c - 1].bitcast(f32),
                                                        op=ALU.subtract).then_inc(s["s_rl"], 1)
                            if c >= DT and 2 * G + SPLIT + c - DT < 3 * G:
                                split_w(dve, 2 * G + SPLIT + c - DT, wl, s["s_wh"], s["s_ws"], s["s_wu"])

                    @block.tensor
                    def _(pe):
                        def project(n, t0):
                            g, k, e = n // G, n % G // 2, n % 2
                            xh_, xl_ = xe[e]
                            pe.wait_ge(s["s_ws"], n + 1)
                            first, end = n % G == 0, k == DT - 1
                            wide = slice(t0 if e else 0, S)
                            for j in range(DT):
                                cut = slice(j * P, (j + 1) * P)
                                if g < 2:
                                    last = three(ps[:, g * 4 + j, wide], w_hi[:, n % SPLIT, cut], w_lo[:, n % SPLIT, cut],
                                                 xh_[:, k, wide], xl_[:, k, wide], first, end,
                                                 skip_group_check=True)
                                elif (j + 1) * P > wide.start:
                                    last = three(ps[:, j, :], xh_[:, k, cut], xl_[:, k, cut],
                                                 w_hi[:, n % SPLIT, :], w_lo[:, n % SPLIT, :], first, end,
                                                 skip_group_check=True)
                            last.then_inc(s["s_wu"], 1)

                        def run(t0):
                            for n in range(2 * G):
                                project(n, t0)
                            for c in range(2 * DT):
                                pe.wait_ge(s["s_qf"], c + 1)
                                nc.tensor.matmul(ps[:, c, :], rot[:, :], plain[:, c, :], start=True, stop=True)\
                                    .then_inc(s["s_rot"], 1)
                            pe.wait_ge(s["s_rp"], 2 * DT)
                            for n in range(2 * G, 3 * G):
                                project(n, t0)

                        for_v_tokens(early_v, run)
                clear(sems)

        def side_work(groups, steps, maxima, lead):
            queue = [o for g in range(groups) for o in [("max", g, i) for i in range(maxima)] + [("turn", g)]]
            first = maxima + 1 + lead
            start, queue, by_step = queue[:first], queue[first:], []
            for u in range(groups * steps):
                g, kt = divmod(u, steps)
                now = [(("flip", "back")[kt], g - 1)] if kt < 2 and g else []
                due = -(-(u + 1) * (maxima + 1) // steps)
                while queue and len(start) + sum(o[0] in ("max", "turn") for d in by_step + [now] for o in d) < first + due:
                    now.append(queue.pop(0))
                by_step.append(now)
            by_step.append([("flip", groups - 1), ("back", groups - 1)])
            return start, by_step

        def flip_sums(bank, sums, heads):
            for q in range(ST):
                last = nc.tensor.matmul(bank[:, 4 * q:4 * q + 4], sums[:, q * P:(q + 1) * P], heads, start=True, stop=True)
            return last

        def spread_back(bank, rq, width):
            heads = P // width
            for q in range(ST):
                for j in range(heads):
                    by = rq[:, heads * q + j:heads * q + j + 1].broadcast_to((P, width))
                    last = nc.tensor.matmul(bank[j * width:(j + 1) * width, q * P:(q + 1) * P], by, ident[:, :],
                                            start=True, stop=True)
            return last

        def self_attention(v_nat, q_st, k_st, ae, late):
            names = "s_late s_fill s_used s_sh s_sc s_exp s_pv s_ob s_part"
            ctx, sems = stage(names)
            s = dict(zip(names.split(), sems))
            NG, SCALE = NH // 4, float(HD) ** -0.5
            start, by_step = side_work(NG, ST, 4 * ST, 10)
            order = start + [o for now in by_step for o in now]
            place = {o: n for n, o in enumerate(order)}
            with ctx:
                row_max = sb("row_max_s", [P, NG, ST, 4], ctx=ctx)
                shift = sb("shift_s", [4, NG, S], ctx=ctx, dt=f32r)
                pT = sb("pT_s", [P, 2, 4, S], ctx=ctx)
                osb = sb("osb_s", [P, 2, S], ctx=ctx)
                rq = sb("rq_s", [P, 4 * ST], ctx=ctx)
                att, own = sb("att_s", [P, S], ctx=ctx), sb("own", [P, 2, S], ctx=ctx)
                with nc.Block() as block:
                    @block.sync
                    def _(sp):
                        stack_heads(sp, k_st, (late[0], late[1], late[0]), HALF, HALF, 0, s["s_late"])
                        for g in range(NG):
                            sp.wait_ge(s["s_used"], place["turn", g] + 1)
                            for j in range(4):
                                sp.dma_start(q_st[3 * HD:3 * HD + 1, 4 * g + j, :].bitcast(f32),
                                             shift[j:j + 1, g, :].bitcast(f32)).then_inc(s["s_sh"], 16)

                    @block.scalar
                    def _(act):
                        for g in range(NG):
                            for kt in range(ST):
                                u, n = g * ST + kt, S - kt * P
                                for half in range(2):
                                    act.wait_ge(s["s_sc"], 2 * u + half + 1)
                                    if u >= 2:
                                        act.wait_ge(s["s_pv"], u - 1)
                                    nc.scalar.activation(pT[:, u % 2, 2 * half:2 * half + 2, 0:n],
                                                         ps[:, 2 + 2 * half:4 + 2 * half, 0:n], ACT.Exp, scale=SCALE)\
                                        .then_inc(s["s_exp"], 1)

                    @block.vector
                    def _(dve):
                        for n, o in enumerate(order):
                            g, bank = o[1], ps[:, n % 2, :]
                            if o[0] == "flip":
                                dve.wait_ge(s["s_pv"], (g + 1) * ST)
                                if g:
                                    dve.wait_ge(s["s_used"], place["back", g - 1] + 1)
                                nc.vector.tensor_copy(osb[:, :, :], ps[:, 6:8, :]).then_inc(s["s_ob"], 1)
                            dve.wait_ge(s["s_fill"], n + 1)
                            if o[0] == "max":
                                q, j = divmod(o[2], 4)
                                last = nc.vector.tensor_reduce(out=row_max[:, g, q, j:j + 1], in_=bank[:, 0:(q + 1) * P],
                                                               axis=AX.X, op=ALU.max)
                            elif o[0] == "turn":
                                last = nc.vector.tensor_copy(shift[:, g, :], bank[0:4, :])
                            elif o[0] == "flip":
                                last = nc.vector.reciprocal(rq[:, :], bank[:, 0:4 * ST])
                            else:
                                if g:
                                    dve.wait_ge(s["s_part"], 6 * g)
                                last = nc.vector.tensor_tensor(out=att[:, :], in0=osb[:, 0, :], in1=bank, op=ALU.mult)
                            last.then_inc(s["s_used"], 1)
                            if o[0] == "back":
                                dve.wait_ge(s["s_used"], n + 1)
                                for e, (hi, lo) in enumerate(ae):
                                    nc.vector.tensor_tensor(out=own[:, e, :], in0=att[:, :], in1=keep_expert[:, e, :],
                                                            op=ALU.mult).then_inc(s["s_part"], 1)
                                for e, (hi, lo) in enumerate(ae):
                                    dve.wait_ge(s["s_part"], 6 * g + e + 1)
                                    nc.vector.tensor_copy(hi[:, g, :], own[:, e, :]).then_inc(s["s_part"], 1)
                                for e, (hi, lo) in enumerate(ae):
                                    dve.wait_ge(s["s_part"], 6 * g + 3 + e)
                                    nc.vector.tensor_tensor(out=lo[:, g, :], in0=own[:, e, :],
                                                            in1=hi[:, g, :].bitcast(f32), op=ALU.subtract)\
                                        .then_inc(s["s_part"], 1)

                    @block.tensor
                    def _(pe):
                        def fill(o):
                            n, g = place[o], o[1]
                            bank = ps[:, n % 2, :]
                            if n >= 2:
                                pe.wait_ge(s["s_used"], n - 1)
                            if o[0] == "max":
                                q, j = divmod(o[2], 4)
                                hd = 4 * g + j
                                if (g, o[2]) == (HALF, 0):
                                    pe.wait_ge(s["s_late"], STACKED_HEADS)
                                nc.tensor.matmul(bank[:, q * P:(q + 1) * P], ident_b[:, :], mask_qk[:, :],
                                                 start=True, stop=False, skip_group_check=True)
                                last = nc.tensor.matmul(bank[:, 0:(q + 1) * P], q_st[:, hd, q * P:(q + 1) * P],
                                                        k_st[:, hd, 0:(q + 1) * P], start=False, stop=True,
                                                        skip_group_check=True)
                            elif o[0] == "turn":
                                pe.wait_ge(s["s_used"], n)
                                for q in range(ST):
                                    last = nc.tensor.matmul(bank[0:4, q * P:(q + 1) * P], row_max[:, g, q, :],
                                                            neg_ident[:, :], start=True, stop=True)
                            elif o[0] == "flip":
                                pe.wait_ge(s["s_ob"], g + 1)
                                last = flip_sums(bank, osb[:, 1, :], sel[:, 0:4])
                            else:
                                pe.wait_ge(s["s_used"], n)
                                last = spread_back(bank, rq, HD)
                            last.then_inc(s["s_fill"], 1)

                        def scores(u, half, todo):
                            g, kt = divmod(u, ST)
                            n = S - kt * P
                            if kt == 0 and half == 0:
                                pe.wait_ge(s["s_sh"], 64 * (g + 1))
                            if u >= 1:
                                pe.wait_ge(s["s_exp"], 2 * (u - 1) + half + 1)
                            for j in range(2):
                                if j and todo:
                                    fill(todo.pop(0))
                                hd, bank = 4 * g + 2 * half + j, 2 + 2 * half + j
                                nc.tensor.matmul(ps[:, bank, 0:P], ident_b[:, :], mask_kq[:, :],
                                                 start=True, stop=False, skip_group_check=True)
                                last = nc.tensor.matmul(ps[:, bank, 0:n], k_st[:, hd, kt * P:(kt + 1) * P],
                                                        q_st[:, hd, kt * P:S], start=False, stop=True,
                                                        skip_group_check=True)
                            last.then_inc(s["s_sc"], 1)

                        for o in start:
                            fill(o)
                        scores(0, 0, [])
                        scores(0, 1, [])
                        for u in range(NG * ST):
                            g, kt = divmod(u, ST)
                            todo = list(by_step[u])
                            for half in range(2):
                                if todo:
                                    fill(todo.pop(0))
                                if u + 1 < NG * ST:
                                    scores(u + 1, half, todo)
                            while todo:
                                fill(todo.pop(0))
                            pe.wait_ge(s["s_exp"], 2 * u + 2)
                            if kt == 0 and g:
                                pe.wait_ge(s["s_ob"], g)
                            n = S - kt * P
                            for j in range(4):
                                nc.tensor.matmul(ps[j * HD:(j + 1) * HD, 6, kt * P:S],
                                                 v_nat[:, kt, (4 * g + j) * HD:(4 * g + j + 1) * HD],
                                                 pT[:, u % 2, j, 0:n], start=kt == 0, stop=kt == ST - 1)
                            for j in range(4):
                                last = nc.tensor.matmul(ps[j * HD:(j + 1) * HD, 7, kt * P:S], ones[:, 0:HD],
                                                        pT[:, u % 2, j, 0:n], start=kt == 0, stop=kt == ST - 1)
                            last.then_inc(s["s_pv"], 1)
                        for o in by_step[NG * ST]:
                            fill(o)
                clear(sems)

        def add_projection(tiles, parts, early_v=None):
            names = "s_add " + WSEMS
            ctx, sems = stage(names)
            s = dict(zip(names.split(), sems))
            wl = [s[f"s_wl{i}"] for i in range(RAW)]
            NW = len(tiles)
            with ctx:
                with nc.Block() as block:
                    @block.sync
                    def _(sp):
                        for n in range(NW):
                            load_w(sp, n, tiles[n], wl, s["s_ws"])

                    @block.vector
                    def _(dve):
                        for n in range(NW):
                            split_w(dve, n, wl, s["s_wh"], s["s_ws"], s["s_wu"])
                        dve.wait_ge(s["s_wu"], NW)
                        for j in range(DT):
                            nc.vector.tensor_tensor(out=h[:, j, :], in0=h[:, j, :], in1=ps[:, j, :], op=ALU.add)

                    @block.tensor
                    def _(pe):
                        def run(t0):
                            for n in range(NW):
                                wide = slice(t0 if n % 2 else 0, S)
                                pe.wait_ge(s["s_ws"], n + 1)
                                for j in range(DT):
                                    cut = slice(j * P, (j + 1) * P)
                                    last = three(ps[:, j, wide], w_hi[:, n % SPLIT, cut], w_lo[:, n % SPLIT, cut],
                                                 parts[n][0][:, wide], parts[n][1][:, wide], n == 0, n >= NW - (1 if early_v is None else 2),
                                                 skip_group_check=True)
                                last.then_inc(s["s_wu"], 1)

                        if early_v is None:
                            run(0)
                        else:
                            for_v_tokens(early_v, run)
                clear(sems)

        def split(src, hi, lo, by=None):
            names = "s_m s_h s_l"
            ctx, (s_m, s_h, s_l) = stage(names)
            n = src.shape[1]
            with ctx:
                tmp = sb("split_tmp", [P, n, S], ctx=ctx) if by is not None else src
                with nc.Block() as block:
                    @block.scalar
                    def _(act):
                        for k in range(n):
                            if by is not None:
                                act.wait_ge(s_m, k + 1)
                            nc.scalar.activation(hi[:, k, :], tmp[:, k, :], ACT.Copy).then_inc(s_h, 1)

                    @block.vector
                    def _(dve):
                        if by is not None:
                            for k in range(n):
                                nc.vector.tensor_tensor(out=tmp[:, k, :], in0=src[:, k, :], in1=by, op=ALU.mult)\
                                    .then_inc(s_m, 1)
                        for k in range(n):
                            dve.wait_ge(s_h, k + 1)
                            nc.vector.tensor_tensor(out=lo[:, k, :], in0=tmp[:, k, :], in1=hi[:, k, :].bitcast(f32),
                                                    op=ALU.subtract)
                clear([s_m, s_h, s_l])

        STEP, SHIFT = P // 2, 3 * CHD

        def context_parts(b, ch, cl, k_st):
            names = "s_c s_tr s_th s_tl"
            ctx, sems = stage(names)
            s_c, s_tr, s_th, s_tl = sems
            units = [(e, kb) for e in range(ET) for kb in range(len(KEY_BANKS))]
            with ctx:
                cs = sb("cs_x", [P, KT, E], ctx=ctx)
                with nc.Block() as block:
                    @block.sync
                    def _(sp):
                        full = KEYS // P
                        sp.dma_start(cs[:, 0:full, :], t["ctx_1024"][b, 0:full * P].rearrange("(a p) n -> p a n", p=P))\
                            .then_inc(s_c, 16)
                        sp.dma_start(cs[0:KEYS - full * P, full, :], t["ctx_1024"][b, full * P:KEYS]).then_inc(s_c, 16)

                    @block.scalar
                    def _(act):
                        for i, (k, kb) in enumerate(units):
                            act.wait_ge(s_tr, i + 1)
                            k0, kn = KEY_BANKS[kb]
                            nc.scalar.activation(ch[:, k, k0:k0 + kn], ps[:, i, 0:kn], ACT.Copy).then_inc(s_th, 1)

                    @block.gpsimd
                    def _(pool):
                        nc.gpsimd.memset(k_st[STEP // 2:STEP, :, :].bitcast(f32), 0.0)

                    @block.vector
                    def _(dve):
                        nc.vector.memset(k_st[STEP + STEP // 2:P, :, :].bitcast(f32), 0.0)
                        nc.vector.memset(ch[:, :, KEYS:KPAD].bitcast(f32), 0.0)
                        nc.vector.memset(cl[:, :, KEYS:KPAD].bitcast(f32), 0.0)
                        for i, (k, kb) in enumerate(units):
                            dve.wait_ge(s_th, i + 1)
                            k0, kn = KEY_BANKS[kb]
                            nc.vector.tensor_tensor(out=cl[:, k, k0:k0 + kn], in0=ps[:, i, 0:kn],
                                                    in1=ch[:, k, k0:k0 + kn].bitcast(f32), op=ALU.subtract)

                    @block.tensor
                    def _(pe):
                        pe.wait_ge(s_c, 32)
                        for i, (k, kb) in enumerate(units):
                            k0, kn = KEY_BANKS[kb]
                            for a in range(-(-kn // P)):
                                n = min(P, kn - a * P)
                                last = nc.tensor.transpose(ps[:, i, a * P:a * P + n], cs[0:n, k0 // P + a, k * P:(k + 1) * P],
                                                           ident[0:n, 0:n])
                            last.then_inc(s_tr, 1)
                clear(sems)

        def to_stack(sp, heads, parts, c, width, back):
            for par in range(2):
                for r, part in enumerate(parts):
                    src = heads_d[part, c * P:(c + 1) * P, 0:width].rearrange("(m two r) n -> two r m n", two=2, r=CHD)[par]
                    sp.dma_start(heads(par)[par * STEP + r * CHD:par * STEP + (r + 1) * CHD, :, 0:width].bitcast(f32), src)\
                        .then_inc(back, 16)

        STACK_DMAS = 2 * 3 * 16
        STACKED = ET * STACK_DMAS + 2 * 16

        def cross_queries(ci, q_st, s_kst, s_qst):
            names = "s_h s_l s_up0 s_up1 s_z " + WSEMS
            ctx, sems = stage(names)
            s = dict(zip(names.split(), sems))
            wl = [s[f"s_wl{i}"] for i in range(RAW)]
            with ctx:
                hi, lo = sb("qc_h", [P, ET, S], f32r, ctx=ctx), sb("qc_l", [P, ET, S], f32r, ctx=ctx)
                with nc.Block() as block:
                    @block.sync
                    def _(sp):
                        for k in range(DT):
                            load_w(sp, k, t["L1_xattn_cq_w"][k * P:(k + 1) * P, :], wl, s["s_ws"])
                        sp.wait_ge(s_kst, STACKED)
                        for c in range(ET):
                            for part, src, ready in ((0, hi, "s_h"), (1, lo, "s_l")):
                                sp.wait_ge(s[ready], c + 1)
                                sp.dma_start(heads_d[part, c * P:(c + 1) * P, 0:S], src[:, c, :].bitcast(f32))\
                                    .then_inc(s[f"s_up{c}"], 16)
                        sp.wait_ge(s["s_z"], 2)
                        for c in range(ET):
                            sp.wait_ge(s[f"s_up{c}"], 32)
                            to_stack(sp, lambda par: q_st[:, 8 * c + par:8 * c + 8:2, :], (0, 0, 1), c, S, s_qst[c])

                    @block.gpsimd
                    def _(pool):
                        nc.gpsimd.memset(q_st[:, 0:NH // 2, :].bitcast(f32), 0.0).then_inc(s["s_z"], 1)

                    @block.scalar
                    def _(act):
                        act.wait_ge(s["s_wu"], DT)
                        for c in range(ET):
                            nc.scalar.activation(hi[:, c, :], ps[:, c, :], ACT.Copy).then_inc(s["s_h"], 1)

                    @block.vector
                    def _(dve):
                        nc.vector.memset(q_st[:, NH // 2:NH, :].bitcast(f32), 0.0).then_inc(s["s_z"], 1)
                        for k in range(DT):
                            split_w(dve, k, wl, s["s_wh"], s["s_ws"], s["s_wu"], width=E)
                        for c in range(ET):
                            dve.wait_ge(s["s_h"], c + 1)
                            nc.vector.tensor_tensor(out=lo[:, c, :], in0=ps[:, c, :], in1=hi[:, c, :].bitcast(f32),
                                                    op=ALU.subtract).then_inc(s["s_l"], 1)

                    @block.tensor
                    def _(pe):
                        for k in range(DT):
                            pe.wait_ge(s["s_ws"], k + 1)
                            for c in range(ET):
                                cut = slice(c * P, (c + 1) * P)
                                last = three(ps[:, c, :], w_hi[:, k % SPLIT, cut], w_lo[:, k % SPLIT, cut],
                                             ci[0][:, k, :], ci[1][:, k, :], k == 0, k == DT - 1)
                            last.then_inc(s["s_wu"], 1)
                clear(sems)

        def cross_keys(ch, cl, k_st, v_aug, s_kst):
            names = "s_k s_h s_l s_v s_vc s_up0 s_up1 s_ms " + WSEMS
            ctx, sems = stage(names)
            s = dict(zip(names.split(), sems))
            wl = [s[f"s_wl{i}"] for i in range(RAW)]
            NB = len(KEY_BANKS)
            with ctx:
                hi, lo = sb("kc_h", [P, ET, KPAD], f32r, ctx=ctx), sb("kc_l", [P, ET, KPAD], f32r, ctx=ctx)
                with nc.Block() as block:
                    @block.sync
                    def _(sp):
                        for k in range(ET):
                            load_w(sp, k, t["L1_xattn_ckv_w"][k * P:(k + 1) * P, :], wl, s["s_ws"])
                        for par in range(2):
                            row = par * STEP + SHIFT
                            sp.dma_start(k_st[row:row + 1, :, :].bitcast(f32), ones_d.rearrange("(a h) n -> a h n", a=1))\
                                .then_inc(s_kst, 16)
                        for c in range(ET):
                            for part, src, ready in ((0, hi, "s_h"), (1, lo, "s_l")):
                                sp.wait_ge(s[ready], (c + 1) * NB)
                                sp.dma_start(heads_d[part, c * P:(c + 1) * P, :], src[:, c, :].bitcast(f32))\
                                    .then_inc(s[f"s_up{c}"], 16)
                        for c in range(ET):
                            sp.wait_ge(s[f"s_up{c}"], 32)
                            to_stack(sp, lambda par: k_st[:, 4 * c:4 * c + 4, :], (0, 1, 0), c, KPAD, s_kst)

                    @block.gpsimd
                    def _(pool):
                        nc.gpsimd.memset(v_aug[:, :, :, CHD:2 * CHD], 0.0).then_inc(s["s_ms"], 1)
                        pool.wait_ge(s["s_ms"], 1)
                        nc.gpsimd.memset(v_aug[:, :, :, CHD:CHD + 1], 1.0)

                    @block.scalar
                    def _(act):
                        for i in range(ET * NB):
                            c, (k0, kn) = i // NB, KEY_BANKS[i % NB]
                            kn += kn % 2
                            act.wait_ge(s["s_k"], i + 1)
                            nc.scalar.activation(hi[:, c, k0:k0 + kn], ps[:, i, 0:kn], ACT.Copy).then_inc(s["s_h"], 1)
                        for kt, (k0, kn) in enumerate(KEY_TILES):
                            act.wait_ge(s["s_v"], kt + 1)
                            nc.scalar.activation(v_aug[0:kn, kt, :, 0:CHD],
                                                 ps[0:kn, kt % 8, 0:E].rearrange("p (h d) -> p h d", d=CHD), ACT.Copy)\
                                .then_inc(s["s_vc"], 1)

                    @block.vector
                    def _(dve):
                        for k in range(ET):
                            split_w(dve, k, wl, s["s_wh"], s["s_ws"], s["s_wu"])
                        for i in range(ET * NB):
                            c, (k0, kn) = i // NB, KEY_BANKS[i % NB]
                            kn += kn % 2
                            dve.wait_ge(s["s_h"], i + 1)
                            nc.vector.tensor_tensor(out=lo[:, c, k0:k0 + kn], in0=ps[:, i, 0:kn],
                                                    in1=hi[:, c, k0:k0 + kn].bitcast(f32), op=ALU.subtract)\
                                .then_inc(s["s_l"], 1)

                    @block.tensor
                    def _(pe):
                        pe.wait_ge(s["s_ws"], ET)
                        for i in range(ET * NB):
                            c, (k0, kn) = i // NB, KEY_BANKS[i % NB]
                            kn += kn % 2
                            cut = slice(c * P, (c + 1) * P)
                            for e in range(ET):
                                last = three(ps[:, i, 0:kn], w_hi[:, e, cut], w_lo[:, e, cut],
                                             ch[:, e, k0:k0 + kn], cl[:, e, k0:k0 + kn], e == 0, e == ET - 1)
                            last.then_inc(s["s_k"], 1)
                        for kt, (k0, kn) in enumerate(KEY_TILES):
                            if kt < 8:
                                pe.wait_ge(s["s_l"], kt + 1)
                            else:
                                pe.wait_ge(s["s_vc"], kt - 7)
                            for e in range(ET):
                                last = three(ps[0:kn, kt % 8, 0:E], ch[:, e, k0:k0 + kn], cl[:, e, k0:k0 + kn],
                                             w_hi[:, e, E:2 * E], w_lo[:, e, E:2 * E], e == 0, e == ET - 1)
                            last.then_inc(s["s_v"], 1)
                clear(sems)

        def cross_attention(q_st, k_st, v_aug, ah, al, s_kst, s_qst):
            names = "s_fill s_used s_rm s_sh s_sc s_exp s_pv s_ob s_part"
            ctx, sems = stage(names)
            s = dict(zip(names.split(), sems))
            NG, SCALE = NH // 4, float(CHD) ** -0.5
            UNITS = 4 * ST * 2
            start, by_step = side_work(NG, KT, UNITS, 5)
            order = start + [o for now in by_step for o in now]
            place = {o: n for n, o in enumerate(order)}
            with ctx:
                halves = sb("halves", [P, NG, ST, 4, 2], ctx=ctx)
                row_max = sb("row_max_x", [P, NG, ST, 4], ctx=ctx)
                shift = sb("shift_x", [4, NG, S], ctx=ctx, dt=f32r)
                pT = sb("pT_x", [P, 2, 4, S], ctx=ctx)
                osb, rq = sb("osb", [P, S], ctx=ctx), sb("rq_x", [P, 4 * ST], ctx=ctx)
                att = sb("att_x", [P, S], ctx=ctx)
                with nc.Block() as block:
                    @block.sync
                    def _(sp):
                        for g in range(NG):
                            sp.wait_ge(s["s_used"], place["turn", g] + 1)
                            for j in range(4):
                                hd = 4 * g + j
                                row = hd % 2 * STEP + SHIFT
                                sp.dma_start(q_st[row:row + 1, hd, :].bitcast(f32),
                                             shift[j:j + 1, g, :].bitcast(f32)).then_inc(s["s_sh"], 16)

                    @block.scalar
                    def _(act):
                        for u in range(NG * KT):
                            kn = KEY_TILES[u % KT][1]
                            for j in range(4):
                                v = 4 * u + j
                                act.wait_ge(s["s_sc"], v + 1)
                                if u >= 2 and j == 0:
                                    act.wait_ge(s["s_pv"], u - 1)
                                nc.scalar.activation(pT[0:kn, u % 2, j, :], ps[0:kn, 5 + v % 3, :], ACT.Exp, scale=SCALE)\
                                    .then_inc(s["s_exp"], 1)

                    @block.vector
                    def _(dve):
                        for n, o in enumerate(order):
                            g, at = o[1], 2 * (n % 2)
                            if o[0] == "flip":
                                dve.wait_ge(s["s_pv"], (g + 1) * KT)
                                if g:
                                    dve.wait_ge(s["s_used"], place["back", g - 1] + 1)
                                nc.vector.tensor_copy(osb[:, :], ps[:, 4, :]).then_inc(s["s_ob"], 1)
                            dve.wait_ge(s["s_fill"], n + 1)
                            if o[0] == "max":
                                j, q, half = o[2] // (2 * ST), o[2] // 2 % ST, o[2] % 2
                                last = nc.vector.tensor_reduce(out=halves[:, g, q, j, half:half + 1],
                                                               in_=ps[:, at:at + 2, 0:MAXW], axis=AX.XY, op=ALU.max)
                            elif o[0] == "turn":
                                last = nc.vector.tensor_copy(shift[:, g, :], ps[0:4, at, :])
                            elif o[0] == "flip":
                                last = nc.vector.reciprocal(rq[:, :], ps[:, at, 0:4 * ST])
                            else:
                                if g:
                                    dve.wait_ge(s["s_part"], 2 * g)
                                last = nc.vector.tensor_tensor(out=att[:, :], in0=osb[:, :], in1=ps[:, at, :], op=ALU.mult)
                            last.then_inc(s["s_used"], 1)
                            if o[0] == "back":
                                dve.wait_ge(s["s_used"], n + 1)
                                nc.vector.tensor_copy(ah[:, g, :], att[:, :]).then_inc(s["s_part"], 1)
                                dve.wait_ge(s["s_part"], 2 * g + 1)
                                nc.vector.tensor_tensor(out=al[:, g, :], in0=att[:, :], in1=ah[:, g, :].bitcast(f32),
                                                        op=ALU.subtract).then_inc(s["s_part"], 1)
                            if o[0] == "max" and o[2] == UNITS - 1:
                                dve.wait_ge(s["s_used"], n + 1)
                                nc.vector.tensor_reduce(out=row_max[:, g, :, :], in_=halves[:, g, :, :, :], axis=AX.X,
                                                        op=ALU.max).then_inc(s["s_rm"], 1)

                    @block.tensor
                    def _(pe):
                        def fill(o):
                            n, g = place[o], o[1]
                            at = 2 * (n % 2)
                            if n >= 2:
                                pe.wait_ge(s["s_used"], n - 1)
                            if o[0] == "max":
                                j, q, half = o[2] // (2 * ST), o[2] // 2 % ST, o[2] % 2
                                hd = 4 * g + j
                                if n == 0:
                                    pe.wait_ge(s_kst, STACKED)
                                if o[2] == 0:
                                    pe.wait_ge(s_qst[hd * CHD // P], STACK_DMAS)
                                for i in range(2):
                                    k0 = MAX_STARTS[2 * half + i]
                                    last = nc.tensor.matmul(ps[:, at + i, 0:MAXW], q_st[:, hd, q * P:(q + 1) * P],
                                                            k_st[:, hd // 2, k0:k0 + MAXW], start=True, stop=True)
                            elif o[0] == "turn":
                                pe.wait_ge(s["s_rm"], g + 1)
                                for q in range(ST):
                                    last = nc.tensor.matmul(ps[0:4, at, q * P:(q + 1) * P], row_max[:, g, q, :],
                                                            neg_ident[:, :], start=True, stop=True)
                            elif o[0] == "flip":
                                pe.wait_ge(s["s_ob"], g + 1)
                                last = flip_sums(ps[:, at, :], osb, sel[:, 4:8])
                            else:
                                pe.wait_ge(s["s_used"], n)
                                last = spread_back(ps[:, at, :], rq, HD)
                            last.then_inc(s["s_fill"], 1)

                        def score(u, j):
                            g, kt = divmod(u, KT)
                            k0, kn = KEY_TILES[kt]
                            v, hd = 4 * u + j, 4 * g + j
                            if kt == 0 and j == 0:
                                pe.wait_ge(s["s_sh"], 64 * (g + 1))
                            if v >= 3:
                                pe.wait_ge(s["s_exp"], v - 2)
                            nc.tensor.matmul(ps[0:kn, 5 + v % 3, :], k_st[:, hd // 2, k0:k0 + kn], q_st[:, hd, :],
                                             start=True, stop=True).then_inc(s["s_sc"], 1)

                        for o in start:
                            fill(o)
                        for j in range(3):
                            score(0, j)
                        for u in range(NG * KT):
                            g, kt = divmod(u, KT)
                            todo = list(by_step[u])

                            def side():
                                if todo:
                                    fill(todo.pop(0))

                            def ahead(v):
                                if v < 4 * NG * KT:
                                    score(v // 4, v % 4)

                            side()
                            ahead(4 * u + 3)
                            ahead(4 * u + 4)
                            side()
                            ahead(4 * u + 5)
                            pe.wait_ge(s["s_exp"], 4 * u + 4)
                            if kt == 0 and g:
                                pe.wait_ge(s["s_ob"], g)
                            kn = KEY_TILES[kt][1]
                            for j in range(4):
                                last = nc.tensor.matmul(ps[j * HD:(j + 1) * HD, 4, :], v_aug[0:kn, kt, 4 * g + j, :],
                                                        pT[0:kn, u % 2, j, :], start=kt == 0, stop=kt == KT - 1)
                            last.then_inc(s["s_pv"], 1)
                            side()
                            ahead(4 * u + 6)
                            while todo:
                                side()
                        for o in by_step[NG * KT]:
                            fill(o)
                clear(sems)

        def store_stream(b):
            ctx, (s_st,) = stage("s_st")
            with ctx:
                with nc.Block() as block:
                    @block.sync
                    def _(sp):
                        sp.dma_start(h_d[b], h[:, :, :]).then_inc(s_st, 16)
                        sp.dma_start(keep_d[:, b, :].rearrange("e (a n) -> a e n", a=1), keep_expert[0:1, :, :]).then_inc(s_st, 16)
                        sp.wait_ge(s_st, 32)
                clear([s_st])

        def load_stream(g, flags):
            names = "s_ld s_fl"
            ctx, (s_ld, s_fl) = stage(names)
            with ctx:
                any_token = sb("any_token", [1, 2], ctx=ctx)
                with nc.Block() as block:
                    @block.sync
                    def _(sp):
                        for b in range(B):
                            sp.dma_start(h[:, :, b * P:(b + 1) * P], h_d[b, :, :, bass.ts(g, P)]).then_inc(s_ld, 16)
                        for e in range(2):
                            sp.dma_start(keep_expert[:, e, :].rearrange("p (b n) -> p b n", n=P),
                                         keep_d[e:e + 1, :, bass.ts(g, P)].broadcast_to((P, B, P))).then_inc(s_ld, 16)
                        sp.wait_ge(s_ld, 16 * (B + 2))

                    @block.vector
                    def _(dve):
                        dve.wait_ge(s_ld, 16 * (B + 2))
                        nc.vector.tensor_reduce(out=any_token[:, :], in_=keep_expert[0:1, :, :], axis=AX.X, op=ALU.max)\
                            .then_inc(s_fl, 1)
                        dve.wait_ge(s_fl, 1)
                        nc.vector.tensor_copy(flags[:, :], any_token[:, :])
                clear([s_ld, s_fl])

        def feed_forward(x, keep, gate_w, up_w, down_w):
            names = "s_si s_kp s_mu s_hi s_lo " + WSEMS
            ctx, sems = stage(names)
            s = dict(zip(names.split(), sems))
            wl = [s[f"s_wl{i}"] for i in range(RAW)]
            NC = len(HID_TILES)
            tiles = [(w, c) for c in range(2) for w in "gu"]
            for c in range(NC):
                tiles.append(("d", c))
                if c + 2 < NC:
                    tiles += [("g", c + 2), ("u", c + 2)]
            place = {o: n for n, o in enumerate(tiles)}
            with ctx:
                sg, prod = sb("sg", [P, 2, S], ctx=ctx), sb("prod", [P, 2, S], ctx=ctx)
                hi, lo = sb("hid_h", [P, 2, S], f32r, ctx=ctx), sb("hid_l", [P, 2, S], f32r, ctx=ctx)
                with nc.Block() as block:
                    @block.sync
                    def _(sp):
                        for n, (w, c) in enumerate(tiles):
                            c0, cn = HID_TILES[c]
                            if w == "d":
                                src = down_w[c0:c0 + cn, :]
                            else:
                                src = (gate_w if w == "g" else up_w)[:, c0:c0 + cn].rearrange("(a p) n -> p a n", p=P)
                            load_w(sp, n, src, wl, s["s_ws"])

                    @block.scalar
                    def _(act):
                        for c, (c0, cn) in enumerate(HID_TILES):
                            act.wait_ge(s["s_wu"], place["g", c] + 1)
                            if c >= 2:
                                act.wait_ge(s["s_mu"], c - 1)
                            nc.scalar.activation(sg[0:cn, c % 2, :], ps[0:cn, 4 + c % 2, :], ACT.Silu).then_inc(s["s_si"], 1)
                            act.wait_ge(s["s_mu"], c + 1)
                            if c >= 2:
                                act.wait_ge(s["s_wu"], place["d", c - 2] + 1)
                            nc.scalar.activation(hi[0:cn, c % 2, :], prod[0:cn, c % 2, :], ACT.Copy).then_inc(s["s_hi"], 1)

                    @block.gpsimd
                    def _(pool):
                        for c, (c0, cn) in enumerate(HID_TILES):
                            pool.wait_ge(s["s_si"], c + 1)
                            nc.gpsimd.tensor_tensor(out=sg[0:cn, c % 2, :], in0=sg[0:cn, c % 2, :], in1=keep[0:cn, :],
                                                    op=ALU.mult).then_inc(s["s_kp"], 1)

                    @block.vector
                    def _(dve):
                        def split_tile(w, c):
                            cn = HID_TILES[c][1]
                            rows, width = (cn, D) if w == "d" else (P, DT * cn)
                            split_w(dve, place[w, c], wl, s["s_wh"], s["s_ws"], s["s_wu"], rows, width)

                        for w, c in tiles[0:4]:
                            split_tile(w, c)
                        for c, (c0, cn) in enumerate(HID_TILES):
                            dve.wait_ge(s["s_kp"], c + 1)
                            dve.wait_ge(s["s_wu"], place["u", c] + 1)
                            nc.vector.tensor_tensor(out=prod[0:cn, c % 2, :], in0=ps[0:cn, 6 + c % 2, :], in1=sg[0:cn, c % 2, :],
                                                    op=ALU.mult).then_inc(s["s_mu"], 1)
                            split_tile("d", c)
                            dve.wait_ge(s["s_hi"], c + 1)
                            nc.vector.tensor_tensor(out=lo[0:cn, c % 2, :], in0=prod[0:cn, c % 2, :],
                                                    in1=hi[0:cn, c % 2, :].bitcast(f32), op=ALU.subtract).then_inc(s["s_lo"], 1)
                            if c + 2 < NC:
                                split_tile("g", c + 2)
                                split_tile("u", c + 2)
                        dve.wait_ge(s["s_wu"], len(tiles))
                        for j in range(DT):
                            nc.vector.tensor_tensor(out=h[:, j, :], in0=h[:, j, :], in1=ps[:, j, :], op=ALU.add)

                    @block.tensor
                    def _(pe):
                        for n, (w, c) in enumerate(tiles):
                            cn, slot = HID_TILES[c][1], n % SPLIT
                            pe.wait_ge(s["s_ws"], n + 1)
                            if w == "d":
                                pe.wait_ge(s["s_lo"], c + 1)
                                for j in range(DT):
                                    cut = slice(j * P, (j + 1) * P)
                                    last = three(ps[:, j, :], w_hi[0:cn, slot, cut], w_lo[0:cn, slot, cut],
                                                 hi[0:cn, c % 2, :], lo[0:cn, c % 2, :], c == 0, c == NC - 1)
                            else:
                                if c >= 2:
                                    pe.wait_ge(s["s_mu"], c - 1)
                                bank = ps[0:cn, (4 if w == "g" else 6) + c % 2, :]
                                for k in range(DT):
                                    cut = slice(k * cn, (k + 1) * cn)
                                    last = three(bank, w_hi[:, slot, cut], w_lo[:, slot, cut], x[0][:, k, :], x[1][:, k, :],
                                                 k == 0, k == DT - 1)
                            last.then_inc(s["s_wu"], 1)
                clear(sems)

        def write_out(g):
            names = "s_t s_e s_o"
            ctx, (s_t, s_e, s_o) = stage(names)
            with ctx:
                rows = sb("rows", [P, B, D], ctx=ctx)
                with nc.Block() as block:
                    @block.sync
                    def _(sp):
                        for b in range(B):
                            sp.wait_ge(s_e, b + 1)
                            sp.dma_start(out[b, bass.ts(g, P), :], rows[:, b, :]).then_inc(s_o, 16)
                        sp.wait_ge(s_o, 16 * B)

                    @block.scalar
                    def _(act):
                        for b in range(B):
                            act.wait_ge(s_t, b + 1)
                            nc.scalar.activation(rows[:, b, :], ps[:, b, :], ACT.Copy).then_inc(s_e, 1)

                    @block.tensor
                    def _(pe):
                        for b in range(B):
                            for k in range(DT):
                                last = nc.tensor.transpose(ps[:, b, k * P:(k + 1) * P], h[:, k, b * P:(b + 1) * P], ident[:, :])
                            last.then_inc(s_t, 1)
                clear([s_t, s_e, s_o])

        early_v = sb("early_v", [1, 1], i32)
        with nc.Fori(0, B) as b:
            with ExitStack() as mem:
                xT = sb("xT", [P, DT, S], ctx=mem)
                xh, xl = sb("xh", [P, DT, S], f32r, ctx=mem), sb("xl", [P, DT, S], f32r, ctx=mem)
                cn_h, cn_l = sb("cn_h", [P, ET, S], f32r, ctx=mem), sb("cn_l", [P, ET, S], f32r, ctx=mem)
                memory_attention(b, xT, xh, xl, cn_h, cn_l, early_v)
                gate(xT, xh, xl, cn_h, cn_l)
            with ExitStack() as mem:
                v_nat = sb("v_nat", [P, ST, D], ctx=mem)
                q_st, k_st = sb("q_st", [P, NH, S], f32r, ctx=mem), sb("k_st", [P, NH, S], f32r, ctx=mem)
                late = [sb(f"late{i}", [P, HALF, S], f32r, ctx=mem) for i in range(2)]
                with ExitStack() as inner:
                    xe = [(sb(f"xe{e}h", [P, DT, S], f32r, ctx=inner), sb(f"xe{e}l", [P, DT, S], f32r, ctx=inner))
                          for e in range(2)]
                    norm(1, xe, twice=True)
                    qkv(xe, v_nat, q_st, k_st, early_v, late)
                ae = [(sb(f"ae{e}h", [P, DT, S], f32r, ctx=mem), sb(f"ae{e}l", [P, DT, S], f32r, ctx=mem))
                      for e in range(2)]
                self_attention(v_nat, q_st, k_st, ae, late)
                add_projection([t[n][k * P:(k + 1) * P, :] for k in range(DT) for n in ("L1_xattn_l_dense", "L1_xattn_v_dense")],
                               [(ae[e][0][:, k, :], ae[e][1][:, k, :]) for k in range(DT) for e in range(2)], early_v)
            with ExitStack() as mem:
                stacking, (s_kst, *s_qst) = stage("s_kst s_qst0 s_qst1")
                with stacking:
                    k_st, v_aug = sb("kx_st", [P, NH // 2, KPAD], f32r, ctx=mem), sb("v_aug", [P, KT, NH, 2 * CHD], ctx=mem)
                    with ExitStack() as inner:
                        ch, cl = sb("chx", [P, ET, KPAD], f32r, ctx=inner), sb("clx", [P, ET, KPAD], f32r, ctx=inner)
                        context_parts(b, ch, cl, k_st)
                        cross_keys(ch, cl, k_st, v_aug, s_kst)
                    q_st = sb("qx_st", [P, NH, S], f32r, ctx=mem)
                    with ExitStack() as inner:
                        ci = (sb("ci_h", [P, DT, S], f32r, ctx=inner), sb("ci_l", [P, DT, S], f32r, ctx=inner))
                        norm(2, [ci])
                        cross_queries(ci, q_st, s_kst, s_qst)
                    ah, al = sb("ax_h", [P, DT, S], f32r, ctx=mem), sb("ax_l", [P, DT, S], f32r, ctx=mem)
                    cross_attention(q_st, k_st, v_aug, ah, al, s_kst, s_qst)
                    clear([s_kst, *s_qst])
                add_projection([cd_d[k * P:(k + 1) * P, :] for k in range(DT)], [(ah[:, k, :], al[:, k, :]) for k in range(DT)])
            store_stream(b)

        flags = sb("flags", [1, 2], i32)
        with nc.Fori(0, ST) as g:
            with ExitStack() as mem:

                x = (sb("mi_h", [P, DT, S], f32r, ctx=mem), sb("mi_l", [P, DT, S], f32r, ctx=mem))
                load_stream(g, flags)
                norm(3, [x])
                for e, w in enumerate("lv"):
                    has_tokens = nc.values_load(flags[0:1, e:e + 1], min_val=0, max_val=1)
                    with nc.If(has_tokens > 0):
                        feed_forward(x, keep_expert[:, e, :], *(t[f"L1_xattn_{w}_{n}"] for n in ("gate", "up", "down")))
            write_out(g)


INPUTS = ["x", "ctx_1024", "pos_1xS", "mask_BxS_ik0"] + ["L0_xattn_" + n for n in ("W_mem", "W_gate", "b_gate", "norm_w")] + [
    "L1_xattn_" + n for n in ("ln_in_w", "ln_post_attn_w", "ln_post_cross_w", "v_qkv", "l_qkv", "v_dense", "l_dense",
                              "cq_w", "ckv_w", "cdense_w", "v_gate", "v_up", "v_down", "l_gate", "l_up", "l_down")]


def constants():
    import numpy as np
    p = np.arange(P)
    c = {"c_ident": np.eye(P, dtype=np.float32)}
    rot = np.zeros((P, P), np.float32)
    low = p % HD < HD // 2
    rot[p[low] + HD // 2, p[low]] = -1.0
    rot[p[~low] - HD // 2, p[~low]] = 1.0
    c["c_rot"] = rot
    c["c_sel"] = (p[:, None] == np.array([[HD * h for h in range(4)] + [HD * h + CHD for h in range(4)]])).astype(np.float32)
    later = p[None, :] > p[:, None]
    c["c_masks"] = np.stack([np.where(later, BIG, 0.0), np.where(later.T, BIG, 0.0)], 1).astype(np.float32)
    inv = (np.float32(1.0) / np.power(np.float32(10000.0), np.arange(0, HD, 2, dtype=np.float32) / np.float32(HD)))
    angle = (np.arange(S, dtype=np.float32)[:, None] * inv[None, :].astype(np.float32)).astype(np.float64)
    angle = np.tile(angle, (1, 2 * P // HD))
    c["c_tab"] = np.stack([np.cos(angle), np.sin(angle)], 1).astype(np.float32)
    c["c_tpos"] = (p[:, None] + P * np.arange(ST)[None, :]).astype(np.float32)
    return c


def columns(arrays):
    import numpy as np
    names = ("L0_xattn_norm_w", "L1_xattn_ln_in_w", "L1_xattn_ln_post_cross_w", "L1_xattn_ln_post_attn_w",
             "L0_xattn_b_gate")
    return np.ascontiguousarray(np.stack([arrays[n].reshape(DT, P).T for n in names], 1))


def kernel(**inputs):
    import numpy as np
    import concourse.bacc as bacc
    from concourse.bass_utils import run_bass_kernel_spmd

    nc = bacc.Bacc("TRN2", target_bir_lowering=False, num_devices=1)
    arrays = {n: np.ascontiguousarray(inputs[n]) for n in INPUTS} | constants()
    arrays["columns"] = columns(arrays)
    t = {n: nc.dram_tensor(n, a.shape, mybir.dt.from_np(a.dtype), kind="ExternalInput").ap() for n, a in arrays.items()}
    out = nc.dram_tensor("out", [B, S, D], mybir.dt.float32, kind="ExternalOutput").ap()
    program(nc, t, out)
    r = run_bass_kernel_spmd(nc, [arrays], core_ids=[0])
    return r.results[0]["out"]
```

```python
import concourse.bass as bass
from concourse import mybir
from contextlib import ExitStack

B, S, D = 4, 512, 512
KEYS, E = 1601, 256
P = 128
DT, ET, ST = D // P, E // P, S // P
KT = -(-KEYS // P)
KEY_TILES = [(i * P, min(P, KEYS - i * P)) for i in range(KT)]
KEY_BANKS = [(i * S, min(S, KEYS - i * S)) for i in range(-(-KEYS // S))]
KPAD = KEYS + KEYS % 2
NH, HD, CHD = 16, 32, 16
HIDDEN = 1376
HID_TILES = [(i * P, min(P, HIDDEN - i * P)) for i in range(-(-HIDDEN // P))]
EPS = 1e-6
MAXW = 402
MAX_STARTS = [0, 400, 800, KEYS - MAXW]
BIG = -1e30


def program(nc, t, out):
    f32, f32r, bf16, i32 = mybir.dt.float32, mybir.dt.float32r, mybir.dt.bfloat16, mybir.dt.int32
    ALU, ACT, AX = mybir.AluOpType, mybir.ActivationFunctionType, mybir.AxisListType

    def scratch(name, shape, dt=f32):
        return nc.dram_tensor(name, shape, dt, kind="Internal").ap()

    wmT_d = scratch("w_mem_transposed", [E, D])
    wgT_d = scratch("w_gate_transposed", [2 * D, D])
    cd_d = scratch("w_cross_dense_padded", [D, D])
    ones_d = scratch("ones_rows", [NH // 2, KPAD])
    k_heads_d = scratch("cross_k_by_part", [2, ET * P, KPAD])
    q_heads_d = scratch("cross_q_by_part", [2, ET * P, S])
    h_d = scratch("stream_after_attention", [B, P, DT, S])
    keep_d = scratch("keep_expert_by_token", [2, B, S])

    with ExitStack() as keep:
        made = {}

        def sb(name, shape, dt=f32, ctx=keep):
            made[name] = made.get(name, 0) + 1
            return ctx.enter_context(nc.sbuf_tensor(f"{name}_{made[name]}" if made[name] > 1 else name, shape, dt))

        ps = keep.enter_context(nc.psum_tensor("ps", [P, 8, 512], f32))
        ident, neg_ident, ones = sb("ident", [P, P]), sb("neg_ident", [P, P]), sb("ones", [P, P])
        ones_r = sb("ones_r", [P, P], f32r)
        ident_b = sb("ident_b", [P, P], bf16)
        mask_qk, mask_kq = sb("mask_qk", [P, P], bf16), sb("mask_kq", [P, P], bf16)
        rot = sb("rot", [P, P])
        cos_t, sin_t = sb("cos_t", [P, S]), sb("sin_t", [P, S])
        cols = sb("cols", [P, 5, DT])
        eps_col = sb("eps_col", [P, 1])
        h = sb("h", [P, DT, S])
        sel = sb("sel", [P, 8])
        RAW, SPLIT = 4, 4
        w_raw = sb("w_raw", [P, RAW, 512])
        w_hi, w_lo = sb("w_hi", [P, SPLIT, 512], f32r), sb("w_lo", [P, SPLIT, 512], f32r)
        keep_expert = sb("keep_expert", [P, 2, S])

        def clear(sems):
            nc.all_engine_barrier()
            lo, hi = min(s.num for s in sems), max(s.num for s in sems)
            nc.gpsimd.sem_clear(range(lo, hi + 1))
            nc.all_engine_barrier()

        def stage(names):
            ctx = ExitStack()
            sems = [ctx.enter_context(nc.semaphore(n)) for n in names.split()]
            return ctx, sems

        ctx, sems = stage("s_z s_zd s_one s_const s_raw s_tr s_ev s_st s_pos s_hot s_tab s_cast s_w s_ms")
        s_z, s_zd, s_one, s_const, s_raw, s_tr, s_ev, s_st, s_pos, s_hot, s_tab, s_cast, s_w, s_ms = sems
        with ctx:
            tab = sb("tab", [P, ST, 2, P], ctx=ctx)
            masks = sb("masks", [P, 2, P], ctx=ctx)
            posi = sb("posi", [P, S], i32, ctx=ctx)
            posf, wrap = sb("posf", [P, S], ctx=ctx), sb("wrap", [P, S], ctx=ctx)
            tpos = sb("tpos", [P, ST], ctx=ctx)
            hot = sb("hot", [P, ST, S], ctx=ctx)
            wm = sb("wm", [P, DT, E], ctx=ctx)
            wg = sb("wg", [P, DT, 2 * D], ctx=ctx)
            ones_big = sb("ones_big", [NH // 2, KPAD], ctx=ctx)
            zeros = sb("zeros", [P, DT, D], ctx=ctx)
            wmT, wgT = sb("wmT", [P, ET, D], ctx=ctx), sb("wgT", [P, 2 * DT, D], ctx=ctx)
            with nc.Block() as block:
                @block.sync
                def _(sp):
                    for dst, src in ((ident[:, :], t["c_ident"]), (rot[:, :], t["c_rot"]), (sel[:, :], t["c_sel"]),
                                     (masks[:, :, :], t["c_masks"]),
                                     (tab[:, :, :, :], t["c_tab"].rearrange("(a p) c n -> p a c n", p=P)),
                                     (tpos[:, :], t["c_tpos"])):
                        sp.dma_start(dst, src).then_inc(s_const, 16)
                    sp.dma_start(wm[:, :, :], t["L0_xattn_W_mem"].rearrange("(a p) n -> p a n", p=P)).then_inc(s_raw, 16)
                    sp.dma_start(wg[:, :, :], t["L0_xattn_W_gate"].rearrange("(a p) n -> p a n", p=P)).then_inc(s_raw, 16)
                    sp.wait_ge(s_ev, 10)
                    sp.dma_start(wmT_d.rearrange("(a p) n -> p a n", p=P), wmT[:, :, :]).then_inc(s_st, 16)
                    sp.dma_start(wgT_d.rearrange("(a p) n -> p a n", p=P), wgT[:, :, :]).then_inc(s_st, 16)
                    sp.wait_ge(s_z, 1)
                    sp.dma_start(cd_d.rearrange("(a p) n -> p a n", p=P), zeros[:, :, :]).then_inc(s_zd, 16)
                    sp.wait_ge(s_zd, 16)
                    sp.dma_start(cd_d.rearrange("(h r) n -> h r n", r=HD)[:, 0:CHD, :],
                                 t["L1_xattn_cdense_w"].rearrange("(h r) n -> h r n", r=CHD)).then_inc(s_st, 16)
                    sp.wait_ge(s_one, 1)
                    sp.dma_start(ones_d, ones_big[:, :]).then_inc(s_st, 16)
                    sp.wait_ge(s_st, 64)

                @block.scalar
                def _(act):
                    act.dma_start(posi[:, :], t["pos_1xS"].broadcast_to((P, S))).then_inc(s_pos, 16)
                    act.dma_start(cols[:, :, :], t["columns"]).then_inc(s_w, 16)
                    act.wait_ge(s_w, 16)

                @block.vector
                def _(dve):
                    nc.vector.memset(ones[:, :], 1.0).then_inc(s_ms, 1)
                    nc.vector.memset(eps_col[:, :], EPS).then_inc(s_ms, 1)
                    nc.vector.memset(zeros[:, :, :], 0.0).then_inc(s_z, 1)
                    dve.wait_ge(s_ms, 2)
                    nc.vector.tensor_copy(ones_r[:, :], ones[:, :])
                    nc.vector.memset(ones_big[:, :], 1.0).then_inc(s_one, 1)
                    dve.wait_ge(s_pos, 16)
                    nc.vector.tensor_copy(posf[:, :], posi[:, :]).then_inc(s_hot, 1)
                    dve.wait_ge(s_hot, 1)
                    nc.vector.tensor_scalar(wrap[:, :], posf[:, :], 0.0, float(S), ALU.is_lt, ALU.mult).then_inc(s_hot, 1)
                    dve.wait_ge(s_hot, 2)
                    nc.vector.tensor_tensor(out=posf[:, :], in0=posf[:, :], in1=wrap[:, :], op=ALU.add).then_inc(s_hot, 1)
                    dve.wait_ge(s_hot, 3)
                    nc.vector.tensor_scalar(posf[:, :], posf[:, :], 0.0, float(S - 1), ALU.max, ALU.min).then_inc(s_hot, 1)
                    dve.wait_ge(s_hot, 4)
                    dve.wait_ge(s_const, 96)
                    nc.vector.tensor_copy(ident_b[:, :], ident[:, :])
                    nc.vector.tensor_scalar(neg_ident[:, :], ident[:, :], -1.0, None, ALU.mult)
                    nc.vector.tensor_copy(mask_qk[:, :], masks[:, 0, :])
                    nc.vector.tensor_copy(mask_kq[:, :], masks[:, 1, :])
                    for a in range(ST):
                        nc.vector.tensor_scalar(hot[:, a, :], posf[:, :], tpos[:, a:a + 1], None,
                                                ALU.is_equal).then_inc(s_hot, 1)
                    dve.wait_ge(s_tab, 2)
                    nc.vector.tensor_copy(cos_t[:, :], ps[:, 0, :]).then_inc(s_cast, 1)
                    nc.vector.tensor_copy(sin_t[:, :], ps[:, 1, :]).then_inc(s_cast, 1)
                    for i in range(10):
                        dve.wait_ge(s_tr, i + 1)
                        dst = wmT[:, i, :] if i < ET else wgT[:, i - ET, :]
                        nc.vector.tensor_copy(dst, ps[:, 2 + i % 6, :]).then_inc(s_ev, 1)

                @block.tensor
                def _(pe):
                    pe.wait_ge(s_hot, 4 + ST)
                    for c in range(2):
                        for a in range(ST):
                            last = nc.tensor.matmul(ps[:, c, :], tab[:, a, c, :], hot[:, a, :],
                                                    start=a == 0, stop=a == ST - 1)
                        last.then_inc(s_tab, 1)
                    pe.wait_ge(s_raw, 32)
                    for i in range(10):
                        if i >= 6:
                            pe.wait_ge(s_ev, i - 5)
                        src, e = (wm, i) if i < ET else (wg, i - ET)
                        for a in range(DT):
                            last = nc.tensor.transpose(ps[:, 2 + i % 6, a * P:(a + 1) * P],
                                                       src[:, a, e * P:(e + 1) * P], ident[:, :])
                        last.then_inc(s_tr, 1)
            clear(sems)


        def load_w(sp, n, src, s_loaded, s_split):
            rows, width = src.shape[0], src.shape[-1] * (src.shape[1] if len(src.shape) == 3 else 1)
            if n >= RAW:
                sp.wait_ge(s_split, n - RAW + 1)
            dst = w_raw[0:rows, n % RAW, 0:width]
            if len(src.shape) == 3:
                dst = dst.rearrange("p (a n) -> p a n", n=src.shape[-1])
            sp.dma_start(dst, src).then_inc(s_loaded[n % RAW], 16)

        def split_w(dve, n, s_loaded, s_high, s_split, s_used, rows=P, width=512):
            raw, hi, lo = (x[0:rows, n % k, 0:width] for x, k in ((w_raw, RAW), (w_hi, SPLIT), (w_lo, SPLIT)))
            dve.wait_ge(s_loaded[n % RAW], 16 * (n // RAW + 1))
            if n >= SPLIT:
                dve.wait_ge(s_used, n - SPLIT + 1)
            nc.vector.tensor_copy(hi, raw).then_inc(s_high, 1)
            dve.wait_ge(s_high, n + 1)
            nc.vector.tensor_tensor(out=lo, in0=raw, in1=hi.bitcast(f32), op=ALU.subtract).then_inc(s_split, 1)

        def three(dst, ah, al, bh, bl, start, stop, **how):
            nc.tensor.matmul(dst, ah, bh, start=start, stop=False, **how)
            nc.tensor.matmul(dst, al, bh, start=False, stop=False, **how)
            return nc.tensor.matmul(dst, ah, bl, start=False, stop=stop, **how)

        def for_v_tokens(early_v, run):
            early = nc.tensor.value_load(early_v[0:1, 0:1], min_val=0, max_val=1)
            with nc.tensor.If(early > 0):
                run(0)
            with nc.tensor.If(early < 1):
                run(S - P)

        WSEMS = " ".join(f"s_wl{i}" for i in range(RAW)) + " s_wh s_ws s_wu "

        def memory_attention(b, xT, xh, xl, cn_h, cn_l, early_v):
            NU = DT + ET * len(KEY_BANKS)
            names = ("s_x s_c s_tr s_th s_tl s_uh s_ul s_max s_mx s_dg s_sc s_exp s_acc s_pv "
                     "s_sum s_cn s_tt s_k " + WSEMS)
            ctx, sems = stage(names)
            s = dict(zip(names.split(), sems))
            wl = [s[f"s_wl{i}"] for i in range(RAW)]
            with ctx:
                xs = sb("xs", [P, ST, D], ctx=ctx)
                cs = sb("cs", [P, KT, E], ctx=ctx)
                ch, cl = sb("ch", [P, ET, KPAD], f32r, ctx=ctx), sb("cl", [P, ET, KPAD], f32r, ctx=ctx)
                uh, ul = sb("uh", [P, ET, S], f32r, ctx=ctx), sb("ul", [P, ET, S], f32r, ctx=ctx)
                row_max = sb("row_max", [P, ST], ctx=ctx)
                tti, one = sb("tti", [P, S], i32, ctx=ctx), sb("one", [P, S], ctx=ctx)
                any_early = sb("any_early", [1, 1], ctx=ctx)
                shift = sb("shift", [P, ST, P], f32r, ctx=ctx)
                pT = sb("pT", [P, 3, S], ctx=ctx)
                acc = sb("acc", [P, S], ctx=ctx)
                rq = sb("rq", [P, ST], ctx=ctx)
                unscaled, tmp = sb("unscaled", [P, ET, S], ctx=ctx), sb("tmp", [P, ET, S], ctx=ctx)
                units = [("x", k, 0) for k in range(DT)] + [("c", e, kb) for e in range(ET)
                                                            for kb in range(len(KEY_BANKS))]
                with nc.Block() as block:
                    @block.sync
                    def _(sp):
                        sp.dma_start(xs[:, :, :], t["x"][b].rearrange("(a p) n -> p a n", p=P)).then_inc(s["s_x"], 16)
                        full = KEYS // P
                        sp.dma_start(cs[:, 0:full, :], t["ctx_1024"][b, 0:full * P].rearrange("(a p) n -> p a n", p=P))\
                            .then_inc(s["s_c"], 16)
                        sp.dma_start(cs[0:KEYS - full * P, full, :], t["ctx_1024"][b, full * P:KEYS]).then_inc(s["s_c"], 16)
                        for k in range(DT):
                            load_w(sp, k, t["L0_xattn_W_mem"][k * P:(k + 1) * P, :], wl, s["s_ws"])
                        sp.dma_start(tti[:, :], t["mask_BxS_ik0"][b].rearrange("(a n) -> a n", a=1).broadcast_to((P, S)))\
                            .then_inc(s["s_tt"], 16)

                    @block.scalar
                    def _(act):
                        for i, (what, k, kb) in enumerate(units):
                            act.wait_ge(s["s_tr"], i + 1)
                            k0, kn = (0, S) if what == "x" else KEY_BANKS[kb]
                            dst = xh[:, k, :] if what == "x" else ch[:, k, k0:k0 + kn]
                            nc.scalar.activation(dst, ps[:, i % 8, 0:kn], ACT.Copy).then_inc(s["s_th"], 1)
                        act.wait_ge(s["s_wu"], DT)
                        for e in range(ET):
                            nc.scalar.activation(uh[:, e, :], ps[:, e, :], ACT.Copy).then_inc(s["s_uh"], 1)
                        for kt, (k0, kn) in enumerate(KEY_TILES):
                            act.wait_ge(s["s_sc"], kt + 1)
                            if kt >= 3:
                                act.wait_ge(s["s_pv"], kt - 2)
                                act.wait_ge(s["s_acc"], kt - 2)
                            nc.scalar.activation(pT[0:kn, kt % 3, :], ps[0:kn, 4 + kt % 3, :], ACT.Exp,
                                                 scale=float(D) ** -0.5).then_inc(s["s_exp"], 1)

                    @block.gpsimd
                    def _(pool):
                        for kt, (k0, kn) in enumerate(KEY_TILES):
                            pool.wait_ge(s["s_exp"], kt + 1)
                            if kt == 0:
                                nc.gpsimd.tensor_copy(acc[:, :], pT[:, 0, :]).then_inc(s["s_acc"], 1)
                            else:
                                pool.wait_ge(s["s_acc"], kt)
                                nc.gpsimd.tensor_tensor(out=acc[0:kn, :], in0=acc[0:kn, :], in1=pT[0:kn, kt % 3, :],
                                                        op=ALU.add).then_inc(s["s_acc"], 1)

                    @block.vector
                    def _(dve):
                        nc.vector.memset(ch[:, :, KEYS:KPAD].bitcast(f32), 0.0)
                        nc.vector.memset(cl[:, :, KEYS:KPAD].bitcast(f32), 0.0)
                        for k in range(SPLIT):
                            split_w(dve, k, wl, s["s_wh"], s["s_ws"], s["s_wu"], width=E)
                        for i, (what, k, kb) in enumerate(units):
                            dve.wait_ge(s["s_th"], i + 1)
                            if what == "x":
                                nc.vector.tensor_copy(xT[:, k, :], ps[:, i % 8, :])
                            k0, kn = (0, S) if what == "x" else KEY_BANKS[kb]
                            hi, lo = (xh[:, k, :], xl[:, k, :]) if what == "x" else (ch[:, k, k0:k0 + kn], cl[:, k, k0:k0 + kn])
                            nc.vector.tensor_tensor(out=lo, in0=ps[:, i % 8, 0:kn], in1=hi.bitcast(f32),
                                                    op=ALU.subtract).then_inc(s["s_tl"], 1)
                        for k in range(SPLIT, DT):
                            split_w(dve, k, wl, s["s_wh"], s["s_ws"], s["s_wu"], width=E)
                        for e in range(ET):
                            dve.wait_ge(s["s_uh"], e + 1)
                            nc.vector.tensor_tensor(out=ul[:, e, :], in0=ps[:, e, :], in1=uh[:, e, :].bitcast(f32),
                                                    op=ALU.subtract).then_inc(s["s_ul"], 1)
                        for q in range(ST):
                            dve.wait_ge(s["s_max"], q + 1)
                            at = 4 - 4 * (q % 2)
                            nc.vector.tensor_reduce(out=row_max[:, q:q + 1], in_=ps[:, at:at + 4, 0:MAXW],
                                                    axis=AX.XY, op=ALU.max).then_inc(s["s_mx"], 1)
                            dve.wait_ge(s["s_mx"], q + 1)
                            nc.vector.tensor_scalar(shift[:, q, :], neg_ident[:, :], row_max[:, q:q + 1], None,
                                                    ALU.mult).then_inc(s["s_dg"], 1)
                        dve.wait_ge(s["s_tt"], 16)
                        nc.vector.tensor_scalar(one[:, :], tti[:, :], 1.0, None, ALU.is_equal).then_inc(s["s_k"], 1)
                        nc.vector.memset(keep_expert[:, 1, S - 1:S], 0.0).then_inc(s["s_k"], 1)
                        dve.wait_ge(s["s_k"], 2)
                        nc.vector.tensor_tensor(out=keep_expert[:, 1, 0:S - 1], in0=one[:, 0:S - 1], in1=one[:, 1:S],
                                                op=ALU.mult).then_inc(s["s_k"], 1)
                        dve.wait_ge(s["s_k"], 3)
                        nc.vector.tensor_scalar(keep_expert[:, 0, :], keep_expert[:, 1, :], -1.0, 1.0, ALU.mult, ALU.add)
                        nc.vector.tensor_reduce(out=any_early[:, :], in_=keep_expert[0:1, 1, 0:S - P], axis=AX.X, op=ALU.max)\
                            .then_inc(s["s_k"], 1)
                        dve.wait_ge(s["s_k"], 4)
                        nc.vector.tensor_copy(early_v[:, :], any_early[:, :])
                        dve.wait_ge(s["s_sum"], 1)
                        nc.vector.reciprocal(rq[:, :], ps[:, 7, 0:ST]).then_inc(s["s_cn"], 1)
                        for e in range(ET):
                            nc.vector.tensor_copy(unscaled[:, e, :], ps[:, e, :]).then_inc(s["s_cn"], 1)
                        dve.wait_ge(s["s_sum"], 2)
                        dve.wait_ge(s["s_cn"], 1 + ET)
                        for e in range(ET):
                            nc.vector.tensor_tensor(out=tmp[:, e, :], in0=unscaled[:, e, :], in1=ps[:, 6, :], op=ALU.mult)\
                                .then_inc(s["s_cn"], 1)
                        for e in range(ET):
                            dve.wait_ge(s["s_cn"], 2 + ET + e)
                            nc.vector.tensor_copy(cn_h[:, e, :], tmp[:, e, :]).then_inc(s["s_cn"], 1)
                        for e in range(ET):
                            dve.wait_ge(s["s_cn"], 2 + 2 * ET + e)
                            nc.vector.tensor_tensor(out=cn_l[:, e, :], in0=tmp[:, e, :], in1=cn_h[:, e, :].bitcast(f32),
                                                    op=ALU.subtract).then_inc(s["s_cn"], 1)

                    @block.tensor
                    def _(pe):
                        pe.wait_ge(s["s_x"], 16)
                        for i, (what, k, kb) in enumerate(units):
                            if i == DT:
                                pe.wait_ge(s["s_c"], 32)
                            if i >= 8:
                                pe.wait_ge(s["s_tl"], i - 7)
                            if what == "x":
                                for a in range(ST):
                                    last = nc.tensor.transpose(ps[:, i % 8, a * P:(a + 1) * P],
                                                               xs[:, a, k * P:(k + 1) * P], ident[:, :])
                            else:
                                k0, kn = KEY_BANKS[kb]
                                for a in range(-(-kn // P)):
                                    n = min(P, kn - a * P)
                                    last = nc.tensor.transpose(ps[:, i % 8, a * P:a * P + n],
                                                               cs[0:n, k0 // P + a, k * P:(k + 1) * P],
                                                               ident[0:n, 0:n])
                            last.then_inc(s["s_tr"], 1)
                        pe.wait_ge(s["s_tl"], NU)
                        for k in range(DT):
                            pe.wait_ge(s["s_ws"], k + 1)
                            for e in range(ET):
                                cut = slice(e * P, (e + 1) * P)
                                last = three(ps[:, e, :], w_hi[:, k % SPLIT, cut], w_lo[:, k % SPLIT, cut],
                                             xh[:, k, :], xl[:, k, :], k == 0, k == DT - 1)
                            last.then_inc(s["s_wu"], 1)
                        pe.wait_ge(s["s_uh"], ET)
                        for q in range(ST):
                            at = 4 - 4 * (q % 2)
                            if q == 1:
                                pe.wait_ge(s["s_ul"], ET)
                            if q >= 2:
                                pe.wait_ge(s["s_mx"], q - 1)
                            for e in range(ET):
                                for n, k0 in enumerate(MAX_STARTS):
                                    last = nc.tensor.matmul(ps[:, at + n, 0:MAXW], uh[:, e, q * P:(q + 1) * P],
                                                            ch[:, e, k0:k0 + MAXW], start=e == 0, stop=e == ET - 1)
                            last.then_inc(s["s_max"], 1)
                        pe.wait_ge(s["s_mx"], ST)
                        pe.wait_ge(s["s_dg"], ST)

                        def scores(kt):
                            k0, kn = KEY_TILES[kt]
                            if kt >= 3:
                                pe.wait_ge(s["s_exp"], kt - 2)
                            bank = ps[0:kn, 4 + kt % 3, :]
                            nc.tensor.matmul(bank, ones_r[:, 0:kn], shift[:, :, :].rearrange("p a n -> p (a n)"),
                                             start=True, stop=False)
                            for e in range(ET):
                                last = three(bank, ch[:, e, k0:k0 + kn], cl[:, e, k0:k0 + kn], uh[:, e, :], ul[:, e, :],
                                             False, e == ET - 1)
                            last.then_inc(s["s_sc"], 1)

                        scores(0)
                        scores(1)
                        for kt, (k0, kn) in enumerate(KEY_TILES):
                            if kt + 2 < KT:
                                scores(kt + 2)
                            pe.wait_ge(s["s_exp"], kt + 1)
                            for e in range(ET):
                                last = nc.tensor.matmul(ps[:, e, :], cs[0:kn, kt, e * P:(e + 1) * P],
                                                        pT[0:kn, kt % 3, :], start=kt == 0, stop=kt == KT - 1)
                            last.then_inc(s["s_pv"], 1)
                        pe.wait_ge(s["s_acc"], KT)
                        for q in range(ST):
                            last = nc.tensor.matmul(ps[:, 7, q:q + 1], acc[:, q * P:(q + 1) * P], ones[:, 0:1],
                                                    start=True, stop=True)
                        last.then_inc(s["s_sum"], 1)
                        pe.wait_ge(s["s_cn"], 1)
                        for q in range(ST):
                            last = nc.tensor.matmul(ps[:, 6, q * P:(q + 1) * P], rq[:, q:q + 1].broadcast_to((P, P)),
                                                    ident[:, :], start=True, stop=True)
                        last.then_inc(s["s_sum"], 1)
                clear(sems)

        def gate(xT, xh, xl, cn_h, cn_l):
            names = "s_mch s_mcc s_mcl s_eg s_g " + WSEMS
            ctx, sems = stage(names)
            s = dict(zip(names.split(), sems))
            wl = [s[f"s_wl{i}"] for i in range(RAW)]
            NW = ET + 2 * DT
            with ctx:
                mc, eg = sb("mc", [P, DT, S], ctx=ctx), sb("eg", [P, DT, S], ctx=ctx)
                mch, mcl = sb("mch", [P, DT, S], f32r, ctx=ctx), sb("mcl", [P, DT, S], f32r, ctx=ctx)
                with nc.Block() as block:
                    @block.sync
                    def _(sp):
                        for n in range(NW):
                            src = wmT_d[n * P:(n + 1) * P, :] if n < ET else wgT_d[(n - ET) * P:(n - ET + 1) * P, :]
                            load_w(sp, n, src, wl, s["s_ws"])

                    @block.scalar
                    def _(act):
                        act.wait_ge(s["s_wu"], ET)
                        for j in range(DT):
                            nc.scalar.activation(mch[:, j, :], ps[:, j, :], ACT.Copy).then_inc(s["s_mch"], 1)
                        act.wait_ge(s["s_wu"], NW)
                        for j in range(DT):
                            nc.scalar.activation(eg[:, j, :], ps[:, 4 + j, :], ACT.Sigmoid, bias=cols[:, 4, j:j + 1])\
                                .then_inc(s["s_eg"], 1)

                    @block.vector
                    def _(dve):
                        for n in range(NW):
                            if n == ET + SPLIT:
                                for j in range(DT):
                                    dve.wait_ge(s["s_mch"], j + 1)
                                    nc.vector.tensor_copy(mc[:, j, :], ps[:, j, :]).then_inc(s["s_mcc"], 1)
                                    nc.vector.tensor_tensor(out=mcl[:, j, :], in0=ps[:, j, :],
                                                            in1=mch[:, j, :].bitcast(f32), op=ALU.subtract)\
                                        .then_inc(s["s_mcl"], 1)
                            split_w(dve, n, wl, s["s_wh"], s["s_ws"], s["s_wu"])
                        for j in range(DT):
                            dve.wait_ge(s["s_eg"], j + 1)
                            nc.vector.tensor_tensor(out=eg[:, j, :], in0=eg[:, j, :], in1=mc[:, j, :], op=ALU.mult)\
                                .then_inc(s["s_g"], 1)
                            dve.wait_ge(s["s_g"], 2 * j + 1)
                            nc.vector.tensor_tensor(out=h[:, j, :], in0=eg[:, j, :], in1=xT[:, j, :], op=ALU.add)\
                                .then_inc(s["s_g"], 1)

                    @block.tensor
                    def _(pe):
                        for n in range(NW):
                            pe.wait_ge(s["s_ws"], n + 1)
                            if n < ET:
                                rh, rl, at = cn_h[:, n, :], cn_l[:, n, :], 0
                                first, end = n == 0, n == ET - 1
                            else:
                                k = n - ET
                                if k == DT:
                                    pe.wait_ge(s["s_mcl"], DT)
                                rh, rl = (xh[:, k, :], xl[:, k, :]) if k < DT else (mch[:, k - DT, :], mcl[:, k - DT, :])
                                at, first, end = 4, k == 0, k == 2 * DT - 1
                            for j in range(DT):
                                cut = slice(j * P, (j + 1) * P)
                                last = three(ps[:, at + j, :], w_hi[:, n % SPLIT, cut], w_lo[:, n % SPLIT, cut], rh, rl,
                                             first, end)
                            last.then_inc(s["s_wu"], 1)
                clear(sems)

        NORM_SEMS = "s_sq s_ss s_ln s_ex s_rs s_kp s_nh s_n s_nhi s_nlo "

        class Norm:

            def __init__(self, s, ctx, w, outs, bank, twice=False):
                self.s, self.w, self.outs, self.bank, self.NS = s, w, outs, bank, 2 if twice else 1
                self.sq = sb("sq", [P, self.NS, DT, S], ctx=ctx)
                self.sums2 = sb("sums2", [P, S], ctx=ctx) if twice else None
                self.lnv, self.rs = ([self.sq[:, n, k, :] for n in range(self.NS)] for k in (2, 3))
                self.kept = sb("kept", [P, 2, S], ctx=ctx) if len(outs) == 2 else None
                self.full = self.sq[:, 0, 0:2, :]

            def squares(self, act):
                for n in range(self.NS):
                    for k in range(DT):
                        nc.scalar.activation(self.sq[:, n, k, :], h[:, k, :], ACT.Square,
                                             scale=cols[:, 0, k:k + 1] if n else 1.0).then_inc(self.s["s_sq"], 1)

            def sums(self, pe):
                for n in range(self.NS):
                    for k in range(DT):
                        pe.wait_ge(self.s["s_sq"], n * DT + k + 1)
                        last = nc.tensor.matmul(ps[:, self.bank + n, :], ones[:, :], self.sq[:, n, k, :],
                                                start=k == 0, stop=k == DT - 1)
                    last.then_inc(self.s["s_ss"], 1)

            def roots(self, act):
                s = self.s
                for n in range(self.NS):
                    act.wait_ge(s["s_ss"], n + 1)
                    if n:
                        act.wait_ge(s["s_rs"], 2)
                    nc.scalar.activation(self.lnv[n], self.sums2[:, :] if n else ps[:, self.bank, :], ACT.Ln,
                                         bias=eps_col[:, 0:1], scale=1.0 / D).then_inc(s["s_ln"], 1)
                    act.wait_ge(s["s_ln"], n + 1)
                    nc.scalar.activation(self.rs[n], self.lnv[n], ACT.Exp, scale=-0.5).then_inc(s["s_ex"], 1)
                for n, (e, k) in enumerate((e, k) for e in range(len(self.outs)) for k in range(DT)):
                    act.wait_ge(s["s_n"], n + 1)
                    nc.scalar.activation(self.outs[e][0][:, k, :], self.full[:, n % 2, :], ACT.Copy).then_inc(s["s_nhi"], 1)

            def apply(self, dve):
                s, rs, outs, full = self.s, self.rs, self.outs, self.full
                dve.wait_ge(s["s_ex"], 1)
                if self.NS == 2:
                    nc.vector.tensor_tensor(out=self.sums2[:, :], in0=rs[0], in1=rs[0], op=ALU.mult).then_inc(s["s_rs"], 1)
                    dve.wait_ge(s["s_ss"], 2)
                    dve.wait_ge(s["s_rs"], 1)
                    nc.vector.tensor_tensor(out=self.sums2[:, :], in0=self.sums2[:, :], in1=ps[:, self.bank + 1, :],
                                            op=ALU.mult).then_inc(s["s_rs"], 1)
                    for k in range(DT):
                        nc.vector.scalar_tensor_tensor(out=h[:, k, :], in0=h[:, k, :], scalar=cols[:, 0, k:k + 1],
                                                       in1=rs[0], op0=ALU.mult, op1=ALU.mult).then_inc(s["s_nh"], 1)
                    dve.wait_ge(s["s_nh"], DT)
                    dve.wait_ge(s["s_ex"], 2)
                by = [rs[-1]]
                if len(outs) == 2:
                    for e in range(2):
                        nc.vector.tensor_tensor(out=self.kept[:, e, :], in0=rs[-1], in1=keep_expert[:, e, :],
                                                op=ALU.mult).then_inc(s["s_kp"], 1)
                    dve.wait_ge(s["s_kp"], 2)
                    by = [self.kept[:, e, :] for e in range(2)]
                tiles = [(e, k) for e in range(len(outs)) for k in range(DT)]
                for n in range(len(tiles) + 1):
                    if n < len(tiles):
                        e, k = tiles[n]
                        if n >= 2:
                            dve.wait_ge(s["s_nlo"], n - 1)
                        nc.vector.scalar_tensor_tensor(out=full[:, n % 2, :], in0=h[:, k, :],
                                                       scalar=cols[:, self.w, k:k + 1], in1=by[e],
                                                       op0=ALU.mult, op1=ALU.mult).then_inc(s["s_n"], 1)
                    if n >= 1:
                        e, k = tiles[n - 1]
                        dve.wait_ge(s["s_nhi"], n)
                        nc.vector.tensor_tensor(out=outs[e][1][:, k, :], in0=full[:, (n - 1) % 2, :],
                                                in1=outs[e][0][:, k, :].bitcast(f32), op=ALU.subtract)\
                            .then_inc(s["s_nlo"], 1)

        def norm(w, outs, twice=False):
            ctx, sems = stage(NORM_SEMS)
            s = dict(zip(NORM_SEMS.split(), sems))
            with ctx:
                n = Norm(s, ctx, w, outs, 0, twice)
                with nc.Block() as block:
                    @block.scalar
                    def _(act):
                        n.squares(act)
                        n.roots(act)

                    @block.tensor
                    def _(pe):
                        n.sums(pe)

                    @block.vector
                    def _(dve):
                        n.apply(dve)
                clear(sems)

        HALF = DT // 2
        STACKED_HEADS = 16 * 3 * P // HD

        def stack_heads(sp, st, parts, c0, n, at, done):
            for j in range(P // HD):
                for r, part in enumerate(parts):
                    sp.dma_start(st[r * HD:(r + 1) * HD, 4 * c0 + j:4 * (c0 + n):P // HD, :].bitcast(f32),
                                 part[j * HD:(j + 1) * HD, at:at + n, :].bitcast(f32)).then_inc(done, 16)

        def qkv(xe, v_nat, q_st, k_st, early_v, late):
            names = "s_z s_qf s_rot s_t1 s_rp s_rh s_rl s_stk " + WSEMS
            ctx, sems = stage(names)
            s = dict(zip(names.split(), sems))
            wl = [s[f"s_wl{i}"] for i in range(RAW)]
            weights = [t["L1_xattn_l_qkv"], t["L1_xattn_v_qkv"]]
            G = 2 * DT
            with ctx:
                plain = sb("plain", [P, 2 * DT, S], ctx=ctx)
                soon = (sb("rhi", [P, 2 * DT - HALF, S], f32r, ctx=ctx), sb("rlo", [P, 2 * DT - HALF, S], f32r, ctx=ctx))
                hi, lo = ([soon[i][:, c, :] for c in range(2 * DT - HALF)] + [late[i][:, c, :] for c in range(HALF)]
                          for i in range(2))
                t1, t2 = sb("t1", [P, 2, S], ctx=ctx), sb("t2", [P, 2, S], ctx=ctx)
                with nc.Block() as block:
                    @block.sync
                    def _(sp):
                        for n in range(3 * G):
                            g, k, e = n // G, n % G // 2, n % 2
                            load_w(sp, n, weights[e][k * P:(k + 1) * P, g * D:(g + 1) * D], wl, s["s_ws"])
                        sp.wait_ge(s["s_z"], 2)
                        sp.dma_start(k_st[3 * HD:3 * HD + 1, :, :].bitcast(f32).rearrange("a (r h) n -> a r (h n)", r=8),
                                     ones_d[:, 0:NH // 8 * S].rearrange("(a r) n -> a r n", a=1)).then_inc(s["s_stk"], 16)
                        sp.wait_ge(s["s_rl"], DT)
                        stack_heads(sp, q_st, (soon[0], soon[0], soon[1]), 0, DT, 0, s["s_stk"])
                        sp.wait_ge(s["s_rl"], DT + HALF)
                        stack_heads(sp, k_st, (soon[0], soon[1], soon[0]), 0, HALF, DT, s["s_stk"])
                        sp.wait_ge(s["s_stk"], 16 + 2 * STACKED_HEADS)

                    @block.scalar
                    def _(act):
                        for c in range(2 * DT):
                            if c % DT == 0:
                                act.wait_ge(s["s_wu"], G * (c // DT + 1))
                            nc.scalar.activation(plain[:, c, :], ps[:, c, :], ACT.Copy).then_inc(s["s_qf"], 1)
                        for c in range(2 * DT):
                            act.wait_ge(s["s_rp"], 2 * c + 2)
                            nc.scalar.activation(hi[c], t1[:, c % 2, :], ACT.Copy).then_inc(s["s_rh"], 1)
                        act.wait_ge(s["s_wu"], 3 * G)
                        for a in range(ST):
                            nc.scalar.activation(v_nat[:, a, :], ps[:, a, :], ACT.Copy)

                    @block.gpsimd
                    def _(pool):
                        nc.gpsimd.memset(q_st[3 * HD:P, :, :].bitcast(f32), 0.0).then_inc(s["s_z"], 1)
                        pool.wait_ge(s["s_z"], 1)
                        nc.gpsimd.memset(k_st[3 * HD:P, :, :].bitcast(f32), 0.0).then_inc(s["s_z"], 1)
                        pool.wait_ge(s["s_z"], 2)
                        for c in range(2 * DT):
                            pool.wait_ge(s["s_qf"], c + 1)
                            if c >= 2:
                                pool.wait_ge(s["s_rl"], c - 1)
                            nc.gpsimd.tensor_tensor(out=t1[:, c % 2, :], in0=plain[:, c, :], in1=cos_t[:, :], op=ALU.mult)\
                                .then_inc(s["s_t1"], 1)

                    @block.vector
                    def _(dve):
                        for n in range(2 * G + SPLIT):
                            split_w(dve, n, wl, s["s_wh"], s["s_ws"], s["s_wu"])
                        for c in range(2 * DT + 1):
                            if c < 2 * DT:
                                dve.wait_ge(s["s_rot"], c + 1)
                                nc.vector.tensor_tensor(out=t2[:, c % 2, :], in0=ps[:, c, :], in1=sin_t[:, :], op=ALU.mult)\
                                    .then_inc(s["s_rp"], 1)
                                dve.wait_ge(s["s_rp"], 2 * c + 1)
                                dve.wait_ge(s["s_t1"], c + 1)
                                nc.vector.tensor_tensor(out=t1[:, c % 2, :], in0=t1[:, c % 2, :], in1=t2[:, c % 2, :],
                                                        op=ALU.add).then_inc(s["s_rp"], 1)
                            if c >= 1:
                                dve.wait_ge(s["s_rh"], c)
                                nc.vector.tensor_tensor(out=lo[c - 1], in0=t1[:, (c - 1) % 2, :], in1=hi[c - 1].bitcast(f32),
                                                        op=ALU.subtract).then_inc(s["s_rl"], 1)
                            if c >= DT and 2 * G + SPLIT + c - DT < 3 * G:
                                split_w(dve, 2 * G + SPLIT + c - DT, wl, s["s_wh"], s["s_ws"], s["s_wu"])

                    @block.tensor
                    def _(pe):
                        def project(n, t0):
                            g, k, e = n // G, n % G // 2, n % 2
                            xh_, xl_ = xe[e]
                            pe.wait_ge(s["s_ws"], n + 1)
                            first, end = n % G == 0, k == DT - 1
                            wide = slice(t0 if e else 0, S)
                            for j in range(DT):
                                cut = slice(j * P, (j + 1) * P)
                                if g < 2:
                                    last = three(ps[:, g * 4 + j, wide], w_hi[:, n % SPLIT, cut], w_lo[:, n % SPLIT, cut],
                                                 xh_[:, k, wide], xl_[:, k, wide], first, end,
                                                 skip_group_check=True)
                                elif (j + 1) * P > wide.start:
                                    last = three(ps[:, j, :], xh_[:, k, cut], xl_[:, k, cut],
                                                 w_hi[:, n % SPLIT, :], w_lo[:, n % SPLIT, :], first, end,
                                                 skip_group_check=True)
                            last.then_inc(s["s_wu"], 1)

                        def run(t0):
                            for n in range(2 * G):
                                project(n, t0)
                            for c in range(2 * DT):
                                pe.wait_ge(s["s_qf"], c + 1)
                                nc.tensor.matmul(ps[:, c, :], rot[:, :], plain[:, c, :], start=True, stop=True)\
                                    .then_inc(s["s_rot"], 1)
                            pe.wait_ge(s["s_rp"], 2 * DT)
                            for n in range(2 * G, 3 * G):
                                project(n, t0)

                        for_v_tokens(early_v, run)
                clear(sems)

        def side_work(groups, steps, maxima, lead):
            queue = [o for g in range(groups) for o in [("max", g, i) for i in range(maxima)] + [("turn", g)]]
            first = maxima + 1 + lead
            start, queue, by_step = queue[:first], queue[first:], []
            for u in range(groups * steps):
                g, kt = divmod(u, steps)
                now = [(("flip", "back")[kt], g - 1)] if kt < 2 and g else []
                due = -(-(u + 1) * (maxima + 1) // steps)
                while queue and len(start) + sum(o[0] in ("max", "turn") for d in by_step + [now] for o in d) < first + due:
                    now.append(queue.pop(0))
                by_step.append(now)
            by_step.append([("flip", groups - 1), ("back", groups - 1)])
            return start, by_step

        def flip_sums(bank, sums, heads):
            for q in range(ST):
                last = nc.tensor.matmul(bank[:, 4 * q:4 * q + 4], sums[:, q * P:(q + 1) * P], heads, start=True, stop=True)
            return last

        def spread_back(bank, rq, width):
            heads = P // width
            for q in range(ST):
                for j in range(heads):
                    by = rq[:, heads * q + j:heads * q + j + 1].broadcast_to((P, width))
                    last = nc.tensor.matmul(bank[j * width:(j + 1) * width, q * P:(q + 1) * P], by, ident[:, :],
                                            start=True, stop=True)
            return last

        def self_attention(v_nat, q_st, k_st, ae, late, next_tiles, s_pre):
            names = "s_late s_fill s_used s_sh s_sc s_exp s_pv s_ob s_part"
            ctx, sems = stage(names)
            s = dict(zip(names.split(), sems))
            NG, SCALE = NH // 4, float(HD) ** -0.5
            start, by_step = side_work(NG, ST, 4 * ST, 4 * ST)
            order = start + [o for now in by_step for o in now]
            place = {o: n for n, o in enumerate(order)}
            with ctx:
                row_max = sb("row_max_s", [P, NG, ST, 4], ctx=ctx)
                shift = sb("shift_s", [4, NG, S], ctx=ctx, dt=f32r)
                pT = sb("pT_s", [P, 2, 4, S], ctx=ctx)
                osb = sb("osb_s", [P, 2, S], ctx=ctx)
                rq = sb("rq_s", [P, 4 * ST], ctx=ctx)
                att, own = sb("att_s", [P, S], ctx=ctx), sb("own", [P, 2, S], ctx=ctx)
                with nc.Block() as block:
                    @block.sync
                    def _(sp):
                        stack_heads(sp, k_st, (late[0], late[1], late[0]), HALF, HALF, 0, s["s_late"])
                        preload(sp, next_tiles, s_pre)
                        for g in range(NG):
                            sp.wait_ge(s["s_used"], place["turn", g] + 1)
                            for j in range(4):
                                sp.dma_start(q_st[3 * HD:3 * HD + 1, 4 * g + j, :].bitcast(f32),
                                             shift[j:j + 1, g, :].bitcast(f32)).then_inc(s["s_sh"], 16)

                    @block.scalar
                    def _(act):
                        for g in range(NG):
                            for kt in range(ST):
                                u, n = g * ST + kt, S - kt * P
                                for half in range(2):
                                    act.wait_ge(s["s_sc"], 2 * u + half + 1)
                                    if u >= 2:
                                        act.wait_ge(s["s_pv"], u - 1)
                                    nc.scalar.activation(pT[:, u % 2, 2 * half:2 * half + 2, 0:n],
                                                         ps[:, 2 + 2 * half:4 + 2 * half, 0:n], ACT.Exp, scale=SCALE)\
                                        .then_inc(s["s_exp"], 1)

                    @block.vector
                    def _(dve):
                        for n, o in enumerate(order):
                            g, bank = o[1], ps[:, n % 2, :]
                            if o[0] == "flip":
                                dve.wait_ge(s["s_pv"], (g + 1) * ST)
                                if g:
                                    dve.wait_ge(s["s_used"], place["back", g - 1] + 1)
                                nc.vector.tensor_copy(osb[:, :, :], ps[:, 6:8, :]).then_inc(s["s_ob"], 1)
                            dve.wait_ge(s["s_fill"], n + 1)
                            if o[0] == "max":
                                q, j = divmod(o[2], 4)
                                last = nc.vector.tensor_reduce(out=row_max[:, g, q, j:j + 1], in_=bank[:, 0:(q + 1) * P],
                                                               axis=AX.X, op=ALU.max)
                            elif o[0] == "turn":
                                last = nc.vector.tensor_copy(shift[:, g, :], bank[0:4, :])
                            elif o[0] == "flip":
                                last = nc.vector.reciprocal(rq[:, :], bank[:, 0:4 * ST])
                            else:
                                if g:
                                    dve.wait_ge(s["s_part"], 6 * g)
                                last = nc.vector.tensor_tensor(out=att[:, :], in0=osb[:, 0, :], in1=bank, op=ALU.mult)
                            last.then_inc(s["s_used"], 1)
                            if o[0] == "back":
                                dve.wait_ge(s["s_used"], n + 1)
                                for e, (hi, lo) in enumerate(ae):
                                    nc.vector.tensor_tensor(out=own[:, e, :], in0=att[:, :], in1=keep_expert[:, e, :],
                                                            op=ALU.mult).then_inc(s["s_part"], 1)
                                for e, (hi, lo) in enumerate(ae):
                                    dve.wait_ge(s["s_part"], 6 * g + e + 1)
                                    nc.vector.tensor_copy(hi[:, g, :], own[:, e, :]).then_inc(s["s_part"], 1)
                                for e, (hi, lo) in enumerate(ae):
                                    dve.wait_ge(s["s_part"], 6 * g + 3 + e)
                                    nc.vector.tensor_tensor(out=lo[:, g, :], in0=own[:, e, :],
                                                            in1=hi[:, g, :].bitcast(f32), op=ALU.subtract)\
                                        .then_inc(s["s_part"], 1)

                    @block.tensor
                    def _(pe):
                        def fill(o):
                            n, g = place[o], o[1]
                            bank = ps[:, n % 2, :]
                            if n >= 2:
                                pe.wait_ge(s["s_used"], n - 1)
                            if o[0] == "max":
                                q, j = divmod(o[2], 4)
                                hd = 4 * g + j
                                if (g, o[2]) == (HALF, 0):
                                    pe.wait_ge(s["s_late"], STACKED_HEADS)
                                nc.tensor.matmul(bank[:, q * P:(q + 1) * P], ident_b[:, :], mask_qk[:, :],
                                                 start=True, stop=False, skip_group_check=True)
                                last = nc.tensor.matmul(bank[:, 0:(q + 1) * P], q_st[:, hd, q * P:(q + 1) * P],
                                                        k_st[:, hd, 0:(q + 1) * P], start=False, stop=True,
                                                        skip_group_check=True)
                            elif o[0] == "turn":
                                pe.wait_ge(s["s_used"], n)
                                for q in range(ST):
                                    last = nc.tensor.matmul(bank[0:4, q * P:(q + 1) * P], row_max[:, g, q, :],
                                                            neg_ident[:, :], start=True, stop=True)
                            elif o[0] == "flip":
                                pe.wait_ge(s["s_ob"], g + 1)
                                last = flip_sums(bank, osb[:, 1, :], sel[:, 0:4])
                            else:
                                pe.wait_ge(s["s_used"], n)
                                last = spread_back(bank, rq, HD)
                            last.then_inc(s["s_fill"], 1)

                        def scores(u, half, todo):
                            g, kt = divmod(u, ST)
                            n = S - kt * P
                            if kt == 0 and half == 0:
                                pe.wait_ge(s["s_sh"], 64 * (g + 1))
                            if u >= 1:
                                pe.wait_ge(s["s_exp"], 2 * (u - 1) + half + 1)
                            for j in range(2):
                                if j and todo:
                                    fill(todo.pop(0))
                                hd, bank = 4 * g + 2 * half + j, 2 + 2 * half + j
                                nc.tensor.matmul(ps[:, bank, 0:P], ident_b[:, :], mask_kq[:, :],
                                                 start=True, stop=False, skip_group_check=True)
                                last = nc.tensor.matmul(ps[:, bank, 0:n], k_st[:, hd, kt * P:(kt + 1) * P],
                                                        q_st[:, hd, kt * P:S], start=False, stop=True,
                                                        skip_group_check=True)
                            last.then_inc(s["s_sc"], 1)

                        for o in start:
                            fill(o)
                        scores(0, 0, [])
                        scores(0, 1, [])
                        for u in range(NG * ST):
                            g, kt = divmod(u, ST)
                            todo = list(by_step[u])
                            for half in range(2):
                                if todo:
                                    fill(todo.pop(0))
                                if u + 1 < NG * ST:
                                    scores(u + 1, half, todo)
                            while todo:
                                fill(todo.pop(0))
                            pe.wait_ge(s["s_exp"], 2 * u + 2)
                            if kt == 0 and g:
                                pe.wait_ge(s["s_ob"], g)
                            n = S - kt * P
                            for j in range(4):
                                nc.tensor.matmul(ps[j * HD:(j + 1) * HD, 6, kt * P:S],
                                                 v_nat[:, kt, (4 * g + j) * HD:(4 * g + j + 1) * HD],
                                                 pT[:, u % 2, j, 0:n], start=kt == 0, stop=kt == ST - 1)
                            for j in range(4):
                                last = nc.tensor.matmul(ps[j * HD:(j + 1) * HD, 7, kt * P:S], ones[:, 0:HD],
                                                        pT[:, u % 2, j, 0:n], start=kt == 0, stop=kt == ST - 1)
                            last.then_inc(s["s_pv"], 1)
                        for o in by_step[NG * ST]:
                            fill(o)
                clear(sems)

        def preload(sp, tiles, s_pre):
            for n in range(RAW):
                load_w(sp, n, tiles[n], s_pre, None)

        def add_projection(tiles, parts, s_pre, early_v=None):
            names = WSEMS
            ctx, sems = stage(names)
            s = dict(zip(names.split(), sems))
            wl = s_pre
            NW = len(tiles)
            with ctx:
                with nc.Block() as block:
                    @block.sync
                    def _(sp):
                        for n in range(RAW, NW):
                            load_w(sp, n, tiles[n], wl, s["s_ws"])

                    @block.vector
                    def _(dve):
                        for n in range(NW):
                            split_w(dve, n, wl, s["s_wh"], s["s_ws"], s["s_wu"])
                        dve.wait_ge(s["s_wu"], NW)
                        for j in range(DT):
                            nc.vector.tensor_tensor(out=h[:, j, :], in0=h[:, j, :], in1=ps[:, j, :], op=ALU.add)

                    @block.tensor
                    def _(pe):
                        def run(t0):
                            for n in range(NW):
                                wide = slice(t0 if n % 2 else 0, S)
                                pe.wait_ge(s["s_ws"], n + 1)
                                for j in range(DT):
                                    cut = slice(j * P, (j + 1) * P)
                                    last = three(ps[:, j, wide], w_hi[:, n % SPLIT, cut], w_lo[:, n % SPLIT, cut],
                                                 parts[n][0][:, wide], parts[n][1][:, wide], n == 0, n >= NW - (1 if early_v is None else 2),
                                                 skip_group_check=True)
                                last.then_inc(s["s_wu"], 1)

                        if early_v is None:
                            run(0)
                        else:
                            for_v_tokens(early_v, run)
                clear(sems)
                clear(s_pre)

        STEP, SHIFT = P // 2, 3 * CHD

        def to_stack(sp, src_d, heads, parts, c, back):
            for par in range(2):
                for r, part in enumerate(parts):
                    src = src_d[part, c * P:(c + 1) * P, :].rearrange("(m two r) n -> two r m n", two=2, r=CHD)[par]
                    sp.dma_start(heads(par)[par * STEP + r * CHD:par * STEP + (r + 1) * CHD, :, 0:src_d.shape[2]].bitcast(f32), src)\
                        .then_inc(back, 16)

        STACK_DMAS = 2 * 3 * 16
        STACKED = ET * STACK_DMAS + 2 * 16

        def cross_queries(ci, q_st, s_cq):
            names = "s_h s_l s_up s_z " + WSEMS
            ctx, sems = stage(names)
            s = dict(zip(names.split(), sems))
            wl = s_cq
            with ctx:
                hi, lo = sb("qc_h", [P, ET, S], f32r, ctx=ctx), sb("qc_l", [P, ET, S], f32r, ctx=ctx)
                with nc.Block() as block:
                    @block.sync
                    def _(sp):
                        for c in range(ET):
                            for part, src, ready in ((0, hi, "s_h"), (1, lo, "s_l")):
                                sp.wait_ge(s[ready], c + 1)
                                sp.dma_start(q_heads_d[part, c * P:(c + 1) * P, :], src[:, c, :].bitcast(f32))\
                                    .then_inc(s["s_up"], 16)
                        sp.wait_ge(s["s_up"], 2 * ET * 16)

                    @block.gpsimd
                    def _(pool):
                        nc.gpsimd.memset(q_st[:, 0:NH // 2, :].bitcast(f32), 0.0).then_inc(s["s_z"], 1)

                    @block.scalar
                    def _(act):
                        act.wait_ge(s["s_wu"], DT)
                        for c in range(ET):
                            nc.scalar.activation(hi[:, c, :], ps[:, c, :], ACT.Copy).then_inc(s["s_h"], 1)

                    @block.vector
                    def _(dve):
                        nc.vector.memset(q_st[:, NH // 2:NH, :].bitcast(f32), 0.0).then_inc(s["s_z"], 1)
                        for k in range(DT):
                            split_w(dve, k, wl, s["s_wh"], s["s_ws"], s["s_wu"], width=E)
                        for c in range(ET):
                            dve.wait_ge(s["s_h"], c + 1)
                            nc.vector.tensor_tensor(out=lo[:, c, :], in0=ps[:, c, :], in1=hi[:, c, :].bitcast(f32),
                                                    op=ALU.subtract).then_inc(s["s_l"], 1)

                    @block.tensor
                    def _(pe):
                        for k in range(DT):
                            pe.wait_ge(s["s_ws"], k + 1)
                            for c in range(ET):
                                cut = slice(c * P, (c + 1) * P)
                                last = three(ps[:, c, :], w_hi[:, k % SPLIT, cut], w_lo[:, k % SPLIT, cut],
                                             ci[0][:, k, :], ci[1][:, k, :], k == 0, k == DT - 1)
                            last.then_inc(s["s_wu"], 1)
                clear(sems)

        def cross_inputs(b, ci, k_st, v_aug, s_kst, s_cq):
            names = "s_c s_tr s_th s_tl s_k s_h s_l s_v s_vc s_up0 s_up1 s_ms " + NORM_SEMS + WSEMS
            ctx, sems = stage(names)
            s = dict(zip(names.split(), sems))
            wl = [s[f"s_wl{i}"] for i in range(RAW)]
            NB, RING = len(KEY_BANKS), 7
            units = [(e, kb) for e in range(ET) for kb in range(NB)]
            with ctx:
                cs = sb("cs_x", [P, KT, E], ctx=ctx)
                ch, cl = sb("chx", [P, ET, KPAD], f32r, ctx=ctx), sb("clx", [P, ET, KPAD], f32r, ctx=ctx)
                hi, lo = sb("kc_h", [P, ET, KPAD], f32r, ctx=ctx), sb("kc_l", [P, ET, KPAD], f32r, ctx=ctx)
                norm2 = Norm(s, ctx, 2, [ci], 7)
                with nc.Block() as block:
                    @block.sync
                    def _(sp):
                        full = KEYS // P
                        sp.dma_start(cs[:, 0:full, :], t["ctx_1024"][b, 0:full * P].rearrange("(a p) n -> p a n", p=P))\
                            .then_inc(s["s_c"], 16)
                        sp.dma_start(cs[0:KEYS - full * P, full, :], t["ctx_1024"][b, full * P:KEYS]).then_inc(s["s_c"], 16)
                        for k in range(ET):
                            load_w(sp, k, t["L1_xattn_ckv_w"][k * P:(k + 1) * P, :], wl, s["s_ws"])
                        sp.wait_ge(s["s_ws"], ET)
                        for k in range(DT):
                            load_w(sp, k, t["L1_xattn_cq_w"][k * P:(k + 1) * P, :], s_cq, None)
                        sp.wait_ge(s["s_ms"], 2)
                        for par in range(2):
                            row = par * STEP + SHIFT
                            sp.dma_start(k_st[row:row + 1, :, :].bitcast(f32), ones_d.rearrange("(a h) n -> a h n", a=1))\
                                .then_inc(s_kst, 16)
                        for c in range(ET):
                            for part, src, ready in ((0, hi, "s_h"), (1, lo, "s_l")):
                                sp.wait_ge(s[ready], (c + 1) * NB)
                                sp.dma_start(k_heads_d[part, c * P:(c + 1) * P, :], src[:, c, :].bitcast(f32))\
                                    .then_inc(s[f"s_up{c}"], 16)
                        for c in range(ET):
                            sp.wait_ge(s[f"s_up{c}"], 32)
                            to_stack(sp, k_heads_d, lambda par: k_st[:, 4 * c:4 * c + 4, :], (0, 1, 0), c, s_kst)

                    @block.gpsimd
                    def _(pool):
                        nc.gpsimd.memset(k_st[STEP // 2:STEP, :, :].bitcast(f32), 0.0).then_inc(s["s_ms"], 1)
                        pool.wait_ge(s["s_ms"], 2)
                        nc.gpsimd.memset(v_aug[:, :, :, CHD:2 * CHD], 0.0).then_inc(s["s_ms"], 1)
                        pool.wait_ge(s["s_ms"], 3)
                        nc.gpsimd.memset(v_aug[:, :, :, CHD:CHD + 1], 1.0)

                    @block.scalar
                    def _(act):
                        norm2.squares(act)
                        for i, (k, kb) in enumerate(units):
                            act.wait_ge(s["s_tr"], i + 1)
                            k0, kn = KEY_BANKS[kb]
                            nc.scalar.activation(ch[:, k, k0:k0 + kn], ps[:, i % RING, 0:kn], ACT.Copy).then_inc(s["s_th"], 1)
                        norm2.roots(act)
                        for i in range(ET * NB):
                            c, (k0, kn) = i // NB, KEY_BANKS[i % NB]
                            kn += kn % 2
                            act.wait_ge(s["s_k"], i + 1)
                            nc.scalar.activation(hi[:, c, k0:k0 + kn], ps[:, i % RING, 0:kn], ACT.Copy).then_inc(s["s_h"], 1)
                        for kt, (k0, kn) in enumerate(KEY_TILES):
                            act.wait_ge(s["s_v"], kt + 1)
                            nc.scalar.activation(v_aug[0:kn, kt, :, 0:CHD],
                                                 ps[0:kn, kt % RING, 0:E].rearrange("p (h d) -> p h d", d=CHD), ACT.Copy)\
                                .then_inc(s["s_vc"], 1)

                    @block.vector
                    def _(dve):
                        nc.vector.memset(k_st[STEP + STEP // 2:P, :, :].bitcast(f32), 0.0).then_inc(s["s_ms"], 1)
                        nc.vector.memset(ch[:, :, KEYS:KPAD].bitcast(f32), 0.0)
                        nc.vector.memset(cl[:, :, KEYS:KPAD].bitcast(f32), 0.0)
                        for i, (k, kb) in enumerate(units):
                            dve.wait_ge(s["s_th"], i + 1)
                            k0, kn = KEY_BANKS[kb]
                            nc.vector.tensor_tensor(out=cl[:, k, k0:k0 + kn], in0=ps[:, i % RING, 0:kn],
                                                    in1=ch[:, k, k0:k0 + kn].bitcast(f32), op=ALU.subtract)\
                                .then_inc(s["s_tl"], 1)
                        for k in range(ET):
                            split_w(dve, k, wl, s["s_wh"], s["s_ws"], s["s_wu"])
                        norm2.apply(dve)
                        for i in range(ET * NB):
                            c, (k0, kn) = i // NB, KEY_BANKS[i % NB]
                            kn += kn % 2
                            dve.wait_ge(s["s_h"], i + 1)
                            nc.vector.tensor_tensor(out=lo[:, c, k0:k0 + kn], in0=ps[:, i % RING, 0:kn],
                                                    in1=hi[:, c, k0:k0 + kn].bitcast(f32), op=ALU.subtract)\
                                .then_inc(s["s_l"], 1)

                    @block.tensor
                    def _(pe):
                        norm2.sums(pe)
                        pe.wait_ge(s["s_c"], 32)
                        for i, (k, kb) in enumerate(units):
                            if i >= RING:
                                pe.wait_ge(s["s_tl"], i - RING + 1)
                            k0, kn = KEY_BANKS[kb]
                            for a in range(-(-kn // P)):
                                n = min(P, kn - a * P)
                                last = nc.tensor.transpose(ps[:, i % RING, a * P:a * P + n],
                                                           cs[0:n, k0 // P + a, k * P:(k + 1) * P], ident[0:n, 0:n])
                            last.then_inc(s["s_tr"], 1)
                        pe.wait_ge(s["s_ws"], ET)
                        pe.wait_ge(s["s_tl"], len(units))
                        for i in range(ET * NB):
                            c, (k0, kn) = i // NB, KEY_BANKS[i % NB]
                            kn += kn % 2
                            cut = slice(c * P, (c + 1) * P)
                            if i >= RING:
                                pe.wait_ge(s["s_l"], i - RING + 1)
                            for e in range(ET):
                                last = three(ps[:, i % RING, 0:kn], w_hi[:, e, cut], w_lo[:, e, cut],
                                             ch[:, e, k0:k0 + kn], cl[:, e, k0:k0 + kn], e == 0, e == ET - 1)
                            last.then_inc(s["s_k"], 1)
                        for kt, (k0, kn) in enumerate(KEY_TILES):
                            if kt < RING:
                                pe.wait_ge(s["s_l"], ET * NB if kt == 0 else kt + 1)
                            else:
                                pe.wait_ge(s["s_vc"], kt - RING + 1)
                            for e in range(ET):
                                last = three(ps[0:kn, kt % RING, 0:E], ch[:, e, k0:k0 + kn], cl[:, e, k0:k0 + kn],
                                             w_hi[:, e, E:2 * E], w_lo[:, e, E:2 * E], e == 0, e == ET - 1)
                            last.then_inc(s["s_v"], 1)
                clear(sems)

        def cross_attention(q_st, k_st, v_aug, ah, al, s_kst, next_tiles, s_pre):
            names = "s_q0 s_q1 s_fill s_used s_rm s_sh s_sc s_exp s_pv s_ob s_part"
            ctx, sems = stage(names)
            s = dict(zip(names.split(), sems))
            NG, SCALE = NH // 4, float(CHD) ** -0.5
            UNITS = 4 * ST * 2
            start, by_step = side_work(NG, KT, UNITS, 7)
            order = start + [o for now in by_step for o in now]
            place = {o: n for n, o in enumerate(order)}
            with ctx:
                halves = sb("halves", [P, NG, ST, 4, 2], ctx=ctx)
                row_max = sb("row_max_x", [P, NG, ST, 4], ctx=ctx)
                shift = sb("shift_x", [4, NG, S], ctx=ctx, dt=f32r)
                pT = sb("pT_x", [P, 2, 4, S], ctx=ctx)
                osb, rq = sb("osb", [P, S], ctx=ctx), sb("rq_x", [P, 4 * ST], ctx=ctx)
                att = sb("att_x", [P, S], ctx=ctx)
                with nc.Block() as block:
                    @block.sync
                    def _(sp):
                        for c in range(ET):
                            to_stack(sp, q_heads_d, lambda par: q_st[:, 8 * c + par:8 * c + 8:2, :], (0, 0, 1), c, s[f"s_q{c}"])
                        preload(sp, next_tiles, s_pre)
                        for g in range(NG):
                            sp.wait_ge(s["s_used"], place["turn", g] + 1)
                            for j in range(4):
                                hd = 4 * g + j
                                row = hd % 2 * STEP + SHIFT
                                sp.dma_start(q_st[row:row + 1, hd, :].bitcast(f32),
                                             shift[j:j + 1, g, :].bitcast(f32)).then_inc(s["s_sh"], 16)

                    @block.scalar
                    def _(act):
                        for u in range(NG * KT):
                            kn = KEY_TILES[u % KT][1]
                            for j in range(4):
                                v = 4 * u + j
                                act.wait_ge(s["s_sc"], v + 1)
                                if u >= 2 and j == 0:
                                    act.wait_ge(s["s_pv"], u - 1)
                                nc.scalar.activation(pT[0:kn, u % 2, j, :], ps[0:kn, 5 + v % 3, :], ACT.Exp, scale=SCALE)\
                                    .then_inc(s["s_exp"], 1)

                    @block.vector
                    def _(dve):
                        for n, o in enumerate(order):
                            g, at = o[1], 2 * (n % 2)
                            if o[0] == "flip":
                                dve.wait_ge(s["s_pv"], (g + 1) * KT)
                                if g:
                                    dve.wait_ge(s["s_used"], place["back", g - 1] + 1)
                                nc.vector.tensor_copy(osb[:, :], ps[:, 4, :]).then_inc(s["s_ob"], 1)
                            dve.wait_ge(s["s_fill"], n + 1)
                            if o[0] == "max":
                                j, q, half = o[2] // (2 * ST), o[2] // 2 % ST, o[2] % 2
                                last = nc.vector.tensor_reduce(out=halves[:, g, q, j, half:half + 1],
                                                               in_=ps[:, at:at + 2, 0:MAXW], axis=AX.XY, op=ALU.max)
                            elif o[0] == "turn":
                                last = nc.vector.tensor_copy(shift[:, g, :], ps[0:4, at, :])
                            elif o[0] == "flip":
                                last = nc.vector.reciprocal(rq[:, :], ps[:, at, 0:4 * ST])
                            else:
                                if g:
                                    dve.wait_ge(s["s_part"], 2 * g)
                                last = nc.vector.tensor_tensor(out=att[:, :], in0=osb[:, :], in1=ps[:, at, :], op=ALU.mult)
                            last.then_inc(s["s_used"], 1)
                            if o[0] == "back":
                                dve.wait_ge(s["s_used"], n + 1)
                                nc.vector.tensor_copy(ah[:, g, :], att[:, :]).then_inc(s["s_part"], 1)
                                dve.wait_ge(s["s_part"], 2 * g + 1)
                                nc.vector.tensor_tensor(out=al[:, g, :], in0=att[:, :], in1=ah[:, g, :].bitcast(f32),
                                                        op=ALU.subtract).then_inc(s["s_part"], 1)
                            if o[0] == "max" and o[2] == UNITS - 1:
                                dve.wait_ge(s["s_used"], n + 1)
                                nc.vector.tensor_reduce(out=row_max[:, g, :, :], in_=halves[:, g, :, :, :], axis=AX.X,
                                                        op=ALU.max).then_inc(s["s_rm"], 1)

                    @block.tensor
                    def _(pe):
                        def fill(o):
                            n, g = place[o], o[1]
                            at = 2 * (n % 2)
                            if n >= 2:
                                pe.wait_ge(s["s_used"], n - 1)
                            if o[0] == "max":
                                j, q, half = o[2] // (2 * ST), o[2] // 2 % ST, o[2] % 2
                                hd = 4 * g + j
                                if n == 0:
                                    pe.wait_ge(s_kst, STACKED)
                                if o[2] == 0:
                                    pe.wait_ge(s[f"s_q{hd * CHD // P}"], STACK_DMAS)
                                for i in range(2):
                                    k0 = MAX_STARTS[2 * half + i]
                                    last = nc.tensor.matmul(ps[:, at + i, 0:MAXW], q_st[:, hd, q * P:(q + 1) * P],
                                                            k_st[:, hd // 2, k0:k0 + MAXW], start=True, stop=True)
                            elif o[0] == "turn":
                                pe.wait_ge(s["s_rm"], g + 1)
                                for q in range(ST):
                                    last = nc.tensor.matmul(ps[0:4, at, q * P:(q + 1) * P], row_max[:, g, q, :],
                                                            neg_ident[:, :], start=True, stop=True)
                            elif o[0] == "flip":
                                pe.wait_ge(s["s_ob"], g + 1)
                                last = flip_sums(ps[:, at, :], osb, sel[:, 4:8])
                            else:
                                pe.wait_ge(s["s_used"], n)
                                last = spread_back(ps[:, at, :], rq, HD)
                            last.then_inc(s["s_fill"], 1)

                        def score(u, j):
                            g, kt = divmod(u, KT)
                            k0, kn = KEY_TILES[kt]
                            v, hd = 4 * u + j, 4 * g + j
                            if kt == 0 and j == 0:
                                pe.wait_ge(s["s_sh"], 64 * (g + 1))
                            if v >= 3:
                                pe.wait_ge(s["s_exp"], v - 2)
                            nc.tensor.matmul(ps[0:kn, 5 + v % 3, :], k_st[:, hd // 2, k0:k0 + kn], q_st[:, hd, :],
                                             start=True, stop=True).then_inc(s["s_sc"], 1)

                        for o in start:
                            fill(o)
                        for j in range(3):
                            score(0, j)
                        for u in range(NG * KT):
                            g, kt = divmod(u, KT)
                            todo = list(by_step[u])

                            def side():
                                if todo:
                                    fill(todo.pop(0))

                            def ahead(v):
                                if v < 4 * NG * KT:
                                    score(v // 4, v % 4)

                            ahead(4 * u + 3)
                            side()
                            ahead(4 * u + 4)
                            side()
                            ahead(4 * u + 5)
                            pe.wait_ge(s["s_exp"], 4 * u + 4)
                            if kt == 0 and g:
                                pe.wait_ge(s["s_ob"], g)
                            kn = KEY_TILES[kt][1]
                            for j in range(4):
                                last = nc.tensor.matmul(ps[j * HD:(j + 1) * HD, 4, :], v_aug[0:kn, kt, 4 * g + j, :],
                                                        pT[0:kn, u % 2, j, :], start=kt == 0, stop=kt == KT - 1)
                            last.then_inc(s["s_pv"], 1)
                            side()
                            ahead(4 * u + 6)
                            while todo:
                                side()
                        for o in by_step[NG * KT]:
                            fill(o)
                clear(sems)

        def store_stream(b):
            ctx, (s_st,) = stage("s_st")
            with ctx:
                with nc.Block() as block:
                    @block.sync
                    def _(sp):
                        sp.dma_start(h_d[b], h[:, :, :]).then_inc(s_st, 16)
                        sp.dma_start(keep_d[:, b, :].rearrange("e (a n) -> a e n", a=1), keep_expert[0:1, :, :]).then_inc(s_st, 16)
                        sp.wait_ge(s_st, 32)
                clear([s_st])

        def load_stream(g, flags):
            names = "s_ld s_fl"
            ctx, (s_ld, s_fl) = stage(names)
            with ctx:
                any_token = sb("any_token", [1, 2], ctx=ctx)
                with nc.Block() as block:
                    @block.sync
                    def _(sp):
                        for b in range(B):
                            sp.dma_start(h[:, :, b * P:(b + 1) * P], h_d[b, :, :, bass.ts(g, P)]).then_inc(s_ld, 16)
                        for e in range(2):
                            sp.dma_start(keep_expert[:, e, :].rearrange("p (b n) -> p b n", n=P),
                                         keep_d[e:e + 1, :, bass.ts(g, P)].broadcast_to((P, B, P))).then_inc(s_ld, 16)
                        sp.wait_ge(s_ld, 16 * (B + 2))

                    @block.vector
                    def _(dve):
                        dve.wait_ge(s_ld, 16 * (B + 2))
                        nc.vector.tensor_reduce(out=any_token[:, :], in_=keep_expert[0:1, :, :], axis=AX.X, op=ALU.max)\
                            .then_inc(s_fl, 1)
                        dve.wait_ge(s_fl, 1)
                        nc.vector.tensor_copy(flags[:, :], any_token[:, :])
                clear([s_ld, s_fl])

        def feed_forward(x, keep, gate_w, up_w, down_w):
            names = "s_si s_kp s_mu s_hi s_lo " + WSEMS
            ctx, sems = stage(names)
            s = dict(zip(names.split(), sems))
            wl = [s[f"s_wl{i}"] for i in range(RAW)]
            NC = len(HID_TILES)
            tiles = [(w, c) for c in range(2) for w in "gu"]
            for c in range(NC):
                tiles.append(("d", c))
                if c + 2 < NC:
                    tiles += [("g", c + 2), ("u", c + 2)]
            place = {o: n for n, o in enumerate(tiles)}
            with ctx:
                sg, prod = sb("sg", [P, 2, S], ctx=ctx), sb("prod", [P, 2, S], ctx=ctx)
                hi, lo = sb("hid_h", [P, 2, S], f32r, ctx=ctx), sb("hid_l", [P, 2, S], f32r, ctx=ctx)
                with nc.Block() as block:
                    @block.sync
                    def _(sp):
                        for n, (w, c) in enumerate(tiles):
                            c0, cn = HID_TILES[c]
                            if w == "d":
                                src = down_w[c0:c0 + cn, :]
                            else:
                                src = (gate_w if w == "g" else up_w)[:, c0:c0 + cn].rearrange("(a p) n -> p a n", p=P)
                            load_w(sp, n, src, wl, s["s_ws"])

                    @block.scalar
                    def _(act):
                        for c, (c0, cn) in enumerate(HID_TILES):
                            act.wait_ge(s["s_wu"], place["g", c] + 1)
                            if c >= 2:
                                act.wait_ge(s["s_mu"], c - 1)
                            nc.scalar.activation(sg[0:cn, c % 2, :], ps[0:cn, 4 + c % 2, :], ACT.Silu).then_inc(s["s_si"], 1)
                            act.wait_ge(s["s_mu"], c + 1)
                            if c >= 2:
                                act.wait_ge(s["s_wu"], place["d", c - 2] + 1)
                            nc.scalar.activation(hi[0:cn, c % 2, :], prod[0:cn, c % 2, :], ACT.Copy).then_inc(s["s_hi"], 1)

                    @block.gpsimd
                    def _(pool):
                        for c, (c0, cn) in enumerate(HID_TILES):
                            pool.wait_ge(s["s_si"], c + 1)
                            nc.gpsimd.tensor_tensor(out=sg[0:cn, c % 2, :], in0=sg[0:cn, c % 2, :], in1=keep[0:cn, :],
                                                    op=ALU.mult).then_inc(s["s_kp"], 1)

                    @block.vector
                    def _(dve):
                        def split_tile(w, c):
                            cn = HID_TILES[c][1]
                            rows, width = (cn, D) if w == "d" else (P, DT * cn)
                            split_w(dve, place[w, c], wl, s["s_wh"], s["s_ws"], s["s_wu"], rows, width)

                        for w, c in tiles[0:4]:
                            split_tile(w, c)
                        for c, (c0, cn) in enumerate(HID_TILES):
                            dve.wait_ge(s["s_kp"], c + 1)
                            dve.wait_ge(s["s_wu"], place["u", c] + 1)
                            nc.vector.tensor_tensor(out=prod[0:cn, c % 2, :], in0=ps[0:cn, 6 + c % 2, :], in1=sg[0:cn, c % 2, :],
                                                    op=ALU.mult).then_inc(s["s_mu"], 1)
                            split_tile("d", c)
                            dve.wait_ge(s["s_hi"], c + 1)
                            nc.vector.tensor_tensor(out=lo[0:cn, c % 2, :], in0=prod[0:cn, c % 2, :],
                                                    in1=hi[0:cn, c % 2, :].bitcast(f32), op=ALU.subtract).then_inc(s["s_lo"], 1)
                            if c + 2 < NC:
                                split_tile("g", c + 2)
                                split_tile("u", c + 2)
                        dve.wait_ge(s["s_wu"], len(tiles))
                        for j in range(DT):
                            nc.vector.tensor_tensor(out=h[:, j, :], in0=h[:, j, :], in1=ps[:, j, :], op=ALU.add)

                    @block.tensor
                    def _(pe):
                        for n, (w, c) in enumerate(tiles):
                            cn, slot = HID_TILES[c][1], n % SPLIT
                            pe.wait_ge(s["s_ws"], n + 1)
                            if w == "d":
                                pe.wait_ge(s["s_lo"], c + 1)
                                for j in range(DT):
                                    cut = slice(j * P, (j + 1) * P)
                                    last = three(ps[:, j, :], w_hi[0:cn, slot, cut], w_lo[0:cn, slot, cut],
                                                 hi[0:cn, c % 2, :], lo[0:cn, c % 2, :], c == 0, c == NC - 1)
                            else:
                                if c >= 2:
                                    pe.wait_ge(s["s_mu"], c - 1)
                                bank = ps[0:cn, (4 if w == "g" else 6) + c % 2, :]
                                for k in range(DT):
                                    cut = slice(k * cn, (k + 1) * cn)
                                    last = three(bank, w_hi[:, slot, cut], w_lo[:, slot, cut], x[0][:, k, :], x[1][:, k, :],
                                                 k == 0, k == DT - 1)
                            last.then_inc(s["s_wu"], 1)
                clear(sems)

        def write_out(g):
            names = "s_t s_e s_o"
            ctx, (s_t, s_e, s_o) = stage(names)
            with ctx:
                rows = sb("rows", [P, B, D], ctx=ctx)
                with nc.Block() as block:
                    @block.sync
                    def _(sp):
                        for b in range(B):
                            sp.wait_ge(s_e, b + 1)
                            sp.dma_start(out[b, bass.ts(g, P), :], rows[:, b, :]).then_inc(s_o, 16)
                        sp.wait_ge(s_o, 16 * B)

                    @block.scalar
                    def _(act):
                        for b in range(B):
                            act.wait_ge(s_t, b + 1)
                            nc.scalar.activation(rows[:, b, :], ps[:, b, :], ACT.Copy).then_inc(s_e, 1)

                    @block.tensor
                    def _(pe):
                        for b in range(B):
                            for k in range(DT):
                                last = nc.tensor.transpose(ps[:, b, k * P:(k + 1) * P], h[:, k, b * P:(b + 1) * P], ident[:, :])
                            last.then_inc(s_t, 1)
                clear([s_t, s_e, s_o])

        early_v = sb("early_v", [1, 1], i32)
        s_pre = [keep.enter_context(nc.semaphore(f"s_pre{i}")) for i in range(RAW)]
        dense = [t[n][k * P:(k + 1) * P, :] for k in range(DT) for n in ("L1_xattn_l_dense", "L1_xattn_v_dense")]
        cross_dense = [cd_d[k * P:(k + 1) * P, :] for k in range(DT)]
        with nc.Fori(0, B) as b:
            with ExitStack() as mem:
                xT = sb("xT", [P, DT, S], ctx=mem)
                xh, xl = sb("xh", [P, DT, S], f32r, ctx=mem), sb("xl", [P, DT, S], f32r, ctx=mem)
                cn_h, cn_l = sb("cn_h", [P, ET, S], f32r, ctx=mem), sb("cn_l", [P, ET, S], f32r, ctx=mem)
                memory_attention(b, xT, xh, xl, cn_h, cn_l, early_v)
                gate(xT, xh, xl, cn_h, cn_l)
            with ExitStack() as mem:
                v_nat = sb("v_nat", [P, ST, D], ctx=mem)
                q_st, k_st = sb("q_st", [P, NH, S], f32r, ctx=mem), sb("k_st", [P, NH, S], f32r, ctx=mem)
                late = [sb(f"late{i}", [P, HALF, S], f32r, ctx=mem) for i in range(2)]
                with ExitStack() as inner:
                    xe = [(sb(f"xe{e}h", [P, DT, S], f32r, ctx=inner), sb(f"xe{e}l", [P, DT, S], f32r, ctx=inner))
                          for e in range(2)]
                    norm(1, xe, twice=True)
                    qkv(xe, v_nat, q_st, k_st, early_v, late)
                ae = [(sb(f"ae{e}h", [P, DT, S], f32r, ctx=mem), sb(f"ae{e}l", [P, DT, S], f32r, ctx=mem))
                      for e in range(2)]
                self_attention(v_nat, q_st, k_st, ae, late, dense, s_pre)
                add_projection(dense,
                               [(ae[e][0][:, k, :], ae[e][1][:, k, :]) for k in range(DT) for e in range(2)], s_pre, early_v)
            with ExitStack() as mem:
                stacking, (s_kst, *s_cq) = stage("s_kst " + " ".join(f"s_cq{i}" for i in range(RAW)))
                with stacking:
                    k_st, v_aug = sb("kx_st", [P, NH // 2, KPAD], f32r, ctx=mem), sb("v_aug", [P, KT, NH, 2 * CHD], ctx=mem)
                    parts = (sb("cross_h", [P, DT, S], f32r, ctx=mem), sb("cross_l", [P, DT, S], f32r, ctx=mem))
                    cross_inputs(b, parts, k_st, v_aug, s_kst, s_cq)
                    q_st = sb("qx_st", [P, NH, S], f32r, ctx=mem)
                    cross_queries(parts, q_st, s_cq)
                    cross_attention(q_st, k_st, v_aug, *parts, s_kst, cross_dense, s_pre)
                    clear([s_kst, *s_cq])
                add_projection(cross_dense, [(parts[0][:, k, :], parts[1][:, k, :]) for k in range(DT)], s_pre)
            store_stream(b)

        flags = sb("flags", [1, 2], i32)
        with nc.Fori(0, ST) as g:
            with ExitStack() as mem:
                x = (sb("mi_h", [P, DT, S], f32r, ctx=mem), sb("mi_l", [P, DT, S], f32r, ctx=mem))
                load_stream(g, flags)
                norm(3, [x])
                for e, w in enumerate("lv"):
                    has_tokens = nc.values_load(flags[0:1, e:e + 1], min_val=0, max_val=1)
                    with nc.If(has_tokens > 0):
                        feed_forward(x, keep_expert[:, e, :], *(t[f"L1_xattn_{w}_{n}"] for n in ("gate", "up", "down")))
            write_out(g)


INPUTS = ["x", "ctx_1024", "pos_1xS", "mask_BxS_ik0"] + ["L0_xattn_" + n for n in ("W_mem", "W_gate", "b_gate", "norm_w")] + [
    "L1_xattn_" + n for n in ("ln_in_w", "ln_post_attn_w", "ln_post_cross_w", "v_qkv", "l_qkv", "v_dense", "l_dense",
                              "cq_w", "ckv_w", "cdense_w", "v_gate", "v_up", "v_down", "l_gate", "l_up", "l_down")]


def constants():
    import numpy as np
    p = np.arange(P)
    c = {"c_ident": np.eye(P, dtype=np.float32)}
    rot = np.zeros((P, P), np.float32)
    low = p % HD < HD // 2
    rot[p[low] + HD // 2, p[low]] = -1.0
    rot[p[~low] - HD // 2, p[~low]] = 1.0
    c["c_rot"] = rot
    c["c_sel"] = (p[:, None] == np.array([[HD * h for h in range(4)] + [HD * h + CHD for h in range(4)]])).astype(np.float32)
    later = p[None, :] > p[:, None]
    c["c_masks"] = np.stack([np.where(later, BIG, 0.0), np.where(later.T, BIG, 0.0)], 1).astype(np.float32)
    inv = (np.float32(1.0) / np.power(np.float32(10000.0), np.arange(0, HD, 2, dtype=np.float32) / np.float32(HD)))
    angle = (np.arange(S, dtype=np.float32)[:, None] * inv[None, :].astype(np.float32)).astype(np.float64)
    angle = np.tile(angle, (1, 2 * P // HD))
    c["c_tab"] = np.stack([np.cos(angle), np.sin(angle)], 1).astype(np.float32)
    c["c_tpos"] = (p[:, None] + P * np.arange(ST)[None, :]).astype(np.float32)
    return c


def columns(arrays):
    import numpy as np
    names = ("L0_xattn_norm_w", "L1_xattn_ln_in_w", "L1_xattn_ln_post_cross_w", "L1_xattn_ln_post_attn_w",
             "L0_xattn_b_gate")
    return np.ascontiguousarray(np.stack([arrays[n].reshape(DT, P).T for n in names], 1))


def kernel(**inputs):
    import numpy as np
    import concourse.bacc as bacc
    from concourse.bass_utils import run_bass_kernel_spmd

    nc = bacc.Bacc("TRN2", target_bir_lowering=False, num_devices=1)
    arrays = {n: np.ascontiguousarray(inputs[n]) for n in INPUTS} | constants()
    arrays["columns"] = columns(arrays)
    t = {n: nc.dram_tensor(n, a.shape, mybir.dt.from_np(a.dtype), kind="ExternalInput").ap() for n, a in arrays.items()}
    out = nc.dram_tensor("out", [B, S, D], mybir.dt.float32, kind="ExternalOutput").ap()
    program(nc, t, out)
    r = run_bass_kernel_spmd(nc, [arrays], core_ids=[0])
    return r.results[0]["out"]
```
